# Optimizing a Trainium2 kernel written in Bass

```python
import numpy as np
import jax
import jax.numpy as jnp

def _softmax(x, axis=-1):
    return jax.nn.softmax(x, axis=axis)

def _gelu(x):
    return jax.nn.gelu(x, approximate=True)

def _silu(x):
    return jax.nn.silu(x)

def _sigmoid(x):
    return jax.nn.sigmoid(x)

def _layernorm(x, axis=-1, eps=1e-05):
    m = jnp.mean(x, axis=axis, keepdims=True)
    v = jnp.var(x, axis=axis, keepdims=True)
    return (x - m) / jnp.sqrt(v + eps)

def _scatter_add(tgt, idx, src, axis=0):
    return tgt.at[idx].add(src)

def _segment_sum(src, seg, n):
    return jax.ops.segment_sum(src, seg, n)
kernel_name = 'mk_xattn_ffn_d2_seqx_r8_0cde20'

def setup_inputs(seed: int=0):
    np.random.seed(seed)
    _w = jnp.asarray

    def _rec_inputs():
        import jax
        import jax.numpy as jnp
        _rk = jax.random.key(seed)
        x = 0.0003765 + 1 * jax.random.normal(jax.random.fold_in(_rk, 1), (8, 128, 256), jnp.float32)
        _lenS = 128 - jax.random.randint(jax.random.fold_in(_rk, 7), (8,), 0, max(1, 128 // 4) + 1, jnp.int32)
        _lenS2 = 128 - jax.random.randint(jax.random.fold_in(_rk, 8), (8,), 0, max(1, 128 // 4) + 1, jnp.int32)
        _ctx_2048P = jax.random.normal(jax.random.fold_in(_rk, 11), (8, 16, 256), jnp.float32)
        _ctx_2048c = jax.random.dirichlet(jax.random.fold_in(_rk, 511), 0.3 * jnp.ones((16,), jnp.float32), (8, 128))
        _ctx_2048t = jnp.einsum('bsk,bkd->bsd', _ctx_2048c, _ctx_2048P)
        _ctx_2048t = _ctx_2048t * jax.lax.rsqrt(jnp.mean(jnp.square(_ctx_2048t)) + 1e-12) * 0.953939
        ctx_2048 = -0.000292821 + 1.00034 * (_ctx_2048t + 0.3 * jax.random.normal(jax.random.fold_in(_rk, 611), (8, 128, 256), jnp.float32))
        return (x, ctx_2048)
    x, ctx_2048 = _rec_inputs()

    def _L0_xattn_setup():
        import jax, jax.numpy as jnp
        import numpy as np
        key = jax.random.key(seed)
        k1, k2, k3, k4, k5 = jax.random.split(key, 5)
        B, D_MODEL, L = (2, 128, 256)
        HEAD_DIM = 8
        H = D_MODEL // HEAD_DIM
        return {'k': jax.random.normal(k1, (B, D_MODEL, L), dtype=jnp.float32), 'v': jax.random.normal(k2, (B, D_MODEL, L), dtype=jnp.float32), 'q': jax.random.normal(k3, (B, D_MODEL, L), dtype=jnp.float32), 'ssm_kernel': jax.random.normal(k4, (H, L), dtype=jnp.float32), 'D': jax.random.normal(k5, (H,), dtype=jnp.float32), 'head_dim': HEAD_DIM}
    _L0_xattn_all = _L0_xattn_setup()
    _L0_xattn_in = {k: v for k, v in _L0_xattn_all.items() if k in ('ssm_kernel', 'D')}
    del _L0_xattn_all

    def _L0_ffn_setup():
        import jax, jax.numpy as jnp
        import numpy as np
        H, I, E, TOP_K = (256, 176, 16, 6)
        IS = 352
        NORM_TOPK_PROB = False

        def _silu_and_mul(gate_up):
            d = gate_up.shape[-1] // 2
            g, u = (gate_up[..., :d], gate_up[..., d:])
            return jax.nn.silu(g) * u
        key = jax.random.key(seed)
        ks = jax.random.split(key, 6)
        s = 0.02
        return {'x': jax.random.normal(ks[0], (1, 256, H), jnp.float32), 'gate_w': jax.random.normal(ks[1], (E, H), jnp.float32) * s, 'w1': jax.random.normal(ks[2], (E, 2 * I, H), jnp.float32) * s, 'w2': jax.random.normal(ks[3], (E, H, I), jnp.float32) * s, 'shared_w1': jax.random.normal(ks[4], (2 * IS, H), jnp.float32) * s, 'shared_w2': jax.random.normal(ks[5], (H, IS), jnp.float32) * s}
    _L0_ffn_all = _L0_ffn_setup()
    _L0_ffn_in = {k: v for k, v in _L0_ffn_all.items() if k in ('gate_w', 'w1', 'w2', 'shared_w1', 'shared_w2')}
    del _L0_ffn_all

    def _L1_xattn_setup():
        import jax, jax.numpy as jnp
        import numpy as np

        def _wkv(time_decay, time_first, k, v):
            w = -jnp.exp(time_decay)
            u = time_first
            B, T, C = k.shape
            aa = jnp.zeros((B, C), dtype=k.dtype)
            bb = jnp.zeros((B, C), dtype=k.dtype)
            pp = jnp.full((B, C), -1e+38, dtype=k.dtype)

            def step(carry, kv_t):
                aa, bb, pp = carry
                kt, vt = kv_t
                ww = u + kt
                q = jnp.maximum(pp, ww)
                e1 = jnp.exp(pp - q)
                e2 = jnp.exp(ww - q)
                y_t = (e1 * aa + e2 * vt) / (e1 * bb + e2)
                ww2 = pp + w
                q2 = jnp.maximum(ww2, kt)
                e1b = jnp.exp(ww2 - q2)
                e2b = jnp.exp(kt - q2)
                new_carry = (e1b * aa + e2b * vt, e1b * bb + e2b, q2)
                return (new_carry, y_t)
            ks = jnp.transpose(k, (1, 0, 2))
            vs = jnp.transpose(v, (1, 0, 2))
            _, ys = jax.lax.scan(step, (aa, bb, pp), (ks, vs))
            return jnp.transpose(ys, (1, 0, 2))
        key = jax.random.key(seed)
        k1, k2, k3, k4 = jax.random.split(key, 4)
        B, T, C = (8, 128, 256)
        return {'batch_size': B, 'seq_len': T, 'embedding_dim': C, 'time_decay': jax.random.normal(k1, (C,), dtype=jnp.float32), 'time_first': jax.random.normal(k2, (C,), dtype=jnp.float32), 'k': jax.random.normal(k3, (B, T, C), dtype=jnp.float32), 'v': jax.random.normal(k4, (B, T, C), dtype=jnp.float32)}
    _L1_xattn_all = _L1_xattn_setup()
    _L1_xattn_in = {k: v for k, v in _L1_xattn_all.items() if k in ('time_decay', 'time_first')}
    del _L1_xattn_all

    def _L1_ffn_setup():
        import jax, jax.numpy as jnp
        import numpy as np
        B, S, H = (2, 256, 256)
        E, K, F = (32, 4, 176)
        FS = 704
        EPS = 1e-06
        CAP = 128
        key = jax.random.key(seed)
        ks = jax.random.split(key, 10)
        s = 0.02
        return {'hidden_states': jax.random.normal(ks[0], (B, S, H), jnp.float32), 'w_norm': 1.0 + 0.02 * jax.random.normal(ks[1], (H,), jnp.float32), 'w_router': s * jax.random.normal(ks[2], (H, E), jnp.float32), 'w_gate': s * jax.random.normal(ks[3], (E, H, F), jnp.float32), 'w_up': s * jax.random.normal(ks[4], (E, H, F), jnp.float32), 'w_down': s * jax.random.normal(ks[5], (E, F, H), jnp.float32), 'sw_gate': s * jax.random.normal(ks[6], (H, FS), jnp.float32), 'sw_up': s * jax.random.normal(ks[7], (H, FS), jnp.float32), 'sw_down': s * jax.random.normal(ks[8], (FS, H), jnp.float32), 'w_shared_gate': s * jax.random.normal(ks[9], (H, 1), jnp.float32)}
    _L1_ffn_all = _L1_ffn_setup()
    _L1_ffn_in = {k: v for k, v in _L1_ffn_all.items() if k in ('w_norm', 'w_router', 'w_gate', 'w_up', 'w_down', 'sw_gate', 'sw_up', 'sw_down', 'w_shared_gate')}
    del _L1_ffn_all
    return {'x': x, 'ctx_2048': ctx_2048, 'L0_xattn_ssm_kernel': _L0_xattn_in['ssm_kernel'], 'L0_xattn_D': _L0_xattn_in['D'], 'L0_ffn_gate_w': _L0_ffn_in['gate_w'], 'L0_ffn_w1': _L0_ffn_in['w1'], 'L0_ffn_w2': _L0_ffn_in['w2'], 'L0_ffn_shared_w1': _L0_ffn_in['shared_w1'], 'L0_ffn_shared_w2': _L0_ffn_in['shared_w2'], 'L1_xattn_time_decay': _L1_xattn_in['time_decay'], 'L1_xattn_time_first': _L1_xattn_in['time_first'], 'L1_ffn_w_norm': _L1_ffn_in['w_norm'], 'L1_ffn_w_router': _L1_ffn_in['w_router'], 'L1_ffn_w_gate': _L1_ffn_in['w_gate'], 'L1_ffn_w_up': _L1_ffn_in['w_up'], 'L1_ffn_w_down': _L1_ffn_in['w_down'], 'L1_ffn_sw_gate': _L1_ffn_in['sw_gate'], 'L1_ffn_sw_up': _L1_ffn_in['sw_up'], 'L1_ffn_sw_down': _L1_ffn_in['sw_down'], 'L1_ffn_w_shared_gate': _L1_ffn_in['w_shared_gate']}

def reference(x, ctx_2048, L0_xattn_ssm_kernel, L0_xattn_D, L0_ffn_gate_w, L0_ffn_w1, L0_ffn_w2, L0_ffn_shared_w1, L0_ffn_shared_w2, L1_xattn_time_decay, L1_xattn_time_first, L1_ffn_w_norm, L1_ffn_w_router, L1_ffn_w_gate, L1_ffn_w_up, L1_ffn_w_down, L1_ffn_sw_gate, L1_ffn_sw_up, L1_ffn_sw_down, L1_ffn_w_shared_gate):
    import jax
    import jax.numpy as jnp

    def _L0_xattn_ref(k, v, q, ssm_kernel, D, head_dim):
        import jax, jax.numpy as jnp
        import numpy as np
        B, HD, L = k.shape
        H = HD // head_dim
        fft_size = 2 * L
        k_ = k.reshape(B, H, head_dim, L)
        v_ = v.reshape(B, H, head_dim, L)
        q_ = q.reshape(B, H, head_dim, L)
        kv = jnp.einsum('bhil,bhjl->bijhl', k_, v_)
        kv_f = jnp.fft.rfft(kv, n=fft_size)
        kernel_f = jnp.fft.rfft(ssm_kernel, n=fft_size)
        y = jnp.fft.irfft(kv_f * kernel_f, n=fft_size)[..., :L]
        out = y + kv * D[None, None, None, :, None]
        out = jnp.einsum('bijhl,bhil->bjhl', out, q_)
        out = jnp.transpose(out, (0, 2, 1, 3)).reshape(B, H * head_dim, L)
        return out.astype(k.dtype)

    def _L0_ffn_ref(x, gate_w, w1, w2, shared_w1, shared_w2):
        import jax, jax.numpy as jnp
        import numpy as np
        H, I, E, TOP_K = (256, 176, 16, 6)
        IS = 352
        NORM_TOPK_PROB = False

        def _silu_and_mul(gate_up):
            d = gate_up.shape[-1] // 2
            g, u = (gate_up[..., :d], gate_up[..., d:])
            return jax.nn.silu(g) * u
        B, S, Hd = x.shape
        xf = x.reshape(-1, Hd)
        T = xf.shape[0]
        shared_out = _silu_and_mul(xf @ shared_w1.T) @ shared_w2.T
        logits = xf @ gate_w.T
        probs = jax.nn.softmax(logits.astype(jnp.float32), axis=-1)
        routing_weights, selected = jax.lax.top_k(probs, TOP_K)
        if NORM_TOPK_PROB:
            routing_weights = routing_weights / routing_weights.sum(-1, keepdims=True)
        combine = jnp.zeros((T, E), jnp.float32).at[jnp.arange(T)[:, None], selected].add(routing_weights).astype(x.dtype)
        gate_up = jnp.einsum('th,eoh->teo', xf, w1)
        act = _silu_and_mul(gate_up)
        moe_out = jnp.einsum('te,tei,ehi->th', combine, act, w2)
        return (moe_out + shared_out).reshape(B, S, Hd)

    def _L1_xattn_ref(batch_size, seq_len, embedding_dim, time_decay, time_first, k, v):
        import jax, jax.numpy as jnp
        import numpy as np

        def _wkv(time_decay, time_first, k, v):
            w = -jnp.exp(time_decay)
            u = time_first
            B, T, C = k.shape
            aa = jnp.zeros((B, C), dtype=k.dtype)
            bb = jnp.zeros((B, C), dtype=k.dtype)
            pp = jnp.full((B, C), -1e+38, dtype=k.dtype)

            def step(carry, kv_t):
                aa, bb, pp = carry
                kt, vt = kv_t
                ww = u + kt
                q = jnp.maximum(pp, ww)
                e1 = jnp.exp(pp - q)
                e2 = jnp.exp(ww - q)
                y_t = (e1 * aa + e2 * vt) / (e1 * bb + e2)
                ww2 = pp + w
                q2 = jnp.maximum(ww2, kt)
                e1b = jnp.exp(ww2 - q2)
                e2b = jnp.exp(kt - q2)
                new_carry = (e1b * aa + e2b * vt, e1b * bb + e2b, q2)
                return (new_carry, y_t)
            ks = jnp.transpose(k, (1, 0, 2))
            vs = jnp.transpose(v, (1, 0, 2))
            _, ys = jax.lax.scan(step, (aa, bb, pp), (ks, vs))
            return jnp.transpose(ys, (1, 0, 2))
        assert seq_len <= 128
        return _wkv(time_decay, time_first, k, v)

    def _L1_ffn_ref(hidden_states, w_norm, w_router, w_gate, w_up, w_down, sw_gate, sw_up, sw_down, w_shared_gate):
        import jax, jax.numpy as jnp
        import numpy as np
        B, S, H = (2, 256, 256)
        E, K, F = (32, 4, 176)
        FS = 704
        EPS = 1e-06
        CAP = 128
        inp = hidden_states
        xf = inp.astype(jnp.float32)
        var = jnp.mean(xf * xf, axis=-1, keepdims=True)
        x = (w_norm * (xf * jax.lax.rsqrt(var + EPS))).astype(inp.dtype)
        Bq, Sq, Hq = x.shape
        x = x.reshape(-1, Hq)
        T = Bq * Sq
        logits = x @ w_router
        probs = jax.nn.softmax(logits.astype(jnp.float32), axis=-1)
        w_topk, sel = jax.lax.top_k(probs, K)
        w_topk = w_topk.astype(x.dtype)
        flat_e = sel.reshape(-1)
        order = jnp.argsort(flat_e)
        sorted_e = flat_e[order]
        counts = jnp.zeros((E,), jnp.int32).at[flat_e].add(1)
        starts = jnp.cumsum(counts) - counts
        pos = jnp.arange(T * K) - starts[sorted_e]
        tok = order // K
        valid = pos < CAP
        dest = jnp.where(valid, pos, CAP)
        buf = jnp.zeros((E, CAP + 1, Hq), x.dtype).at[sorted_e, dest].set(x[tok])
        buf = buf[:, :CAP]
        g = jnp.einsum('ech,ehf->ecf', buf, w_gate)
        u = jnp.einsum('ech,ehf->ecf', buf, w_up)
        y = jnp.einsum('ecf,efh->ech', jax.nn.silu(g) * u, w_down)
        wv = w_topk.reshape(-1)[order] * valid.astype(x.dtype)
        gath = y[sorted_e, jnp.minimum(pos, CAP - 1)]
        out = jnp.zeros((T, Hq), x.dtype).at[tok].add(gath * wv[:, None])
        sh = jax.nn.silu(x @ sw_gate) * (x @ sw_up) @ sw_down
        sh = jax.nn.sigmoid(x @ w_shared_gate) * sh
        out = out + sh
        return inp + out.reshape(Bq, Sq, Hq)
    x = x + _L0_xattn_ref(ctx_2048, ctx_2048, _layernorm(x, axis=-1), L0_xattn_ssm_kernel, L0_xattn_D, 8)
    x = x + _L0_ffn_ref(_layernorm(x, axis=-1), L0_ffn_gate_w, L0_ffn_w1, L0_ffn_w2, L0_ffn_shared_w1, L0_ffn_shared_w2)
    x = x + _L1_xattn_ref(8, 128, 256, L1_xattn_time_decay, L1_xattn_time_first, _layernorm(x, axis=-1), ctx_2048)
    x = x + _L1_ffn_ref(_layernorm(x, axis=-1), L1_ffn_w_norm, L1_ffn_w_router, L1_ffn_w_gate, L1_ffn_w_up, L1_ffn_w_down, L1_ffn_sw_gate, L1_ffn_sw_up, L1_ffn_sw_down, L1_ffn_w_shared_gate)
    return x

_drawn_inputs = setup_inputs


def setup_inputs(seed=0):
    import zlib

    import numpy as np

    out = dict(_drawn_inputs(seed))
    spreads = {}
    factors = {'L0_ffn_gate_w': 8.0,
     'L0_ffn_w1': 8.0,
     'L0_ffn_w2': 8.0,
     'L0_ffn_shared_w1': 8.0,
     'L0_ffn_shared_w2': 8.0,
     'L1_xattn_time_decay': 8.0,
     'L1_xattn_time_first': 8.0,
     'L1_ffn_w_norm': 8.0,
     'L1_ffn_w_router': 8.0,
     'L1_ffn_w_gate': 8.0,
     'L1_ffn_w_up': 8.0,
     'L1_ffn_w_down': 8.0,
     'L1_ffn_sw_gate': 8.0,
     'L1_ffn_sw_up': 8.0,
     'L1_ffn_sw_down': 8.0,
     'L1_ffn_w_shared_gate': 8.0}
    for name, (base, spread) in spreads.items():
        noise = np.random.default_rng([zlib.crc32(name.encode()), seed]).standard_normal(out[name].shape)
        drawn = base * np.exp(spread * noise) if base else spread * noise
        out[name] = jnp.asarray(drawn.astype(out[name].dtype))
    for name, factor in factors.items():
        out[name] = (out[name] * factor).astype(out[name].dtype)
    return out
```

```python
from contextlib import ExitStack

import concourse.bass as bass
from concourse import mybir

F32 = mybir.dt.float32
I32 = mybir.dt.int32
ALU = mybir.AluOpType
ACT = mybir.ActivationFunctionType
AX = mybir.AxisListType

P = 128
NB = 8
C = 256
KT = C // P
NH = 16
HD = 8
F = 176
FH = F // 2
E0, K0, SU0 = 16, 6, 2
E1, K1, SU1 = 32, 4, 4
NT0 = 64
NT1 = E1
NTOK = NB * P
T1 = P + 1
LOW = -1e38
UNUSED = 8192.0
RING = 4


class Steps:

    def __init__(self, sem):
        self.sem, self.n = sem, 0

    def done(self, instruction):
        instruction.then_inc(self.sem, 1)
        self.n += 1
        return self.n


class Layer:

    def __init__(self, number, experts, choices, slices, tiles):
        self.number, self.experts, self.choices, self.slices, self.tiles = number, experts, choices, slices, tiles


def build(nc, x, ctx_t, toep, d_skip, gate0, w1_0, w2_0, sw1_0, sw2_0, decay, first, norm_w,
          gate1, w1_1, w2_1, sw1_1, sw2_1, out):
    stack = ExitStack()
    with stack:
        def sem(name):
            return stack.enter_context(nc.semaphore(name))

        def sb(name, shape, dt=F32):
            return stack.enter_context(nc.sbuf_tensor(name, shape, dt))

        X = sb("X", [P, NB, C])
        CT = sb("CT", [P, KT, NB, P])
        XN = sb("XN", [P, NB, C])
        XNT = sb("XNT", [P, KT, NB, P])
        W1 = sb("W1", [P, E0, KT, 2 * F])
        W2 = sb("W2", [FH, E0, 2, C])
        SW1 = sb("SW1", [P, SU0 + SU1, KT, 2 * F])
        SW2 = sb("SW2", [FH, SU0 + SU1, 2, C])
        GATE0 = sb("GATE0", [P, KT, E0])
        GATE1 = sb("GATE1", [P, KT, E1 + 1])
        NORM_W = sb("NORM_W", [P, C])
        IDENT = sb("IDENT", [P, P])
        UPPER = sb("UPPER", [P, P])
        ONES = sb("ONES", [P, P])
        IOTA = sb("IOTA", [P, P])
        VAL = sb("VAL", [P, K0, NB])
        IOTA_I = sb("IOTA_I", [P, P], I32)
        VAL_I = sb("VAL_I", [P, K0, NB], I32)
        LIM = sb("LIM", [P, NB])
        RES = sb("RES", [P, NB * E1])
        RES1 = sb("RES1", [P, NB * E1])
        RES8 = sb("RES8", [P, E1 * NB])
        DEC = sb("DEC", [P, KT])
        FIRST = sb("FIRST", [P, KT])
        STAT = sb("STAT", [P, NB, 6])
        MV = sb("MV", [P, NB, 2])
        STD = sb("STD", [P, NB])
        RSTD = sb("RSTD", [P, NB])
        PS = stack.enter_context(nc.psum_tensor("PS", [P, 8, 512], F32))

        xn_dram = [nc.dram_tensor(f"xn_rows{i}", [NTOK, C], F32, kind="Internal").ap() for i in range(2)]
        y_dram = [nc.dram_tensor(f"y_rows{i}", [k * NTOK, C], F32, kind="Internal").ap()
                  for i, k in enumerate((K0, K1))]

        loaded_x = sem("loaded_x")
        loaded_ctx = sem("loaded_ctx")
        loaded_toep = sem("loaded_toep")
        loaded_small = sem("loaded_small")
        loaded_w0 = sem("loaded_w0")
        loaded_shared = sem("loaded_shared")
        consts_ready = sem("consts_ready")
        vec = Steps(sem("vector_step"))
        pool = Steps(sem("gpsimd_step"))

        def v_link(instruction):
            nc.vector.wait_ge(vec.sem, vec.done(instruction))

        def p_link(instruction):
            nc.gpsimd.wait_ge(pool.sem, pool.done(instruction))

        def normalize(dve, eps, standard_ready, variance_ready, number, src, dst):
            for i in range(NB):
                v_link(nc.vector.bn_stats(STAT[:, i, :], src[:, i, :]))
                v_link(nc.vector.bn_aggr(MV[:, i, :], STAT[:, i, :]))
            v_link(nc.vector.tensor_scalar(STD[:, :], MV[:, :, 1], eps, None, ALU.add))
            nc.vector.engine_nop().then_inc(variance_ready, 1)
            dve.wait_ge(standard_ready, number)
            v_link(nc.vector.reciprocal(RSTD[:, :], STD[:, :]))
            for i in range(NB):
                v_link(nc.vector.tensor_scalar(dst[:, i, :], src[:, i, :], MV[:, i, 0:1], RSTD[:, i:i + 1],
                                               ALU.subtract, ALU.mult))

        def to_features(pe, done):
            for n in range(4):
                for j in range(4):
                    k, b = n // 2, 4 * (n % 2) + j
                    last = nc.tensor.transpose(PS[:, 4 + n, j * P:(j + 1) * P],
                                               XN[:, b, k * P:(k + 1) * P], IDENT[:, :])
                last.then_inc(done, 1)

        def features_out(act, done, copied, dst):
            for n in range(4):
                act.wait_ge(done, n + 1)
                k, b = n // 2, 4 * (n % 2)
                nc.scalar.activation(dst[:, k, b:b + 4, :], PS[:, 4 + n, :].rearrange("p (b t) -> p b t", b=4),
                                     ACT.Copy).then_inc(copied, 1)

        def to_tokens(pe, src, ready, done):
            for n in range(4):
                for j in range(4):
                    b, k = 2 * n + j // 2, j % 2
                    last = nc.tensor.transpose(PS[:, 4 + n, j * P:(j + 1) * P], src[:, k, b, :], IDENT[:, :])
                last.then_inc(done, 1)

        def add_tokens(dve, done):
            for n in range(4):
                dve.wait_ge(done, n + 1)
                v_link(nc.vector.tensor_tensor(X[:, 2 * n:2 * n + 2, :],
                                               PS[:, 4 + n, :].rearrange("p (b c) -> p b c", b=2),
                                               X[:, 2 * n:2 * n + 2, :], ALU.add))

        a_std = sem("a_std"); a_var = sem("a_var"); a_xn = sem("a_xn"); a_tp = sem("a_tp")
        a_qt = sem("a_qt"); a_toep = sem("a_toep"); a_kv = sem("a_kv"); a_conv = sem("a_conv")
        a_prod = sem("a_prod"); a_out = sem("a_out"); a_back = sem("a_back"); a_dec = sem("a_dec")
        KVR = 3
        with ExitStack() as sa:
            TOEP = sa.enter_context(nc.sbuf_tensor("TOEP", [P, NH, C], F32))
            DSK = sa.enter_context(nc.sbuf_tensor("DSK", [P, NH], F32))
            KV = sa.enter_context(nc.sbuf_tensor("KV", [P, KVR, KT * NB, HD, HD], F32))
            Z = sa.enter_context(nc.sbuf_tensor("Z", [P, 2, NB, HD, HD], F32))
            OT = sa.enter_context(nc.sbuf_tensor("OT", [P, KT, NB, P], F32))
            TD = sa.enter_context(nc.sbuf_tensor("TD", [P, KT], F32))
            block = sa.enter_context(nc.Block())

            @block.sync
            def _(sp):
                sp.dma_start(X[:, :, :], x.rearrange("b p c -> p b c")).then_inc(loaded_x, 16)
                sp.dma_start(CT[:, :, :, :], ctx_t).then_inc(loaded_ctx, 16)
                sp.dma_start(TOEP[:, :, :], toep).then_inc(loaded_toep, 16)
                for q in range(4):
                    sp.dma_start(SW1[:, 0:SU0, :, :] if q == 0 else W1[:, 4 * q:4 * q + 4, :, :],
                                 sw1_0 if q == 0 else w1_0[:, 4 * q:4 * q + 4, :, :]
                                 ).then_inc(loaded_shared if q == 0 else loaded_w0, 16)
                sp.dma_start(W1[:, 0:4, :, :], w1_0[:, 0:4, :, :]).then_inc(loaded_w0, 16)
                sp.dma_start(SW2[:, 0:SU0, :, :], sw2_0).then_inc(loaded_shared, 16)
                sp.dma_start(W2[:, :, :, :], w2_0).then_inc(loaded_w0, 16)
                sp.dma_start(SW1[:, SU0:, :, :], sw1_1).then_inc(loaded_shared, 16)
                sp.dma_start(SW2[:, SU0:, :, :], sw2_1).then_inc(loaded_shared, 16)

            @block.gpsimd
            def _(gp):
                p_link(nc.gpsimd.memset(IDENT[:, :], 0.0))
                p_link(nc.gpsimd.affine_select(out=IDENT[:, :], in_=IDENT[:, :], compare_op=ALU.not_equal, fill=1.0,
                                               base=0, pattern=[[-1, P]], channel_multiplier=1))
                nc.gpsimd.memset(ONES[:, :], 1.0).then_inc(consts_ready, 1)
                gp.wait_ge(loaded_ctx, 16)
                for h in range(NH):
                    if h >= KVR:
                        gp.wait_ge(a_conv, 2 * (h - KVR + 1))
                    c = CT[:, :, :, h * HD:(h + 1) * HD].rearrange("p k b i -> p (k b) i")
                    nc.gpsimd.tensor_tensor(
                        KV[:, h % KVR, :, :, :],
                        c.rearrange("p n (i o) -> p n i o", o=1).broadcast_to([P, KT * NB, HD, HD]),
                        c.rearrange("p n (o i) -> p n o i", o=1).broadcast_to([P, KT * NB, HD, HD]),
                        ALU.mult).then_inc(a_kv, 1)
                p_link(nc.gpsimd.memset(UPPER[:, :], 1.0))
                p_link(nc.gpsimd.affine_select(out=UPPER[:, :], in_=UPPER[:, :], compare_op=ALU.is_ge, fill=0.0,
                                               base=-1, pattern=[[1, P]], channel_multiplier=-1))
                p_link(nc.gpsimd.iota(IOTA_I[:, :], [[1, P]], base=0, channel_multiplier=0))
                p_link(nc.gpsimd.iota(VAL_I[:, :, :], [[NTOK, K0], [P, NB]], base=1, channel_multiplier=1))
                p_link(nc.gpsimd.tensor_copy(IOTA[:, :], IOTA_I[:, :]))
                p_link(nc.gpsimd.tensor_copy(VAL[:, :, :], VAL_I[:, :, :]))
                p_link(nc.gpsimd.tensor_scalar(LIM[:, :], IOTA[:, 0:NB], float(P), None, ALU.mult))
                for r, n in ((RES, E0), (RES1, E1), (RES8, NB)):
                    p_link(nc.gpsimd.memset(r[:, :], 1.0))
                    p_link(nc.gpsimd.memset(r[:, :].rearrange("p (g n) -> p g n", n=n)[:, :, 0:1], 0.0))

            @block.scalar
            def _(act):
                for dst, src in ((DSK[:, :], d_skip), (GATE0[:, :, :], gate0), (GATE1[:, :, :], gate1),
                                 (NORM_W[:, :], norm_w), (TD[:, :], decay), (FIRST[:, :], first)):
                    act.dma_start(dst, src).then_inc(loaded_small, 16)
                act.wait_ge(a_var, 1)
                nc.scalar.activation(STD[:, :], STD[:, :], ACT.Sqrt).then_inc(a_std, 1)
                features_out(act, a_tp, a_qt, XNT)
                act.wait_ge(loaded_small, 96)
                nc.scalar.activation(DEC[:, :], TD[:, :], ACT.Exp).then_inc(a_dec, 1)
                act.wait_ge(a_dec, 1)
                nc.scalar.mul(DEC[:, :], DEC[:, :], -1.0).then_inc(a_dec, 1)

            @block.vector
            def _(dve):
                dve.wait_ge(loaded_x, 16)
                normalize(dve, 1e-5, a_std, a_var, 1, X, XN)
                nc.vector.engine_nop().then_inc(a_xn, 1)
                dve.wait_ge(loaded_toep, 16)
                dve.wait_ge(loaded_small, 96)
                dve.wait_ge(consts_ready, 1)
                for h in range(NH):
                    nc.vector.scalar_tensor_tensor(TOEP[:, h, 0:P], IDENT[:, :], DSK[:, h:h + 1], TOEP[:, h, 0:P],
                                                   ALU.mult, ALU.add).then_inc(a_toep, 1)
                for n in range(2 * NH):
                    h, lt = n // 2, n % 2
                    dve.wait_ge(a_conv, n + 1)
                    dve.wait_ge(a_qt, 2 * lt + 2)
                    if n >= 2:
                        dve.wait_ge(a_out, n - 1)
                    y = PS[:, n % 4, :].rearrange("p (b i j) -> p b j i", b=NB, i=HD)
                    q = XNT[:, lt, :, h * HD:(h + 1) * HD].rearrange("p b (o i) -> p b o i", o=1)
                    nc.vector.tensor_tensor(Z[:, n % 2, :, :, :], y, q.broadcast_to([P, NB, HD, HD]),
                                            ALU.mult).then_inc(a_prod, 1)
                    dve.wait_ge(a_prod, n + 1)
                    nc.vector.tensor_reduce(OT[:, lt, :, h * HD:(h + 1) * HD], Z[:, n % 2, :, :, :], AX.X,
                                            ALU.add).then_inc(a_out, 1)
                add_tokens(dve, a_back)

            @block.tensor
            def _(pe):
                pe.wait_ge(consts_ready, 1)
                pe.wait_ge(a_xn, 1)
                to_features(pe, a_tp)
                for h in range(NH):
                    pe.wait_ge(a_kv, h + 1)
                    pe.wait_ge(a_toep, h + 1)
                    for lt in range(KT):
                        n = 2 * h + lt
                        if n >= 4:
                            pe.wait_ge(a_prod, n - 3)
                        kv = KV[:, h % KVR, :, :, :].rearrange("p (k b) i j -> p k (b i j)", k=KT)
                        if lt == 0:
                            last = nc.tensor.matmul(PS[:, n % 4, :], TOEP[:, h, 0:P], kv[:, 0, :], start=True, stop=True)
                        else:
                            nc.tensor.matmul(PS[:, n % 4, :], TOEP[:, h, P:C], kv[:, 0, :], start=True, stop=False)
                            last = nc.tensor.matmul(PS[:, n % 4, :], TOEP[:, h, 0:P], kv[:, 1, :],
                                                    start=False, stop=True)
                        last.then_inc(a_conv, 1)
                pe.wait_ge(a_out, 2 * NH)
                pe.wait_ge(a_qt, 4)
                to_tokens(pe, OT, None, a_back)

        def routed(lay):
            L, E, K, SU, NT = lay.number, lay.experts, lay.choices, lay.slices, lay.tiles
            S0 = 0 if L == 0 else SU0
            G = E + (1 if L else 0)
            s = lambda name: sem(f"r{L}_{name}")
            var, std, xn_ok, tp, xnt, xn_rows = s("var"), s("std"), s("xn"), s("tp"), s("xnt"), s("xn_rows")
            ms, msr = s("ms"), s("msr")
            logit, shifted, expd, sel_ok, counts, onehot_b, table, tables_ok = (
                s("logit"), s("shifted"), s("exp"), s("sel"), s("counts"), 
                s("onehot_b"), s("table"), s("tables"))
            gathered = [s(f"gathered{i}") for i in range(RING)]
            scattered = [s(f"scattered{i}") for i in range(RING)]
            zeroed = s("zeroed")
            tx, xgt, gu, silu, hid, ta, at, dn, yout = (
                s("tx"), s("xgt"), s("gu"), s("silu"), s("hid"), s("ta"), s("at"), s("dn"), s("yout"))
            ygot = [s(f"ygot{i}") for i in range(2)]
            yused, final, stored, weights = s("yused"), s("final"), s("stored"), s("weights")
            acc_zero = s("acc")
            NS = NB * SU
            N = NS + NT

            with ExitStack() as sr:
                def rb(name, shape, dt=F32):
                    return sr.enter_context(nc.sbuf_tensor(f"{name}_{L}", shape, dt))
                SH = rb("SH", [P, NB, E]); EX = rb("EX", [P, NB, E]); PR = rb("PR", [P, NB, E])
                GT = rb("GT", [P, NB, E]); EQ = rb("EQ", [P, NB, E]); CE = rb("CE", [P, NB, E])
                SEL = rb("SEL", [P, NB, E]); RK = rb("RK", [P, NB, E]); TMP = rb("TMP", [P, NB, E])
                TOT = rb("TOT", [P, E, NB]); INC = rb("INC", [P, E, NB]); CMP = rb("CMP", [P, E, NB])
                POS = rb("POS", [P, NB, E]); EID = rb("EID", [P, NB, E])
                M8 = rb("M8", [P, NB, 8]); MX = rb("MX", [P, NB]); NEED = rb("NEED", [P, NB])
                NTE = rb("NTE", [P, E]); ENDS = rb("ENDS", [P, E]); BASE = rb("BASE", [P, E])
                CK = rb("CK", [P, K, NB]); JK = rb("JK", [P, K, NB]); WK = rb("WK", [P, K, NB])
                GI = rb("GI", [P, K, NB], I32); CI = rb("CI", [P, K, NB], I32); JI = rb("JI", [P, K, NB], I32)
                OHA = rb("OHA", [P, 2, NB, P]); OHB = rb("OHB", [P, 2, NB, NT])
                ETC = rb("ETC", [1, NT, E]); ETF = rb("ETF", [1, NT]); ETI = rb("ETI", [1, NT], I32)
                DZ = rb("DZ", [P, NT]); DF = rb("DF", [P, NT]); DST = rb("DST", [P, NT], I32)
                SRC = rb("SRC", [P, NT], I32)
                SIG = rb("SIG", [P, NB])
                XG = rb("XG", [P, RING, C]); XGT = rb("XGT", [P, 2, KT, P])
                SG = rb("SG", [P, 2, F]); HID = rb("HID", [P, 2, F]); AT = rb("AT", [FH, 2, 2, P])
                Y = rb("Y", [P, RING, C]); YL = rb("YL", [P, 2, K, C])
                block = sr.enter_context(nc.Block())
                lg = PS[:, 0, 0:NB * G].rearrange("p (i e) -> p i e", e=G)
                pw = PS[:, 1, 0:NB * E].rearrange("p (i e) -> p i e", e=E)
                tot = PS[:, 2, 0:NB * E].rearrange("p (i e) -> p e i", e=E)
                tab = PS[:, 3, 0:NT]
                b_gu, b_tx, b_ta, b_dn = 0, 2, 4, 6

                def per_tile(a, n=E):
                    return a[:, :].rearrange("p (i o) -> p i o", o=1).broadcast_to([P, NB, n])

                @block.sync
                def _(sp):
                    if L == 1:
                        lay.load_ring(sp, dn, NS)
                    sp.wait_ge(xn_ok, 1)
                    sp.dma_start(xn_dram[L].rearrange("(i p) c -> p i c", p=P), XN[:, :, :]).then_inc(xn_rows, 16)
                    if L == 1:
                        lay.load_rest(sp, dn, NS)
                    for r in range(RING):
                        sp.wait_ge(scattered[r], 16 * (NT // RING))
                    yv = y_dram[L].rearrange("(k i p) c -> i p k c", k=K, p=P)
                    for i in range(NB):
                        if i >= 2:
                            sp.wait_ge(yused, i - 1)
                        sp.dma_start(YL[:, i % 2, :, :], yv[i]).then_inc(ygot[i % 2], 16)
                    if L == 1:
                        for i in range(NB):
                            sp.wait_ge(final, i + 1)
                            sp.dma_start(out[i], X[:, i, :]).then_inc(stored, 16)
                        sp.wait_ge(stored, 16 * NB)

                @block.gpsimd
                def _(gp):
                    gp.wait_ge(tables_ok, 1)
                    gp.wait_ge(xn_rows, 16)
                    if L == 1:
                        gp.wait_ge(lay.zero_rows, 16 * 8)

                    def gather(j):
                        if j >= RING:
                            gp.wait_ge(tx, j - RING + 1)
                        nc.gpsimd.indirect_dma_start(
                            XG[:, j % RING, :], None, xn_dram[L],
                            bass.IndirectOffsetOnAxis(ap=SRC[:, j:j + 1], axis=0)).then_inc(gathered[j % RING], 16)

                    def scatter(j):
                        gp.wait_ge(yout, j + 1)
                        nc.gpsimd.indirect_dma_start(
                            y_dram[L], bass.IndirectOffsetOnAxis(ap=DST[:, j:j + 1], axis=0),
                            Y[:, j % RING, :], None, bounds_check=K * NTOK - 1,
                            oob_is_err=False).then_inc(scattered[j % RING], 16)
                    for j in range(NT + 3):
                        if j < NT:
                            gather(j)
                        if j >= 3:
                            scatter(j - 3)

                @block.scalar
                def _(act):
                    act.wait_ge(var, 1)
                    nc.scalar.activation(STD[:, :], STD[:, :], ACT.Sqrt).then_inc(std, 1)
                    if L == 1:
                        act.wait_ge(ms, 1)
                        nc.scalar.activation(STD[:, :], STD[:, :], ACT.Sqrt).then_inc(msr, 1)
                    features_out(act, tp, xnt, XNT)
                    act.wait_ge(shifted, 1)
                    nc.scalar.activation(EX[:, :, :], SH[:, :, :], ACT.Exp).then_inc(expd, 1)
                    if L == 1:
                        nc.scalar.activation(SIG[:, :], lg[:, :, E], ACT.Exp, scale=-1.0).then_inc(expd, 1)

                    def unit_silu(n, s_):
                        act.wait_ge(gu, n + 1)
                        act.wait_ge(hid, n - 1) if not isinstance(n, int) or n >= 2 else None
                        nc.scalar.activation(SG[:, s_, :], PS[:, b_gu + s_, 0:F], ACT.Silu).then_inc(silu, 1)

                    def unit_at(n, s_):
                        act.wait_ge(ta, n + 1)
                        act.wait_ge(dn, n - 1) if not isinstance(n, int) or n >= 2 else None
                        nc.scalar.activation(AT[:, s_, :, :],
                                             PS[0:FH, b_ta + s_, 0:2 * P].rearrange("p (k t) -> p k t", k=2),
                                             ACT.Copy).then_inc(at, 1)

                    def unit_y(n, s_, r, j):
                        act.wait_ge(dn, n + 1)
                        if not isinstance(j, int) or j >= RING:
                            act.wait_ge(scattered[r], lay.sent(j, r))
                        nc.scalar.activation(Y[:, r, :], PS[:, b_dn + s_, 0:C], ACT.Copy).then_inc(yout, 1)

                    for n in range(N + 1):
                        if n >= 1:
                            unit_at(n - 1, (n - 1) % 2)
                        if n < N:
                            unit_silu(n, n % 2)
                        j = n - 2 - NS
                        if j >= 0:
                            unit_y(n - 2, n % 2, j % RING, j)
                    unit_y(N - 1, (N - 1) % 2, (NT - 1) % RING, NT - 1)

                @block.vector
                def _(dve):
                    normalize(dve, 1e-5, std, var, 1, X, XN)
                    if L == 1:
                        for i in range(NB):
                            v_link(nc.vector.tensor_tensor(X[:, i, :], X[:, i, :], XN[:, i, :], ALU.add))
                            v_link(nc.vector.bn_stats(STAT[:, i, :], XN[:, i, :]))
                            v_link(nc.vector.bn_aggr(MV[:, i, :], STAT[:, i, :]))
                        v_link(nc.vector.tensor_tensor(MV[:, :, 0], MV[:, :, 0], MV[:, :, 0], ALU.mult))
                        v_link(nc.vector.scalar_tensor_tensor(STD[:, :], MV[:, :, 1], 1e-6, MV[:, :, 0],
                                                              ALU.add, ALU.add))
                        nc.vector.engine_nop().then_inc(ms, 1)
                        dve.wait_ge(msr, 1)
                        v_link(nc.vector.reciprocal(RSTD[:, :], STD[:, :]))
                        for i in range(NB):
                            v_link(nc.vector.scalar_tensor_tensor(XN[:, i, :], XN[:, i, :], RSTD[:, i:i + 1],
                                                                  NORM_W[:, :], ALU.mult, ALU.mult))
                    nc.vector.engine_nop().then_inc(xn_ok, 1)

                    dve.wait_ge(logit, 1)
                    v_link(nc.vector.tensor_reduce(MX[:, :], lg[:, :, 0:E], AX.X, ALU.max))
                    nc.vector.tensor_tensor(SH[:, :, :], lg[:, :, 0:E], per_tile(MX), ALU.subtract).then_inc(shifted, 1)
                    dve.wait_ge(expd, 1 + L)
                    v_link(nc.vector.tensor_reduce(MX[:, :], EX[:, :, :], AX.X, ALU.add))
                    v_link(nc.vector.reciprocal(MX[:, :], MX[:, :]))
                    v_link(nc.vector.tensor_tensor(PR[:, :, :], EX[:, :, :], per_tile(MX), ALU.mult))
                    if L == 1:
                        v_link(nc.vector.tensor_scalar(SIG[:, :], SIG[:, :], 1.0, None, ALU.add))
                        v_link(nc.vector.reciprocal(SIG[:, :], SIG[:, :]))
                    for i in range(NB):
                        v_link(nc.vector.max(M8[:, i, :], PR[:, i, :]))
                    kth = M8[:, :, K - 1:K].broadcast_to([P, NB, E])
                    v_link(nc.vector.tensor_tensor(GT[:, :, :], PR[:, :, :], kth, ALU.is_gt))
                    v_link(nc.vector.tensor_tensor(EQ[:, :, :], PR[:, :, :], kth, ALU.is_equal))
                    v_link(nc.vector.tensor_reduce(MX[:, :], GT[:, :, :], AX.X, ALU.add))
                    v_link(nc.vector.tensor_scalar(NEED[:, :], MX[:, :], -1.0, float(K), ALU.mult, ALU.add))
                    flat = lambda a: a[:, :, :].rearrange("p a b -> p (a b)")
                    resets = (RES1 if L else RES)[:, 0:NB * E]
                    v_link(nc.vector.tensor_tensor_scan(flat(CE), resets, flat(EQ), 0.0, ALU.mult, ALU.add))
                    v_link(nc.vector.tensor_tensor(CE[:, :, :], CE[:, :, :], per_tile(NEED), ALU.is_le))
                    v_link(nc.vector.tensor_tensor(EQ[:, :, :], EQ[:, :, :], CE[:, :, :], ALU.mult))
                    v_link(nc.vector.tensor_tensor(SEL[:, :, :], GT[:, :, :], EQ[:, :, :], ALU.add))
                    nc.vector.engine_nop().then_inc(sel_ok, 1)
                    v_link(nc.vector.tensor_tensor_scan(flat(RK), resets, flat(SEL), 0.0, ALU.mult, ALU.add))
                    dve.wait_ge(counts, 1)
                    v_link(nc.vector.tensor_copy(TOT[:, :, :], tot))
                    v_link(nc.vector.tensor_tensor_scan(flat(INC), RES8[:, 0:NB * E], flat(TOT), 0.0,
                                                        ALU.mult, ALU.add))
                    if L == 0:
                        total = INC[:, :, NB - 1:NB].broadcast_to([P, E, NB])
                        lim = LIM[:, :].rearrange("p (o i) -> p o i", o=1).broadcast_to([P, E, NB])
                        v_link(nc.vector.tensor_tensor(CMP[:, :, :], total, lim, ALU.is_gt))
                        v_link(nc.vector.tensor_reduce(NTE[:, :], CMP[:, :, :], AX.X, ALU.add))
                        v_link(nc.vector.tensor_tensor_scan(ENDS[:, :], ONES[:, 0:E], NTE[:, :], 0.0,
                                                            ALU.mult, ALU.add))
                        v_link(nc.vector.tensor_tensor(BASE[:, :], ENDS[:, :], NTE[:, :], ALU.subtract))
                        v_link(nc.vector.tensor_tensor(
                            ETC[:, :, :], IOTA[0:1, 0:NT].rearrange("p (j o) -> p j o", o=1).broadcast_to([1, NT, E]),
                            ENDS[0:1, :].rearrange("p (o e) -> p o e", o=1).broadcast_to([1, NT, E]), ALU.is_ge))
                        v_link(nc.vector.tensor_reduce(ETF[:, :], ETC[:, :, :], AX.X, ALU.add))
                        v_link(nc.vector.tensor_scalar(ETF[:, :], ETF[:, :], float(E - 1), None, ALU.min))
                        v_link(nc.vector.tensor_copy(ETI[:, :], ETF[:, :]))
                    v_link(nc.vector.tensor_tensor(INC[:, :, :], INC[:, :, :], TOT[:, :, :], ALU.subtract))
                    v_link(nc.vector.tensor_tensor(POS[:, :, :], pw, INC[:, :, :].rearrange("p e i -> p i e"), ALU.add))
                    if L == 0:
                        base = BASE[:, :].rearrange("p (o e) -> p o e", o=1).broadcast_to([P, NB, E])
                        v_link(nc.vector.tensor_scalar(BASE[:, :], BASE[:, :], float(P), None, ALU.mult))
                        v_link(nc.vector.tensor_tensor(POS[:, :, :], POS[:, :, :], base, ALU.add))
                    else:
                        v_link(nc.vector.scalar_tensor_tensor(flat(SEL), flat(POS), float(P), flat(SEL),
                                                              ALU.is_lt, ALU.mult))
                        eid = IOTA[:, 1:E + 1].rearrange("p (o e) -> p o e", o=1).broadcast_to([P, NB, E])
                        v_link(nc.vector.tensor_tensor(EID[:, :, :], SEL[:, :, :], eid, ALU.mult))
                    v_link(nc.vector.scalar_tensor_tensor(flat(POS), flat(POS), 1.0, flat(SEL), ALU.add, ALU.mult))
                    v_link(nc.vector.tensor_tensor(PR[:, :, :], PR[:, :, :], SEL[:, :, :], ALU.mult))
                    for k in range(K):
                        picks = [(POS, CK), (PR, WK)] + ([(EID, JK)] if L else [])
                        for src, dst in picks:
                            v_link(nc.vector.scalar_tensor_tensor(flat(TMP), flat(RK), float(k + 1), flat(src),
                                                                  ALU.is_equal, ALU.mult))
                            v_link(nc.vector.tensor_reduce(dst[:, k, :], TMP[:, :, :], AX.X, ALU.add))
                    if L == 0:
                        v_link(nc.vector.tensor_scalar(CK[:, :, :], CK[:, :, :], -1.0, None, ALU.add))
                        v_link(nc.vector.tensor_copy(GI[:, :, :], CK[:, :, :]))
                        v_link(nc.vector.tensor_scalar(CI[:, :, :], GI[:, :, :], P - 1, None, ALU.bitwise_and))
                        v_link(nc.vector.tensor_scalar(JI[:, :, :], GI[:, :, :], 7, None, ALU.logical_shift_right))
                        v_link(nc.vector.tensor_copy(CK[:, :, :], CI[:, :, :]))
                        v_link(nc.vector.tensor_copy(JK[:, :, :], JI[:, :, :]))
                    else:
                        v_link(nc.vector.tensor_scalar(CK[:, :, :], CK[:, :, :], -1.0, None, ALU.add))
                        v_link(nc.vector.tensor_scalar(JK[:, :, :], JK[:, :, :], -1.0, None, ALU.add))
                    for k in range(K):
                        if k >= 2:
                            dve.wait_ge(table, k - 1)
                        for i in range(NB):
                            nc.vector.tensor_scalar(OHA[:, k % 2, i, :], IOTA[:, :], CK[:, k, i:i + 1], None,
                                                    ALU.is_equal)
                            last = nc.vector.tensor_scalar(OHB[:, k % 2, i, :], IOTA[:, 0:NT], JK[:, k, i:i + 1],
                                                           VAL[:, k, i:i + 1], ALU.is_equal, ALU.mult)
                        last.then_inc(onehot_b, 1)
                    dve.wait_ge(table, K)
                    v_link(nc.vector.tensor_scalar(DZ[:, :], tab, 0.0, UNUSED, ALU.is_equal, ALU.mult))
                    v_link(nc.vector.scalar_tensor_tensor(DF[:, :], tab, -1.0, DZ[:, :], ALU.add, ALU.add))
                    v_link(nc.vector.tensor_copy(DST[:, :], DF[:, :]))
                    v_link(nc.vector.tensor_scalar(SRC[:, :], DST[:, :], NTOK - 1, None, ALU.bitwise_and))
                    nc.vector.engine_nop().then_inc(tables_ok, 1)

                    def unit_hidden(n, s_):
                        dve.wait_ge(silu, n + 1)
                        if not isinstance(n, int) or n >= 2:
                            dve.wait_ge(ta, n - 1)
                        nc.vector.tensor_tensor(HID[:, s_, :], SG[:, s_, :], PS[:, b_gu + s_, F:2 * F],
                                                ALU.mult).then_inc(hid, 1)

                    def unit_rows(j, s_, g):
                        dve.wait_ge(tx, j + 1)
                        if not isinstance(j, int) or j >= 2:
                            dve.wait_ge(gu, NS + j - 1)
                        nc.vector.tensor_copy(XGT[:, s_, :, :],
                                              PS[:, b_tx + s_, 0:C].rearrange("p (k t) -> p k t", k=KT)).then_inc(xgt, 1)

                    def shared_out(i, bank):
                        dve.wait_ge(dn, (i + 1) * SU)
                        if L == 0:
                            v_link(nc.vector.tensor_tensor(X[:, i, :], PS[:, bank, 0:C], X[:, i, :], ALU.add))
                        else:
                            v_link(nc.vector.scalar_tensor_tensor(X[:, i, :], PS[:, bank, 0:C], SIG[:, i:i + 1],
                                                                  X[:, i, :], ALU.mult, ALU.add))
                        nc.vector.engine_nop().then_inc(acc_zero, 1)

                    for n in range(N + 2):
                        j = n + 1 - NS
                        if 0 <= j < NT:
                            unit_rows(j, j % 2, RING)
                        if n < N:
                            unit_hidden(n, n % 2)
                        m = n - 2
                        if 0 <= m < NS and (m + 1) % SU == 0:
                            shared_out(m // SU, b_dn + (m // SU) % 2)
                    for i in range(NB):
                        dve.wait_ge(ygot[i % 2], 16 * (i // 2 + 1))
                        for k in range(K):
                            ins = nc.vector.scalar_tensor_tensor(X[:, i, :], YL[:, i % 2, k, :], WK[:, k, i:i + 1],
                                                                 X[:, i, :], ALU.mult, ALU.add)
                            v_link(ins)
                        nc.vector.engine_nop().then_inc(yused, 1)
                        nc.vector.engine_nop().then_inc(final, 1)

                @block.tensor
                def _(pe):
                    pe.wait_ge(xn_ok, 1)
                    to_features(pe, tp)
                    pe.wait_ge(xnt, 4)
                    gate = GATE1 if L else GATE0
                    for i in range(NB):
                        for k in range(KT):
                            last = nc.tensor.matmul(lg[:, i, :], XNT[:, k, i, :], gate[:, k, :],
                                                    start=(k == 0), stop=(k == KT - 1))
                    last.then_inc(logit, 1)
                    pe.wait_ge(sel_ok, 1)
                    flat = SEL[:, :, :].rearrange("p a b -> p (a b)")
                    nc.tensor.matmul(PS[:, 1, 0:NB * E], UPPER[:, :], flat, start=True, stop=True)
                    nc.tensor.matmul(PS[:, 2, 0:NB * E], ONES[:, :], flat, start=True, stop=True).then_inc(counts, 1)
                    for k in range(K):
                        pe.wait_ge(onehot_b, k + 1)
                        for i in range(NB):
                            last = nc.tensor.matmul(tab, OHA[:, k % 2, i, :], OHB[:, k % 2, i, :],
                                                    start=(k == 0 and i == 0), stop=(k == K - 1 and i == NB - 1))
                        last.then_inc(table, 1)
                    pe.wait_ge(tables_ok, 1)
                    pe.wait_ge(loaded_shared, 64)
                    lay.wait_weights(pe, None)

                    def rows(j, s_, r, cnt):
                        pe.wait_ge(gathered[r], cnt)
                        if not isinstance(j, int) or j >= 2:
                            pe.wait_ge(xgt, j - 1)
                        for k in range(KT):
                            last = nc.tensor.transpose(PS[:, b_tx + s_, k * P:(k + 1) * P],
                                                       XG[:, r, k * P:(k + 1) * P], IDENT[:, :])
                        last.then_inc(tx, 1)

                    def gate_up(n, s_, lhs, w):
                        if not isinstance(n, int) or n >= 2:
                            pe.wait_ge(hid, n - 1)
                        for k in range(KT):
                            last = nc.tensor.matmul(PS[:, b_gu + s_, 0:2 * F], lhs(k), w(k),
                                                    start=(k == 0), stop=(k == KT - 1))
                        last.then_inc(gu, 1)

                    def hidden_t(n, s_):
                        pe.wait_ge(hid, n + 1)
                        if not isinstance(n, int) or n >= 2:
                            pe.wait_ge(at, n - 1)
                        for k in range(2):
                            last = nc.tensor.transpose(PS[0:FH, b_ta + s_, k * P:(k + 1) * P],
                                                       HID[:, s_, k * FH:(k + 1) * FH], IDENT[:, :])
                        last.then_inc(ta, 1)

                    def down(n, s_, bank, w, start=True, stop=True):
                        pe.wait_ge(at, n + 1)
                        for k in range(2):
                            last = nc.tensor.matmul(PS[:, bank, 0:C], AT[:, s_, k, :], w(k),
                                                    start=(start and k == 0), stop=(stop and k == 1))
                        last.then_inc(dn, 1)

                    def down_unit(n):
                        if n < NS:
                            i, u = n // SU, n % SU
                            if u == 0 and i >= 2:
                                pe.wait_ge(acc_zero, i - 1)
                            down(n, n % 2, b_dn + i % 2, lambda k: SW2[:, S0 + u, k, :], u == 0, u == SU - 1)
                        else:
                            j = n - NS
                            if j < 2:
                                pe.wait_ge(acc_zero, NB)
                            else:
                                pe.wait_ge(yout, j - 1)
                            w2 = lay.down_weights(pe, j)
                            down(n, n % 2, b_dn + n % 2, w2)

                    for n in range(N + 1):
                        if n >= 1:
                            hidden_t(n - 1, (n - 1) % 2)
                        j = n + 1 - NS
                        if 0 <= j < NT:
                            rows(j, j % 2, j % RING, 16 * (j // RING + 1))
                        if n < NS:
                            i, u = n // SU, n % SU
                            gate_up(n, n % 2, lambda k: XNT[:, k, i, :], lambda k: SW1[:, S0 + u, k, :])
                        elif n < N:
                            j = n - NS
                            pe.wait_ge(xgt, j + 1)
                            w1 = lay.up_weights(pe, j, ETI)
                            gate_up(n, n % 2, lambda k: XGT[:, j % 2, k, :], w1)
                        if n >= 1:
                            down_unit(n - 1)

        lay0 = Layer(number=0, experts=E0, choices=K0, slices=SU0, tiles=NT0)
        lay0.sent = lambda j, r: 16 * (j // RING)
        lay0.wait_weights = lambda pe, j: pe.wait_ge(loaded_w0, 80)
        held = {}

        def up0(pe, j, eti):
            e = pe.value_load(eti[0:1, j:j + 1], min_val=0, max_val=E0 - 1)
            held[j] = e
            return lambda k: W1[:, bass.ds(e, 1), k, :].rearrange("p o n -> p (o n)")

        def down0(pe, j):
            e = held.pop(j)
            return lambda k: W2[:, bass.ds(e, 1), k, :].rearrange("p o n -> p (o n)")
        lay0.up_weights, lay0.down_weights = up0, down0
        routed(lay0)

        ring_w1 = [sem(f"ring_up{i}") for i in range(4)]
        ring_w2 = [sem(f"ring_down{i}") for i in range(4)]
        zero_rows = sem("zero_rows")
        c_std = sem("c_std"); c_var = sem("c_var"); c_xn = sem("c_xn"); c_tp = sem("c_tp"); c_kt = sem("c_kt")
        c_pad = sem("c_pad"); c_diff = sem("c_diff"); c_exp = sem("c_exp"); c_y = sem("c_y"); c_back = sem("c_back")
        c_zero = sem("c_zero")
        with ExitStack() as sc:
            def cb(name):
                return sc.enter_context(nc.sbuf_tensor(name, [P, KT, NB, T1], F32))
            KX = cb("KX"); WF = cb("WF"); PP = cb("PP"); E1B = cb("E1B"); E2B = cb("E2B"); KB = cb("KB")
            AA = sc.enter_context(nc.sbuf_tensor("AA", [P, NB, T1], F32))
            BB = sc.enter_context(nc.sbuf_tensor("BB", [P, NB, T1], F32))
            D3 = XNT
            D4 = XN[:, :, :].rearrange("p b c -> p (b c)").rearrange("p (k b t) -> p k b t", k=KT, b=NB)
            ZR = sc.enter_context(nc.sbuf_tensor("ZR", [P, 1024], F32))
            block = sc.enter_context(nc.Block())

            @block.sync
            def _(sp):
                sp.wait_ge(c_zero, 1)
                z = y_dram[1].rearrange("(g p r) c -> g p (r c)", p=P, r=4)
                for g in range(8):
                    sp.dma_start(z[g], ZR[:, :]).then_inc(zero_rows, 16)
                for q in range(4):
                    sp.dma_start(W1[:, 4 * q:4 * q + 4, :, :], w1_1[:, 4 * q:4 * q + 4, :, :]).then_inc(ring_w1[q], 16)
                    sp.dma_start(W2[:, 4 * q:4 * q + 4, :, :], w2_1[:, 4 * q:4 * q + 4, :, :]).then_inc(ring_w2[q], 16)

            @block.gpsimd
            def _(gp):
                nc.gpsimd.memset(ZR[:, :], 0.0).then_inc(c_zero, 1)
                p_link(nc.gpsimd.memset(WF[:, :, :, :], 0.0))
                for k in range(KT):
                    p_link(nc.gpsimd.tensor_scalar(WF[:, k, :, :], WF[:, k, :, :], DEC[:, k:k + 1], None, ALU.add))
                p_link(nc.gpsimd.memset(WF[:, :, :, 0:1], LOW))
                nc.gpsimd.memset(KX[:, :, :, 0:1], LOW)
                for a in (E1B, E2B, KB):
                    last = nc.gpsimd.memset(a[:, :, :, 0:1], 0.0)
                last.then_inc(c_pad, 1)

            @block.scalar
            def _(act):
                act.wait_ge(c_var, 1)
                nc.scalar.activation(STD[:, :], STD[:, :], ACT.Sqrt).then_inc(c_std, 1)
                features_out(act, c_tp, c_kt, KX[:, :, :, 1:T1])
                for k in range(KT):
                    act.wait_ge(c_diff, 4 * k + 1)
                    nc.scalar.activation(E1B[:, k, :, 1:T1], E1B[:, k, :, 1:T1], ACT.Exp,
                                         bias=DEC[:, k:k + 1]).then_inc(c_exp, 1)
                    act.wait_ge(c_diff, 4 * k + 2)
                    nc.scalar.activation(E2B[:, k, :, 1:T1], E2B[:, k, :, 1:T1], ACT.Exp).then_inc(c_exp, 1)
                    act.wait_ge(c_diff, 4 * k + 3)
                    nc.scalar.activation(D3[:, k, :, :], D3[:, k, :, :], ACT.Exp).then_inc(c_exp, 1)
                    act.wait_ge(c_diff, 4 * k + 4)
                    nc.scalar.activation(D4[:, k, :, :], D4[:, k, :, :], ACT.Exp, scale=-1.0).then_inc(c_exp, 1)

            @block.vector
            def _(dve):
                normalize(dve, 1e-5, c_std, c_var, 1, X, XN)
                nc.vector.engine_nop().then_inc(c_xn, 1)
                dve.wait_ge(c_pad, 1)
                dve.wait_ge(c_kt, 4)
                two = lambda a, k: a[:, k, :, :].rearrange("p b t -> p (b t)")
                for k in range(KT):
                    v_link(nc.vector.tensor_tensor_scan(two(PP, k), two(WF, k), two(KX, k), 0.0, ALU.add, ALU.max))
                    prev, cur = PP[:, k, :, 0:P], PP[:, k, :, 1:T1]
                    kx = KX[:, k, :, 1:T1]
                    nc.vector.tensor_tensor(E1B[:, k, :, 1:T1], prev, cur, ALU.subtract).then_inc(c_diff, 1)
                    nc.vector.tensor_tensor(E2B[:, k, :, 1:T1], kx, cur, ALU.subtract).then_inc(c_diff, 1)
                    v_link(nc.vector.scalar_tensor_tensor(D4[:, k, :, :], prev, FIRST[:, k:k + 1], kx,
                                                          ALU.subtract, ALU.subtract))
                    v_link(nc.vector.tensor_scalar(D3[:, k, :, :], D4[:, k, :, :], 0.0, None, ALU.min))
                    nc.vector.engine_nop().then_inc(c_diff, 1)
                    v_link(nc.vector.tensor_scalar(D4[:, k, :, :], D4[:, k, :, :], 0.0, None, ALU.max))
                    nc.vector.engine_nop().then_inc(c_diff, 1)
                for k in range(KT):
                    v = CT[:, k, :, :]
                    dve.wait_ge(c_exp, 4 * k + 2)
                    v_link(nc.vector.tensor_tensor(KB[:, k, :, 1:T1], E2B[:, k, :, 1:T1], v, ALU.mult))
                    v_link(nc.vector.tensor_tensor_scan(AA[:, :, :].rearrange("p b t -> p (b t)"), two(E1B, k), two(KB, k), 0.0, ALU.mult, ALU.add))
                    v_link(nc.vector.tensor_tensor_scan(BB[:, :, :].rearrange("p b t -> p (b t)"), two(E1B, k), two(E2B, k), 0.0, ALU.mult, ALU.add))
                    dve.wait_ge(c_exp, 4 * k + 4)
                    aap, bbp = AA[:, :, 0:P], BB[:, :, 0:P]
                    num, den = KB[:, k, :, 0:P], E2B[:, k, :, 0:P]
                    v_link(nc.vector.tensor_tensor(num, D3[:, k, :, :], aap, ALU.mult))
                    v_link(nc.vector.tensor_tensor(den, D3[:, k, :, :], bbp, ALU.mult))
                    v_link(nc.vector.tensor_tensor(den, den, D4[:, k, :, :], ALU.add))
                    v_link(nc.vector.tensor_tensor(D4[:, k, :, :], D4[:, k, :, :], v, ALU.mult))
                    v_link(nc.vector.tensor_tensor(num, num, D4[:, k, :, :], ALU.add))
                    v_link(nc.vector.reciprocal(den, den))
                    v_link(nc.vector.tensor_tensor(D3[:, k, :, :], num, den, ALU.mult))
                nc.vector.engine_nop().then_inc(c_y, 1)
                add_tokens(dve, c_back)

            @block.tensor
            def _(pe):
                pe.wait_ge(c_xn, 1)
                to_features(pe, c_tp)
                pe.wait_ge(c_kt, 4)
                pe.wait_ge(c_y, 1)
                to_tokens(pe, D3, None, c_back)

        lay1 = Layer(number=1, experts=E1, choices=K1, slices=SU1, tiles=NT1)
        lay1.zero_rows = zero_rows
        lay1.sent = lambda j, r: 16 * (j // RING)
        lay1.wait_weights = lambda pe, j: None

        def load_rest(sp, dn, ns):
            for q in range(4, 8):
                sp.wait_ge(dn, ns + 4 * (q - 3))
                s4 = 4 * (q - 4)
                sp.dma_start(W1[:, s4:s4 + 4, :, :], w1_1[:, 4 * q:4 * q + 4, :, :]).then_inc(ring_w1[q - 4], 16)
                sp.dma_start(W2[:, s4:s4 + 4, :, :], w2_1[:, 4 * q:4 * q + 4, :, :]).then_inc(ring_w2[q - 4], 16)
        lay1.load_ring = lambda sp, dn, ns: None
        lay1.load_rest = load_rest

        def up1(pe, j, eti):
            q = j // 4
            pe.wait_ge(ring_w1[q % 4], 16 * (q // 4 + 1))
            return lambda k: W1[:, j % 16, k, :]

        def down1(pe, j):
            q = j // 4
            pe.wait_ge(ring_w2[q % 4], 16 * (q // 4 + 1))
            return lambda k: W2[:, j % 16, k, :]
        lay1.up_weights, lay1.down_weights = up1, down1
        routed(lay1)


_ORDER = ["x", "ctx_t", "toep", "d_skip", "gate0", "w1_0", "w2_0", "sw1_0", "sw2_0", "decay", "first",
          "norm_w", "gate1", "w1_1", "w2_1", "sw1_1", "sw2_1"]


def kernel(**inputs):
    import numpy as np
    import concourse.bacc as bacc
    from concourse.bass_utils import run_bass_kernel_spmd

    g = {k: np.asarray(v) for k, v in inputs.items()}

    def rows_first(a):
        a = a.reshape(*a.shape[:-2], KT, P, a.shape[-1])
        return np.moveaxis(a, -2, 0)

    def halves(a):
        a = a.reshape(*a.shape[:-2], 2, FH, a.shape[-1])
        return np.moveaxis(a, -2, 0)

    ker = g["L0_xattn_ssm_kernel"]
    lag = np.arange(C)[None, :] - np.arange(P)[:, None]
    padded = np.concatenate([np.zeros((NH, P), ker.dtype), ker], 1)
    a = {
        "x": g["x"],
        "ctx_t": g["ctx_2048"].transpose(2, 0, 1).reshape(KT, P, NB, P).transpose(1, 0, 2, 3),
        "toep": padded[:, lag + P].transpose(1, 0, 2),
        "d_skip": np.broadcast_to(g["L0_xattn_D"], (P, NH)),
        "gate0": rows_first(g["L0_ffn_gate_w"].T),
        "w1_0": rows_first(g["L0_ffn_w1"].transpose(0, 2, 1)),
        "w2_0": halves(g["L0_ffn_w2"].transpose(0, 2, 1)),
        "decay": g["L1_xattn_time_decay"].reshape(KT, P).T,
        "first": g["L1_xattn_time_first"].reshape(KT, P).T,
        "norm_w": np.broadcast_to(g["L1_ffn_w_norm"], (P, C)),
        "gate1": rows_first(np.concatenate([g["L1_ffn_w_router"], g["L1_ffn_w_shared_gate"]], 1)),
        "w1_1": rows_first(np.concatenate([g["L1_ffn_w_gate"], g["L1_ffn_w_up"]], 2)),
        "w2_1": halves(g["L1_ffn_w_down"]),
    }
    s0 = g["L0_ffn_shared_w1"].T.reshape(C, 2, SU0, F).transpose(2, 0, 1, 3).reshape(SU0, C, 2 * F)
    s1 = np.stack([g["L1_ffn_sw_gate"].reshape(C, SU1, F), g["L1_ffn_sw_up"].reshape(C, SU1, F)], 2)
    a["sw1_0"] = rows_first(s0)
    a["sw2_0"] = halves(g["L0_ffn_shared_w2"].T.reshape(SU0, F, C))
    a["sw1_1"] = rows_first(s1.transpose(1, 0, 2, 3).reshape(SU1, C, 2 * F))
    a["sw2_1"] = halves(g["L1_ffn_sw_down"].reshape(SU1, F, C))

    nc = bacc.Bacc("TRN2", target_bir_lowering=False, num_devices=1)
    arrays, args = {}, []
    for name in _ORDER:
        v = np.ascontiguousarray(a[name])
        arrays[f"in_{name}"] = v
        args.append(nc.dram_tensor(f"in_{name}", v.shape, mybir.dt.from_np(v.dtype), kind="ExternalInput").ap())
    out = nc.dram_tensor("out_x", (NB, P, C), F32, kind="ExternalOutput").ap()
    build(nc, *args, out)
    r = run_bass_kernel_spmd(nc, [arrays], core_ids=[0])
    return r.results[0]["out_x"]
```

```python
from contextlib import ExitStack

import concourse.bass as bass
from concourse import mybir

F32 = mybir.dt.float32
I32 = mybir.dt.int32
ALU = mybir.AluOpType
ACT = mybir.ActivationFunctionType
AX = mybir.AxisListType

P = 128
NB = 8
C = 256
KT = C // P
NH = 16
HD = 8
F = 176
FH = F // 2
E0, K0, SU0 = 16, 6, 2
E1, K1, SU1 = 32, 4, 4
NT0 = 64
NT1 = E1
NTOK = NB * P
T1 = P + 1
LOW = -1e38
UNUSED = 8192.0
GR = 8
RING = 4


class Steps:

    def __init__(self, sem):
        self.sem, self.n = sem, 0

    def done(self, instruction):
        instruction.then_inc(self.sem, 1)
        self.n += 1
        return self.n


class Layer:

    def __init__(self, number, experts, choices, slices, tiles):
        self.number, self.experts, self.choices, self.slices, self.tiles = number, experts, choices, slices, tiles


def build(nc, x, ctx_t, toep, d_skip, gate0, w1_0, w2_0, sw1_0, sw2_0, decay, first, norm_w,
          gate1, w1_1, w2_1, sw1_1, sw2_1, out):
    stack = ExitStack()
    with stack:
        def sem(name):
            return stack.enter_context(nc.semaphore(name))

        def sb(name, shape, dt=F32):
            return stack.enter_context(nc.sbuf_tensor(name, shape, dt))

        X = sb("X", [P, NB, C])
        CT = sb("CT", [P, KT, NB, P])
        XN = sb("XN", [P, NB, C])
        XNT = sb("XNT", [P, KT, NB, P])
        W1 = sb("W1", [P, E0, KT, 2 * F])
        W2 = sb("W2", [FH, E0, 2, C])
        SW1 = sb("SW1", [P, SU0 + SU1, KT, 2 * F])
        SW2 = sb("SW2", [FH, SU0 + SU1, 2, C])
        GATE0 = sb("GATE0", [P, KT, E0])
        GATE1 = sb("GATE1", [P, KT, E1 + 1])
        NORM_W = sb("NORM_W", [P, C])
        IDENT = sb("IDENT", [P, P])
        UPPER = sb("UPPER", [P, P])
        ONES = sb("ONES", [P, P])
        IOTA = sb("IOTA", [P, P])
        VAL = sb("VAL", [P, K0, NB])
        IOTA_I = sb("IOTA_I", [P, P], I32)
        VAL_I = sb("VAL_I", [P, K0, NB], I32)
        LIM = sb("LIM", [P, NB])
        RES = sb("RES", [P, NB * E1])
        RES1 = sb("RES1", [P, NB * E1])
        RES8 = sb("RES8", [P, E1 * NB])
        DEC = sb("DEC", [P, KT])
        FIRST = sb("FIRST", [P, KT])
        STAT = sb("STAT", [P, NB, 6])
        MV = sb("MV", [P, NB, 2])
        STD = sb("STD", [P, NB])
        RSTD = sb("RSTD", [P, NB])
        PS = stack.enter_context(nc.psum_tensor("PS", [P, 8, 512], F32))

        xn_dram = [nc.dram_tensor(f"xn_rows{i}", [NTOK, C], F32, kind="Internal").ap() for i in range(2)]
        y_dram = [nc.dram_tensor(f"y_rows{i}", [k * NTOK, C], F32, kind="Internal").ap()
                  for i, k in enumerate((K0, K1))]

        loaded_x = sem("loaded_x")
        loaded_ctx = sem("loaded_ctx")
        loaded_toep = sem("loaded_toep")
        loaded_small = sem("loaded_small")
        loaded_w0 = sem("loaded_w0")
        loaded_shared = sem("loaded_shared")
        consts_ready = sem("consts_ready")
        vec = Steps(sem("vector_step"))
        pool = Steps(sem("gpsimd_step"))

        def v_link(instruction):
            nc.vector.wait_ge(vec.sem, vec.done(instruction))

        def v_do(instruction):
            vec.done(instruction)

        def v_sync():
            nc.vector.wait_ge(vec.sem, vec.n)

        def p_link(instruction):
            nc.gpsimd.wait_ge(pool.sem, pool.done(instruction))

        def normalize(dve, eps, standard_ready, variance_ready, number, src, dst):
            for i in range(NB):
                v_do(nc.vector.bn_stats(STAT[:, i, :], src[:, i, :]))
            v_sync()
            for i in range(NB):
                v_do(nc.vector.bn_aggr(MV[:, i, :], STAT[:, i, :]))
            v_sync()
            v_link(nc.vector.tensor_scalar(STD[:, :], MV[:, :, 1], eps, None, ALU.add))
            nc.vector.engine_nop().then_inc(variance_ready, 1)
            dve.wait_ge(standard_ready, number)
            v_link(nc.vector.reciprocal(RSTD[:, :], STD[:, :]))
            for i in range(NB):
                v_do(nc.vector.tensor_scalar(dst[:, i, :], src[:, i, :], MV[:, i, 0:1], RSTD[:, i:i + 1],
                                             ALU.subtract, ALU.mult))
            v_sync()

        def to_features(pe, done):
            for n in range(4):
                for j in range(4):
                    k, b = n // 2, 4 * (n % 2) + j
                    last = nc.tensor.transpose(PS[:, 4 + n, j * P:(j + 1) * P],
                                               XN[:, b, k * P:(k + 1) * P], IDENT[:, :])
                last.then_inc(done, 1)

        def features_out(act, done, copied, dst):
            for n in range(4):
                act.wait_ge(done, n + 1)
                k, b = n // 2, 4 * (n % 2)
                nc.scalar.activation(dst[:, k, b:b + 4, :], PS[:, 4 + n, :].rearrange("p (b t) -> p b t", b=4),
                                     ACT.Copy).then_inc(copied, 1)

        def to_tokens(pe, src, ready, done):
            for n in range(4):
                for j in range(4):
                    b, k = 2 * n + j // 2, j % 2
                    last = nc.tensor.transpose(PS[:, 4 + n, j * P:(j + 1) * P], src[:, k, b, :], IDENT[:, :])
                last.then_inc(done, 1)

        def add_tokens(dve, done):
            for n in range(4):
                dve.wait_ge(done, n + 1)
                v_do(nc.vector.tensor_tensor(X[:, 2 * n:2 * n + 2, :],
                                             PS[:, 4 + n, :].rearrange("p (b c) -> p b c", b=2),
                                             X[:, 2 * n:2 * n + 2, :], ALU.add))
            v_sync()

        a_std = sem("a_std"); a_var = sem("a_var"); a_xn = sem("a_xn"); a_tp = sem("a_tp")
        a_qt = sem("a_qt"); a_toep = sem("a_toep"); a_kv = sem("a_kv"); a_conv = sem("a_conv")
        a_prod = sem("a_prod"); a_out = sem("a_out"); a_back = sem("a_back"); a_dec = sem("a_dec")
        KVR = 3
        with ExitStack() as sa:
            TOEP = sa.enter_context(nc.sbuf_tensor("TOEP", [P, NH, C], F32))
            DSK = sa.enter_context(nc.sbuf_tensor("DSK", [P, NH], F32))
            KV = sa.enter_context(nc.sbuf_tensor("KV", [P, KVR, KT * NB, HD, HD], F32))
            Z = sa.enter_context(nc.sbuf_tensor("Z", [P, 2, NB, HD, HD], F32))
            OT = sa.enter_context(nc.sbuf_tensor("OT", [P, KT, NB, P], F32))
            TD = sa.enter_context(nc.sbuf_tensor("TD", [P, KT], F32))
            block = sa.enter_context(nc.Block())

            @block.sync
            def _(sp):
                sp.dma_start(X[:, :, :], x.rearrange("b p c -> p b c")).then_inc(loaded_x, 16)
                sp.dma_start(CT[:, :, :, :], ctx_t).then_inc(loaded_ctx, 16)
                sp.dma_start(TOEP[:, :, :], toep).then_inc(loaded_toep, 16)
                sp.wait_ge(loaded_toep, 16)
                for q in range(4):
                    sp.dma_start(SW1[:, 0:SU0, :, :] if q == 0 else W1[:, 4 * q:4 * q + 4, :, :],
                                 sw1_0 if q == 0 else w1_0[:, 4 * q:4 * q + 4, :, :]
                                 ).then_inc(loaded_shared if q == 0 else loaded_w0, 16)
                sp.dma_start(W1[:, 0:4, :, :], w1_0[:, 0:4, :, :]).then_inc(loaded_w0, 16)
                sp.dma_start(SW2[:, 0:SU0, :, :], sw2_0).then_inc(loaded_shared, 16)
                sp.dma_start(W2[:, :, :, :], w2_0).then_inc(loaded_w0, 16)
                sp.dma_start(SW1[:, SU0:, :, :], sw1_1).then_inc(loaded_shared, 16)
                sp.dma_start(SW2[:, SU0:, :, :], sw2_1).then_inc(loaded_shared, 16)

            @block.gpsimd
            def _(gp):
                p_link(nc.gpsimd.memset(IDENT[:, :], 0.0))
                p_link(nc.gpsimd.affine_select(out=IDENT[:, :], in_=IDENT[:, :], compare_op=ALU.not_equal, fill=1.0,
                                               base=0, pattern=[[-1, P]], channel_multiplier=1))
                nc.gpsimd.memset(ONES[:, :], 1.0).then_inc(consts_ready, 1)
                gp.wait_ge(loaded_ctx, 16)
                for h in range(NH):
                    if h >= KVR:
                        gp.wait_ge(a_conv, 2 * (h - KVR + 1))
                    c = CT[:, :, :, h * HD:(h + 1) * HD].rearrange("p k b i -> p (k b) i")
                    nc.gpsimd.tensor_tensor(
                        KV[:, h % KVR, :, :, :],
                        c.rearrange("p n (i o) -> p n i o", o=1).broadcast_to([P, KT * NB, HD, HD]),
                        c.rearrange("p n (o i) -> p n o i", o=1).broadcast_to([P, KT * NB, HD, HD]),
                        ALU.mult).then_inc(a_kv, 1)
                p_link(nc.gpsimd.memset(UPPER[:, :], 1.0))
                p_link(nc.gpsimd.affine_select(out=UPPER[:, :], in_=UPPER[:, :], compare_op=ALU.is_ge, fill=0.0,
                                               base=-1, pattern=[[1, P]], channel_multiplier=-1))
                p_link(nc.gpsimd.iota(IOTA_I[:, :], [[1, P]], base=0, channel_multiplier=0))
                p_link(nc.gpsimd.iota(VAL_I[:, :, :], [[NTOK, K0], [P, NB]], base=1, channel_multiplier=1))
                p_link(nc.gpsimd.tensor_copy(IOTA[:, :], IOTA_I[:, :]))
                p_link(nc.gpsimd.tensor_copy(VAL[:, :, :], VAL_I[:, :, :]))
                p_link(nc.gpsimd.tensor_scalar(LIM[:, :], IOTA[:, 0:NB], float(P), None, ALU.mult))
                for r, n in ((RES, E0), (RES1, E1), (RES8, NB)):
                    p_link(nc.gpsimd.memset(r[:, :], 1.0))
                    p_link(nc.gpsimd.memset(r[:, :].rearrange("p (g n) -> p g n", n=n)[:, :, 0:1], 0.0))

            @block.scalar
            def _(act):
                for dst, src in ((DSK[:, :], d_skip), (GATE0[:, :, :], gate0), (GATE1[:, :, :], gate1),
                                 (NORM_W[:, :], norm_w), (TD[:, :], decay), (FIRST[:, :], first)):
                    act.dma_start(dst, src).then_inc(loaded_small, 16)
                act.wait_ge(a_var, 1)
                nc.scalar.activation(STD[:, :], STD[:, :], ACT.Sqrt).then_inc(a_std, 1)
                features_out(act, a_tp, a_qt, XNT)
                act.wait_ge(loaded_small, 96)
                nc.scalar.activation(DEC[:, :], TD[:, :], ACT.Exp).then_inc(a_dec, 1)
                act.wait_ge(a_dec, 1)
                nc.scalar.mul(DEC[:, :], DEC[:, :], -1.0).then_inc(a_dec, 1)

            @block.vector
            def _(dve):
                dve.wait_ge(loaded_x, 16)
                normalize(dve, 1e-5, a_std, a_var, 1, X, XN)
                nc.vector.engine_nop().then_inc(a_xn, 1)
                dve.wait_ge(loaded_toep, 16)
                dve.wait_ge(loaded_small, 96)
                dve.wait_ge(consts_ready, 1)
                for h in range(NH):
                    nc.vector.scalar_tensor_tensor(TOEP[:, h, 0:P], IDENT[:, :], DSK[:, h:h + 1], TOEP[:, h, 0:P],
                                                   ALU.mult, ALU.add).then_inc(a_toep, 1)
                for n in range(2 * NH):
                    h, lt = n // 2, n % 2
                    dve.wait_ge(a_conv, n + 1)
                    dve.wait_ge(a_qt, 2 * lt + 2)
                    if n >= 2:
                        dve.wait_ge(a_out, n - 1)
                    y = PS[:, n % 4, :].rearrange("p (b i j) -> p b j i", b=NB, i=HD)
                    q = XNT[:, lt, :, h * HD:(h + 1) * HD].rearrange("p b (o i) -> p b o i", o=1)
                    nc.vector.tensor_tensor(Z[:, n % 2, :, :, :], y, q.broadcast_to([P, NB, HD, HD]),
                                            ALU.mult).then_inc(a_prod, 1)
                    dve.wait_ge(a_prod, n + 1)
                    nc.vector.tensor_reduce(OT[:, lt, :, h * HD:(h + 1) * HD], Z[:, n % 2, :, :, :], AX.X,
                                            ALU.add).then_inc(a_out, 1)
                add_tokens(dve, a_back)

            @block.tensor
            def _(pe):
                pe.wait_ge(consts_ready, 1)
                pe.wait_ge(a_xn, 1)
                to_features(pe, a_tp)
                for h in range(NH):
                    pe.wait_ge(a_kv, h + 1)
                    pe.wait_ge(a_toep, h + 1)
                    for lt in range(KT):
                        n = 2 * h + lt
                        if n >= 4:
                            pe.wait_ge(a_prod, n - 3)
                        kv = KV[:, h % KVR, :, :, :].rearrange("p (k b) i j -> p k (b i j)", k=KT)
                        if lt == 0:
                            last = nc.tensor.matmul(PS[:, n % 4, :], TOEP[:, h, 0:P], kv[:, 0, :], start=True, stop=True)
                        else:
                            nc.tensor.matmul(PS[:, n % 4, :], TOEP[:, h, P:C], kv[:, 0, :], start=True, stop=False)
                            last = nc.tensor.matmul(PS[:, n % 4, :], TOEP[:, h, 0:P], kv[:, 1, :],
                                                    start=False, stop=True)
                        last.then_inc(a_conv, 1)
                pe.wait_ge(a_out, 2 * NH)
                pe.wait_ge(a_qt, 4)
                to_tokens(pe, OT, None, a_back)

        def routed(lay):
            L, E, K, SU, NT = lay.number, lay.experts, lay.choices, lay.slices, lay.tiles
            S0 = 0 if L == 0 else SU0
            G = E + (1 if L else 0)
            s = lambda name: sem(f"r{L}_{name}")
            var, std, xn_ok, tp, xnt, xn_rows = s("var"), s("std"), s("xn"), s("tp"), s("xnt"), s("xn_rows")
            ms, msr, sig_ok = s("ms"), s("msr"), s("sig")
            logit, shifted, expd, sel_ok, counts, onehot, table, tables_ok = (
                s("logit"), s("shifted"), s("exp"), s("sel"), s("counts"), s("onehot"), s("table"), s("tables"))
            gathered = [s(f"gathered{i}") for i in range(GR)]
            scattered = [s(f"scattered{i}") for i in range(RING)]
            tx, xgt, gu, silu, up, hid, ta, at, dn, yout, so, so_used = (
                s("tx"), s("xgt"), s("gu"), s("silu"), s("up"), s("hid"), s("ta"), s("at"), s("dn"), s("yout"),
                s("so"), s("so_used"))
            hidx = s("hid_experts")
            YR = 4
            ygot = [s(f"ygot{i}") for i in range(YR)]
            v_summed, p_summed, stored = s("v_summed"), s("p_summed"), s("stored")
            NS = NB * SU
            N = NS + NT
            P_TILES = (1, 4, 6)

            with ExitStack() as sr:
                def rb(name, shape, dt=F32):
                    return sr.enter_context(nc.sbuf_tensor(f"{name}_{L}", shape, dt))
                SH = rb("SH", [P, NB, E]); EX = rb("EX", [P, NB, E]); PR = rb("PR", [P, NB, E])
                GT = rb("GT", [P, NB, E]); EQ = rb("EQ", [P, NB, E]); CE = rb("CE", [P, NB, E])
                SEL = rb("SEL", [P, NB, E]); RK = rb("RK", [P, NB, E]); TMP = rb("TMP", [P, 3, NB, E])
                TOT = rb("TOT", [P, E, NB]); INC = rb("INC", [P, E, NB]); CMP = rb("CMP", [P, E, NB])
                POS = rb("POS", [P, NB, E]); EID = rb("EID", [P, NB, E])
                M8 = rb("M8", [P, NB, 8]); MX = rb("MX", [P, NB]); NEED = rb("NEED", [P, NB])
                NTE = rb("NTE", [P, E]); ENDS = rb("ENDS", [P, E]); BASE = rb("BASE", [P, E])
                CK = rb("CK", [P, K, NB]); JK = rb("JK", [P, K, NB]); WK = rb("WK", [P, K, NB])
                GI = rb("GI", [P, K, NB], I32); CI = rb("CI", [P, K, NB], I32); JI = rb("JI", [P, K, NB], I32)
                OHA = rb("OHA", [P, 2, NB, P]); OHB = rb("OHB", [P, 2, NB, 2 * NT])
                ETC = rb("ETC", [1, NT, E]); ETF = rb("ETF", [1, NT]); ETI = rb("ETI", [1, NT], I32)
                DZ = rb("DZ", [P, NT]); DF = rb("DF", [P, NT]); DST = rb("DST", [P, NT], I32)
                SRC = rb("SRC", [P, NT], I32); WS = rb("WS", [P, NT])
                SIG = rb("SIG", [P, NB])
                XG = rb("XG", [P, GR, C]); XGT = rb("XGT", [P, 2, KT, P])
                SG = rb("SG", [P, 2, F]); UP = rb("UP", [P, 2, F]); HID = rb("HID", [P, 2, F])
                AT = rb("AT", [FH, 2, 2, P]); SO = rb("SO", [P, 2, C])
                Y = rb("Y", [P, RING, C])
                YL = W1[:, :, :, :].rearrange("p e k n -> p (e k n)")[:, 0:YR * K * C].rearrange(
                    "p (r k c) -> p r k c", r=YR, k=K)
                block = sr.enter_context(nc.Block())
                b_gu, b_tx, b_ta, b_dn = 0, 2, 4, 6
                lg = PS[:, 2, 0:NB * G].rearrange("p (i e) -> p i e", e=G)
                pw = PS[:, 3, 0:NB * E].rearrange("p (i e) -> p i e", e=E)
                tot = PS[:, 3, 256:256 + NB * E].rearrange("p (i e) -> p e i", e=E)
                tab = PS[:, 2, 0:2 * NT]

                def wait_hidden(eng, n):
                    if isinstance(n, int) and n < NS:
                        eng.wait_ge(hid, n + 1)
                    else:
                        eng.wait_ge(hidx, n - NS + 1)

                def per_tile(a, n=E):
                    return a[:, :].rearrange("p (i o) -> p i o", o=1).broadcast_to([P, NB, n])

                @block.sync
                def _(sp):
                    sp.wait_ge(xn_ok, 1)
                    sp.dma_start(xn_dram[L].rearrange("(i p) c -> p i c", p=P), XN[:, :, :]).then_inc(xn_rows, 16)
                    if L == 1:
                        lay.load_rest(sp, dn, NS)
                    for r in range(RING):
                        sp.wait_ge(scattered[r], 16 * (NT // RING))
                    yv = y_dram[L].rearrange("(k i p) c -> i p k c", k=K, p=P)
                    for i in range(NB):
                        if i >= YR:
                            last = i - YR
                            if last in P_TILES:
                                sp.wait_ge(p_summed, P_TILES.index(last) + 1)
                            else:
                                sp.wait_ge(v_summed, last + 1 - sum(t < last for t in P_TILES))
                        sp.dma_start(YL[:, i % YR, :, :], yv[i]).then_inc(ygot[i % YR], 16)
                    if L == 1:
                        for i in range(NB):
                            if i in P_TILES:
                                sp.wait_ge(p_summed, P_TILES.index(i) + 1)
                            else:
                                sp.wait_ge(v_summed, i + 1 - sum(t < i for t in P_TILES))
                            sp.dma_start(out[i], X[:, i, :]).then_inc(stored, 16)
                        sp.wait_ge(stored, 16 * NB)

                @block.gpsimd
                def _(gp):
                    def add_shared(i):
                        gp.wait_ge(so, i + 1)
                        nc.gpsimd.tensor_tensor(X[:, i, :], SO[:, i % 2, :], X[:, i, :],
                                                ALU.add).then_inc(so_used, 1)

                    for n in range(NS):
                        gp.wait_ge(up, n + 1)
                        if n >= 2:
                            gp.wait_ge(ta, n - 1)
                        nc.gpsimd.tensor_tensor(HID[:, n % 2, :], SG[:, n % 2, :], UP[:, n % 2, :],
                                                ALU.mult).then_inc(hid, 1)
                        if n >= 3 and (n - 2) % SU == 0:
                            add_shared((n - 2) // SU - 1)
                    gp.wait_ge(tables_ok, 1)
                    gp.wait_ge(xn_rows, 16)
                    if L == 1:
                        gp.wait_ge(lay.zero_rows, 16 * 8)

                    def gather(j):
                        if j >= GR:
                            gp.wait_ge(tx, j - GR + 1)
                        nc.gpsimd.indirect_dma_start(
                            XG[:, j % GR, :], None, xn_dram[L],
                            bass.IndirectOffsetOnAxis(ap=SRC[:, j:j + 1], axis=0)).then_inc(gathered[j % GR], 16)

                    def scatter(j):
                        gp.wait_ge(yout, j + 1)
                        nc.gpsimd.indirect_dma_start(
                            y_dram[L], bass.IndirectOffsetOnAxis(ap=DST[:, j:j + 1], axis=0),
                            Y[:, j % RING, :], None, bounds_check=K * NTOK - 1,
                            oob_is_err=False).then_inc(scattered[j % RING], 16)
                    for j in range(GR - 1):
                        gather(j)
                    for i in range((NS - 3) // SU, NB):
                        add_shared(i)
                    for j in range(NT):
                        if j + GR - 1 < NT:
                            gather(j + GR - 1)
                        scatter(j)
                    for i in P_TILES:
                        gp.wait_ge(ygot[i % YR], 16 * (i // YR + 1))
                        for k in range(1, K):
                            p_link(nc.gpsimd.tensor_tensor(YL[:, i % YR, 0, :], YL[:, i % YR, 0, :],
                                                           YL[:, i % YR, k, :], ALU.add))
                        nc.gpsimd.tensor_tensor(X[:, i, :], X[:, i, :], YL[:, i % YR, 0, :],
                                                ALU.add).then_inc(p_summed, 1)

                def shared_out(act, i):
                    act.wait_ge(dn, (i + 1) * SU)
                    if i >= 2:
                        act.wait_ge(so_used, i - 1)
                    if L == 1 and i == 0:
                        act.wait_ge(sig_ok, 1)
                    scale = SIG[:, i:i + 1] if L else 1.0
                    nc.scalar.activation(SO[:, i % 2, :], PS[:, b_dn + i % 2, 0:C], ACT.Copy,
                                         scale=scale).then_inc(so, 1)

                @block.scalar
                def _(act):
                    act.wait_ge(var, 1)
                    nc.scalar.activation(STD[:, :], STD[:, :], ACT.Sqrt).then_inc(std, 1)
                    if L == 1:
                        act.wait_ge(ms, 1)
                        nc.scalar.activation(STD[:, :], STD[:, :], ACT.Sqrt).then_inc(msr, 1)
                    features_out(act, tp, xnt, XNT)
                    act.wait_ge(shifted, 1)
                    nc.scalar.activation(EX[:, :, :], SH[:, :, :], ACT.Exp).then_inc(expd, 1)
                    if L == 1:
                        nc.scalar.activation(SIG[:, :], lg[:, :, E], ACT.Exp, scale=-1.0).then_inc(expd, 1)

                    def silu_step(n, s_):
                        act.wait_ge(gu, n + 1)
                        if not isinstance(n, int) or n >= 2:
                            wait_hidden(act, n - 2)
                        nc.scalar.activation(SG[:, s_, :], PS[:, b_gu + s_, 0:F], ACT.Silu).then_inc(silu, 1)

                    def hidden_out(n, s_):
                        act.wait_ge(ta, n + 1)
                        if not isinstance(n, int) or n >= 2:
                            act.wait_ge(dn, n - 1)
                        nc.scalar.activation(AT[:, s_, :, :],
                                             PS[0:FH, b_ta + s_, 0:2 * P].rearrange("p (k t) -> p k t", k=2),
                                             ACT.Copy).then_inc(at, 1)

                    for n in range(NS):
                        if n >= 3 and (n - 2) % SU == 0:
                            shared_out(act, (n - 2) // SU - 1)
                        if n >= 2:
                            hidden_out(n - 2, n % 2)
                        silu_step(n, n % 2)
                        nc.scalar.activation(UP[:, n % 2, :], PS[:, b_gu + n % 2, F:2 * F], ACT.Copy).then_inc(up, 1)
                    done = (NS - 3) // SU

                    def expert_step(j, n, s_, r, sent, first=False, last=False):
                        if r is not None:
                            act.wait_ge(dn, n - 2)
                            if sent is not None:
                                act.wait_ge(scattered[r], sent)
                            nc.scalar.activation(Y[:, r, :], PS[:, b_dn + (s_ + 1) % 2, 0:C], ACT.Copy,
                                                 scale=WS[:, bass.ds(j - 3, 1)]).then_inc(yout, 1)
                        hidden_out(n - 2, s_ % 2)
                        silu_step(n, s_ % 2)

                    for j in range(3):
                        if j == 0 and done < NB - 1:
                            shared_out(act, NB - 2)
                        hidden_out(NS + j - 2, j % 2)
                        if j == 0:
                            act.wait_ge(tables_ok, 1)
                        if j == 1:
                            shared_out(act, NB - 1)
                        silu_step(NS + j, j % 2)
                    for j in range(3, 8):
                        expert_step(j, NS + j, j, (j - 3) % RING, 16 * ((j - 3) // RING) or None)
                    if lay.looped:
                        with act.Fori(1, NT // 8) as q:
                            for t in range(8):
                                expert_step(8 * q + t, NS + 8 * q + t, t, (t - 3) % RING, 16 * (2 * q + (t - 3) // RING))
                    else:
                        for j in range(8, NT):
                            expert_step(j, NS + j, j, (j - 3) % RING, 16 * ((j - 3) // RING))
                    for j in range(NT, NT + 3):
                        act.wait_ge(dn, NS + j - 2)
                        act.wait_ge(scattered[(j - 3) % RING], 16 * ((j - 3) // RING))
                        nc.scalar.activation(Y[:, (j - 3) % RING, :], PS[:, b_dn + (j + 1) % 2, 0:C], ACT.Copy,
                                             scale=WS[:, j - 3:j - 2]).then_inc(yout, 1)
                        if j < NT + 2:
                            hidden_out(NS + j - 2, j % 2)

                @block.vector
                def _(dve):
                    normalize(dve, 1e-5, std, var, 1, X, XN)
                    if L == 1:
                        for i in range(NB):
                            v_do(nc.vector.bn_stats(STAT[:, i, :], XN[:, i, :]))
                        v_sync()
                        for i in range(NB):
                            v_do(nc.vector.bn_aggr(MV[:, i, :], STAT[:, i, :]))
                        v_sync()
                        v_link(nc.vector.tensor_tensor(MV[:, :, 0], MV[:, :, 0], MV[:, :, 0], ALU.mult))
                        v_link(nc.vector.scalar_tensor_tensor(STD[:, :], MV[:, :, 1], 1e-6, MV[:, :, 0],
                                                              ALU.add, ALU.add))
                        nc.vector.engine_nop().then_inc(ms, 1)
                        for i in range(NB):
                            v_do(nc.vector.tensor_tensor(X[:, i, :], X[:, i, :], XN[:, i, :], ALU.add))
                        dve.wait_ge(msr, 1)
                        v_link(nc.vector.reciprocal(RSTD[:, :], STD[:, :]))
                        for i in range(NB):
                            v_do(nc.vector.scalar_tensor_tensor(XN[:, i, :], XN[:, i, :], RSTD[:, i:i + 1],
                                                                NORM_W[:, :], ALU.mult, ALU.mult))
                        v_sync()
                    nc.vector.engine_nop().then_inc(xn_ok, 1)

                    dve.wait_ge(logit, 1)
                    v_link(nc.vector.tensor_reduce(MX[:, :], lg[:, :, 0:E], AX.X, ALU.max))
                    nc.vector.tensor_tensor(SH[:, :, :], lg[:, :, 0:E], per_tile(MX), ALU.subtract).then_inc(shifted, 1)
                    dve.wait_ge(expd, 1 + L)
                    v_link(nc.vector.tensor_reduce(MX[:, :], EX[:, :, :], AX.X, ALU.add))
                    v_link(nc.vector.reciprocal(MX[:, :], MX[:, :]))
                    v_do(nc.vector.tensor_tensor(PR[:, :, :], EX[:, :, :], per_tile(MX), ALU.mult))
                    if L == 1:
                        v_link(nc.vector.tensor_scalar(SIG[:, :], SIG[:, :], 1.0, None, ALU.add))
                        v_do(nc.vector.reciprocal(SIG[:, :], SIG[:, :]))
                    v_sync()
                    nc.vector.engine_nop().then_inc(sig_ok, 1)
                    for i in range(NB):
                        v_do(nc.vector.max(M8[:, i, :], PR[:, i, :]))
                    v_sync()
                    kth = M8[:, :, K - 1:K].broadcast_to([P, NB, E])
                    v_do(nc.vector.tensor_tensor(GT[:, :, :], PR[:, :, :], kth, ALU.is_gt))
                    v_do(nc.vector.tensor_tensor(EQ[:, :, :], PR[:, :, :], kth, ALU.is_equal))
                    v_sync()
                    flat = lambda a: a[:, :, :].rearrange("p a b -> p (a b)")
                    resets = (RES1 if L else RES)[:, 0:NB * E]
                    v_do(nc.vector.tensor_reduce(MX[:, :], GT[:, :, :], AX.X, ALU.add))
                    v_do(nc.vector.tensor_tensor_scan(flat(CE), resets, flat(EQ), 0.0, ALU.mult, ALU.add))
                    v_sync()
                    v_link(nc.vector.tensor_scalar(NEED[:, :], MX[:, :], -1.0, float(K), ALU.mult, ALU.add))
                    v_link(nc.vector.tensor_tensor(CE[:, :, :], CE[:, :, :], per_tile(NEED), ALU.is_le))
                    v_link(nc.vector.tensor_tensor(EQ[:, :, :], EQ[:, :, :], CE[:, :, :], ALU.mult))
                    v_link(nc.vector.tensor_tensor(SEL[:, :, :], GT[:, :, :], EQ[:, :, :], ALU.add))
                    nc.vector.engine_nop().then_inc(sel_ok, 1)
                    v_do(nc.vector.tensor_tensor_scan(flat(RK), resets, flat(SEL), 0.0, ALU.mult, ALU.add))
                    dve.wait_ge(counts, 1)
                    v_link(nc.vector.tensor_copy(TOT[:, :, :], tot))
                    v_link(nc.vector.tensor_tensor_scan(flat(INC), RES8[:, 0:NB * E], flat(TOT), 0.0,
                                                        ALU.mult, ALU.add))
                    if L == 0:
                        total = INC[:, :, NB - 1:NB].broadcast_to([P, E, NB])
                        lim = LIM[:, :].rearrange("p (o i) -> p o i", o=1).broadcast_to([P, E, NB])
                        v_link(nc.vector.tensor_tensor(CMP[:, :, :], total, lim, ALU.is_gt))
                        v_link(nc.vector.tensor_reduce(NTE[:, :], CMP[:, :, :], AX.X, ALU.add))
                        v_link(nc.vector.tensor_tensor_scan(ENDS[:, :], ONES[:, 0:E], NTE[:, :], 0.0,
                                                            ALU.mult, ALU.add))
                        v_do(nc.vector.tensor_tensor(BASE[:, :], ENDS[:, :], NTE[:, :], ALU.subtract))
                        v_link(nc.vector.tensor_tensor(
                            ETC[:, :, :], IOTA[0:1, 0:NT].rearrange("p (j o) -> p j o", o=1).broadcast_to([1, NT, E]),
                            ENDS[0:1, :].rearrange("p (o e) -> p o e", o=1).broadcast_to([1, NT, E]), ALU.is_ge))
                        v_link(nc.vector.tensor_reduce(ETF[:, :], ETC[:, :, :], AX.X, ALU.add))
                        v_link(nc.vector.tensor_scalar(ETF[:, :], ETF[:, :], float(E - 1), None, ALU.min))
                        v_do(nc.vector.tensor_copy(ETI[:, :], ETF[:, :]))
                        v_do(nc.vector.tensor_scalar(BASE[:, :], BASE[:, :], float(P), None, ALU.mult))
                    v_link(nc.vector.tensor_tensor(INC[:, :, :], INC[:, :, :], TOT[:, :, :], ALU.subtract))
                    v_link(nc.vector.tensor_tensor(POS[:, :, :], pw, INC[:, :, :].rearrange("p e i -> p i e"), ALU.add))
                    if L == 0:
                        base = BASE[:, :].rearrange("p (o e) -> p o e", o=1).broadcast_to([P, NB, E])
                        v_link(nc.vector.tensor_tensor(POS[:, :, :], POS[:, :, :], base, ALU.add))
                    else:
                        v_link(nc.vector.scalar_tensor_tensor(flat(SEL), flat(POS), float(P), flat(SEL),
                                                              ALU.is_lt, ALU.mult))
                        eid = IOTA[:, 1:E + 1].rearrange("p (o e) -> p o e", o=1).broadcast_to([P, NB, E])
                        v_do(nc.vector.tensor_tensor(EID[:, :, :], SEL[:, :, :], eid, ALU.mult))
                    v_do(nc.vector.scalar_tensor_tensor(flat(POS), flat(POS), 1.0, flat(SEL), ALU.add, ALU.mult))
                    v_do(nc.vector.tensor_tensor(PR[:, :, :], PR[:, :, :], SEL[:, :, :], ALU.mult))
                    v_sync()
                    picks = [(POS, CK), (PR, WK)] + ([(EID, JK)] if L else [])
                    for k in range(K):
                        for m, (src, dst) in enumerate(picks):
                            v_do(nc.vector.scalar_tensor_tensor(TMP[:, m, :, :].rearrange("p a b -> p (a b)"),
                                                                flat(RK), float(k + 1), flat(src),
                                                                ALU.is_equal, ALU.mult))
                        v_sync()
                        for m, (src, dst) in enumerate(picks):
                            v_do(nc.vector.tensor_reduce(dst[:, k, :], TMP[:, m, :, :], AX.X, ALU.add))
                        v_sync()
                    v_link(nc.vector.tensor_scalar(CK[:, :, :], CK[:, :, :], -1.0, None, ALU.add))
                    if L == 0:
                        v_link(nc.vector.tensor_copy(GI[:, :, :], CK[:, :, :]))
                        v_do(nc.vector.tensor_scalar(CI[:, :, :], GI[:, :, :], P - 1, None, ALU.bitwise_and))
                        v_do(nc.vector.tensor_scalar(JI[:, :, :], GI[:, :, :], 7, None, ALU.logical_shift_right))
                        v_sync()
                        v_do(nc.vector.tensor_copy(CK[:, :, :], CI[:, :, :]))
                        v_do(nc.vector.tensor_copy(JK[:, :, :], JI[:, :, :]))
                    else:
                        v_do(nc.vector.tensor_scalar(JK[:, :, :], JK[:, :, :], -1.0, None, ALU.add))
                    v_sync()
                    for k in range(K):
                        if k >= 2:
                            dve.wait_ge(table, k - 1)
                        for i in range(NB):
                            nc.vector.tensor_scalar(OHA[:, k % 2, i, :], IOTA[:, :], CK[:, k, i:i + 1], None,
                                                    ALU.is_equal)
                            nc.vector.tensor_scalar(OHB[:, k % 2, i, 0:NT], IOTA[:, 0:NT], JK[:, k, i:i + 1],
                                                    VAL[:, k, i:i + 1], ALU.is_equal, ALU.mult)
                            last = nc.vector.tensor_scalar(OHB[:, k % 2, i, NT:], IOTA[:, 0:NT], JK[:, k, i:i + 1],
                                                           WK[:, k, i:i + 1], ALU.is_equal, ALU.mult)
                        last.then_inc(onehot, 1)
                    dve.wait_ge(table, K)
                    v_do(nc.vector.tensor_copy(WS[:, :], tab[:, NT:]))
                    v_link(nc.vector.tensor_scalar(DZ[:, :], tab[:, 0:NT], 0.0, UNUSED, ALU.is_equal, ALU.mult))
                    v_link(nc.vector.scalar_tensor_tensor(DF[:, :], tab[:, 0:NT], -1.0, DZ[:, :], ALU.add, ALU.add))
                    v_link(nc.vector.tensor_copy(DST[:, :], DF[:, :]))
                    v_link(nc.vector.tensor_scalar(SRC[:, :], DST[:, :], NTOK - 1, None, ALU.bitwise_and))
                    nc.vector.engine_nop().then_inc(tables_ok, 1)

                    def rows_out(j, s_):
                        dve.wait_ge(tx, j + 1)
                        if not isinstance(j, int) or j >= 2:
                            dve.wait_ge(gu, NS + j - 1)
                        nc.vector.tensor_copy(XGT[:, s_, :, :],
                                              PS[:, b_tx + s_, 0:C].rearrange("p (k t) -> p k t", k=KT)).then_inc(xgt, 1)

                    def hidden(n, s_):
                        dve.wait_ge(silu, n + 1)
                        dve.wait_ge(ta, n - 1)
                        nc.vector.tensor_tensor(HID[:, s_, :], SG[:, s_, :], PS[:, b_gu + s_, F:2 * F],
                                                ALU.mult).then_inc(hidx, 1)

                    rows_out(0, 0)
                    for j in range(8):
                        rows_out(j + 1, (j + 1) % 2)
                        hidden(NS + j, j % 2)
                    if lay.looped:
                        with dve.Fori(1, NT // 8 - 1) as q:
                            for t in range(8):
                                rows_out(8 * q + t + 1, (t + 1) % 2)
                                hidden(NS + 8 * q + t, t % 2)
                    else:
                        for j in range(8, NT - 8):
                            rows_out(j + 1, (j + 1) % 2)
                            hidden(NS + j, j % 2)
                    for j in range(NT - 8, NT):
                        if j + 1 < NT:
                            rows_out(j + 1, (j + 1) % 2)
                        hidden(NS + j, j % 2)
                    for i in (t for t in range(NB) if t not in P_TILES):
                        r, half = i % YR, K // 2
                        dve.wait_ge(ygot[r], 16 * (i // YR + 1))
                        v_link(nc.vector.tensor_tensor(YL[:, r, 0:half, :], YL[:, r, 0:half, :],
                                                       YL[:, r, half:K, :], ALU.add))
                        v_do(nc.vector.tensor_tensor(YL[:, r, 0, :], YL[:, r, 0, :], YL[:, r, 1, :], ALU.add))
                        if half == 3:
                            v_do(nc.vector.tensor_tensor(X[:, i, :], X[:, i, :], YL[:, r, 2, :], ALU.add))
                        v_sync()
                        nc.vector.tensor_tensor(X[:, i, :], X[:, i, :], YL[:, r, 0, :], ALU.add).then_inc(v_summed, 1)

                @block.tensor
                def _(pe):
                    pe.wait_ge(xn_ok, 1)
                    to_features(pe, tp)
                    pe.wait_ge(xnt, 4)
                    gate = GATE1 if L else GATE0
                    for i in range(NB):
                        for k in range(KT):
                            last = nc.tensor.matmul(lg[:, i, :], XNT[:, k, i, :], gate[:, k, :],
                                                    start=(k == 0), stop=(k == KT - 1))
                    last.then_inc(logit, 1)
                    pe.wait_ge(loaded_shared, 64)

                    def queue_counts():
                        pe.wait_ge(sel_ok, 1)
                        flat = SEL[:, :, :].rearrange("p a b -> p (a b)")
                        nc.tensor.matmul(PS[:, 3, 0:NB * E], UPPER[:, :], flat, start=True, stop=True)
                        nc.tensor.matmul(PS[:, 3, 256:256 + NB * E], ONES[:, :], flat, start=True,
                                         stop=True).then_inc(counts, 1)

                    def tables(k):
                        pe.wait_ge(onehot, k + 1)
                        for i in range(NB):
                            last = nc.tensor.matmul(tab, OHA[:, k % 2, i, :], OHB[:, k % 2, i, :],
                                                    start=(k == 0 and i == 0), stop=(k == K - 1 and i == NB - 1))
                        last.then_inc(table, 1)

                    def rows_t(j, s_, r, cnt):
                        pe.wait_ge(gathered[r], cnt)
                        if not isinstance(j, int) or j >= 2:
                            pe.wait_ge(xgt, j - 1)
                        for k in range(KT):
                            last = nc.tensor.transpose(PS[:, b_tx + s_, k * P:(k + 1) * P],
                                                       XG[:, r, k * P:(k + 1) * P], IDENT[:, :])
                        last.then_inc(tx, 1)

                    def gate_up(n, s_, lhs, w):
                        if not isinstance(n, int) or n >= 2:
                            wait_hidden(pe, n - 2)
                        for k in range(KT):
                            last = nc.tensor.matmul(PS[:, b_gu + s_, 0:2 * F], lhs(k), w(k),
                                                    start=(k == 0), stop=(k == KT - 1))
                        last.then_inc(gu, 1)

                    def hidden_t(n, s_):
                        wait_hidden(pe, n)
                        if not isinstance(n, int) or n >= 2:
                            pe.wait_ge(at, n - 1)
                        for k in range(2):
                            last = nc.tensor.transpose(PS[0:FH, b_ta + s_, k * P:(k + 1) * P],
                                                       HID[:, s_, k * FH:(k + 1) * FH], IDENT[:, :])
                        last.then_inc(ta, 1)

                    def down(n, s_, bank, w, start=True, stop=True):
                        pe.wait_ge(at, n + 1)
                        for k in range(2):
                            last = nc.tensor.matmul(PS[:, bank, 0:C], AT[:, s_, k, :], w(k),
                                                    start=(start and k == 0), stop=(stop and k == 1))
                        last.then_inc(dn, 1)

                    def down_shared(n):
                        i, u = n // SU, n % SU
                        if u == 0 and i >= 2:
                            pe.wait_ge(so, i - 1)
                        down(n, n % 2, b_dn + i % 2, lambda k: SW2[:, S0 + u, k, :], u == 0, u == SU - 1)

                    def down_expert(j, n, s_, e):
                        if not isinstance(j, int) or j >= 2:
                            pe.wait_ge(yout, j - 1)
                        down(n, s_, b_dn + s_, lay.down_weights(pe, j, e))

                    for n in range(NS):
                        i, u = n // SU, n % SU
                        if n == lay.counts_at:
                            queue_counts()
                        if n in lay.tables_at:
                            tables(lay.tables_at.index(n))
                        if n >= 2:
                            hidden_t(n - 2, n % 2)
                        gate_up(n, n % 2, lambda k: XNT[:, k, i, :], lambda k: SW1[:, S0 + u, k, :])
                        if n >= 2:
                            down_shared(n - 2)
                    for k in range(len(lay.tables_at), K):
                        tables(k)
                    pe.wait_ge(tables_ok, 1)
                    lay.wait_weights(pe)

                    def expert_unit(j, n, t, e, before, cnt, more=True):
                        if more:
                            rows_t(j + 1, (t + 1) % 2, (t + 1) % GR, cnt)
                        hidden_t(n - 2, t % 2)
                        pe.wait_ge(xgt, j + 1)
                        gate_up(n, t % 2, lambda k: XGT[:, t % 2, k, :], lay.up_weights(pe, j, e))
                        down_expert(j - 2, n - 2, t % 2, before)

                    rows_t(0, 0, 0, 16)
                    expert = lambda j: lay.expert_of(pe, ETI, j)
                    for j in range(8):
                        e = expert(j)
                        if j < 2:
                            rows_t(j + 1, (j + 1) % 2, j + 1, 16)
                            hidden_t(NS + j - 2, j % 2)
                            pe.wait_ge(xgt, j + 1)
                            gate_up(NS + j, j % 2, lambda k: XGT[:, j % 2, k, :], lay.up_weights(pe, j, e))
                            down_shared(NS + j - 2)
                            if j == 1:
                                pe.wait_ge(so, NB)
                        else:
                            expert_unit(j, NS + j, j, e, expert(j - 2), 16 * ((j + 1) // GR + 1))
                    if lay.looped:
                        with pe.Fori(1, NT // 8 - 1) as q:
                            for t in range(8):
                                j = 8 * q + t
                                expert_unit(j, NS + 8 * q + t, t, expert(j), expert(8 * q + t - 2),
                                            16 * (q + (t + 1) // GR + 1))
                    else:
                        for j in range(8, NT - 8):
                            expert_unit(j, NS + j, j, expert(j), expert(j - 2), 16 * ((j + 1) // GR + 1))
                    for j in range(NT - 8, NT):
                        expert_unit(j, NS + j, j, expert(j), expert(j - 2), 16 * ((j + 1) // GR + 1), j + 1 < NT)
                    for j in range(NT, NT + 2):
                        hidden_t(NS + j - 2, j % 2)
                        down_expert(j - 2, NS + j - 2, j % 2, expert(j - 2))

        lay0 = Layer(number=0, experts=E0, choices=K0, slices=SU0, tiles=NT0)
        lay0.looped = True
        lay0.wait_weights = lambda pe: pe.wait_ge(loaded_w0, 80)
        lay0.counts_at, lay0.tables_at = 3, (11, 13, 15)

        def expert_of(pe, eti, j):
            return pe.value_load(eti[0:1, bass.ds(j, 1)], min_val=0, max_val=E0 - 1)
        lay0.expert_of = expert_of
        lay0.up_weights = lambda pe, j, e: lambda k: W1[:, bass.ds(e, 1), k, :].rearrange("p o n -> p (o n)")
        lay0.down_weights = lambda pe, j, e: lambda k: W2[:, bass.ds(e, 1), k, :].rearrange("p o n -> p (o n)")
        routed(lay0)

        ring_w1 = [sem(f"ring_up{i}") for i in range(4)]
        ring_w2 = [sem(f"ring_down{i}") for i in range(4)]
        zero_rows = sem("zero_rows")
        c_std = sem("c_std"); c_var = sem("c_var"); c_xn = sem("c_xn"); c_tp = sem("c_tp"); c_kt = sem("c_kt")
        c_pad = sem("c_pad"); c_diff = sem("c_diff"); c_exp = sem("c_exp"); c_y = sem("c_y"); c_back = sem("c_back")
        c_zero = sem("c_zero")
        with ExitStack() as sc:
            def cb(name):
                return sc.enter_context(nc.sbuf_tensor(name, [P, KT, NB, T1], F32))
            KX = cb("KX"); WF = cb("WF"); PP = cb("PP"); E1B = cb("E1B"); E2B = cb("E2B"); KB = cb("KB")
            AA = sc.enter_context(nc.sbuf_tensor("AA", [P, NB, T1], F32))
            BB = sc.enter_context(nc.sbuf_tensor("BB", [P, NB, T1], F32))
            D3 = XNT
            D4 = XN[:, :, :].rearrange("p b c -> p (b c)").rearrange("p (k b t) -> p k b t", k=KT, b=NB)
            ZR = sc.enter_context(nc.sbuf_tensor("ZR", [P, 1024], F32))
            block = sc.enter_context(nc.Block())

            @block.sync
            def _(sp):
                sp.wait_ge(c_zero, 1)
                z = y_dram[1].rearrange("(g p r) c -> g p (r c)", p=P, r=4)
                for g in range(8):
                    sp.dma_start(z[g], ZR[:, :]).then_inc(zero_rows, 16)
                for q in range(4):
                    sp.dma_start(W1[:, 4 * q:4 * q + 4, :, :], w1_1[:, 4 * q:4 * q + 4, :, :]).then_inc(ring_w1[q], 16)
                    sp.dma_start(W2[:, 4 * q:4 * q + 4, :, :], w2_1[:, 4 * q:4 * q + 4, :, :]).then_inc(ring_w2[q], 16)

            @block.gpsimd
            def _(gp):
                nc.gpsimd.memset(ZR[:, :], 0.0).then_inc(c_zero, 1)
                p_link(nc.gpsimd.memset(WF[:, :, :, :], 0.0))
                for k in range(KT):
                    p_link(nc.gpsimd.tensor_scalar(WF[:, k, :, :], WF[:, k, :, :], DEC[:, k:k + 1], None, ALU.add))
                p_link(nc.gpsimd.memset(WF[:, :, :, 0:1], LOW))
                nc.gpsimd.memset(KX[:, :, :, 0:1], LOW)
                for a in (E1B, E2B, KB):
                    last = nc.gpsimd.memset(a[:, :, :, 0:1], 0.0)
                last.then_inc(c_pad, 1)

            @block.scalar
            def _(act):
                act.wait_ge(c_var, 1)
                nc.scalar.activation(STD[:, :], STD[:, :], ACT.Sqrt).then_inc(c_std, 1)
                features_out(act, c_tp, c_kt, KX[:, :, :, 1:T1])
                for k in range(KT):
                    act.wait_ge(c_diff, 4 * k + 1)
                    nc.scalar.activation(E1B[:, k, :, 1:T1], E1B[:, k, :, 1:T1], ACT.Exp,
                                         bias=DEC[:, k:k + 1]).then_inc(c_exp, 1)
                    act.wait_ge(c_diff, 4 * k + 2)
                    nc.scalar.activation(E2B[:, k, :, 1:T1], E2B[:, k, :, 1:T1], ACT.Exp).then_inc(c_exp, 1)
                    act.wait_ge(c_diff, 4 * k + 3)
                    nc.scalar.activation(D3[:, k, :, :], D3[:, k, :, :], ACT.Exp).then_inc(c_exp, 1)
                    act.wait_ge(c_diff, 4 * k + 4)
                    nc.scalar.activation(D4[:, k, :, :], D4[:, k, :, :], ACT.Exp, scale=-1.0).then_inc(c_exp, 1)

            @block.vector
            def _(dve):
                normalize(dve, 1e-5, c_std, c_var, 1, X, XN)
                nc.vector.engine_nop().then_inc(c_xn, 1)
                dve.wait_ge(c_pad, 1)
                dve.wait_ge(c_kt, 4)
                two = lambda a, k: a[:, k, :, :].rearrange("p b t -> p (b t)")
                for k in range(KT):
                    v_link(nc.vector.tensor_tensor_scan(two(PP, k), two(WF, k), two(KX, k), 0.0, ALU.add, ALU.max))
                    prev, cur = PP[:, k, :, 0:P], PP[:, k, :, 1:T1]
                    kx = KX[:, k, :, 1:T1]
                    nc.vector.tensor_tensor(E1B[:, k, :, 1:T1], prev, cur, ALU.subtract).then_inc(c_diff, 1)
                    nc.vector.tensor_tensor(E2B[:, k, :, 1:T1], kx, cur, ALU.subtract).then_inc(c_diff, 1)
                    v_link(nc.vector.scalar_tensor_tensor(D4[:, k, :, :], prev, FIRST[:, k:k + 1], kx,
                                                          ALU.subtract, ALU.subtract))
                    v_link(nc.vector.tensor_scalar(D3[:, k, :, :], D4[:, k, :, :], 0.0, None, ALU.min))
                    nc.vector.engine_nop().then_inc(c_diff, 1)
                    v_link(nc.vector.tensor_scalar(D4[:, k, :, :], D4[:, k, :, :], 0.0, None, ALU.max))
                    nc.vector.engine_nop().then_inc(c_diff, 1)
                for k in range(KT):
                    v = CT[:, k, :, :]
                    dve.wait_ge(c_exp, 4 * k + 2)
                    v_link(nc.vector.tensor_tensor(KB[:, k, :, 1:T1], E2B[:, k, :, 1:T1], v, ALU.mult))
                    v_link(nc.vector.tensor_tensor_scan(AA[:, :, :].rearrange("p b t -> p (b t)"), two(E1B, k), two(KB, k), 0.0, ALU.mult, ALU.add))
                    v_link(nc.vector.tensor_tensor_scan(BB[:, :, :].rearrange("p b t -> p (b t)"), two(E1B, k), two(E2B, k), 0.0, ALU.mult, ALU.add))
                    dve.wait_ge(c_exp, 4 * k + 4)
                    aap, bbp = AA[:, :, 0:P], BB[:, :, 0:P]
                    num, den = KB[:, k, :, 0:P], E2B[:, k, :, 0:P]
                    v_link(nc.vector.tensor_tensor(num, D3[:, k, :, :], aap, ALU.mult))
                    v_link(nc.vector.tensor_tensor(den, D3[:, k, :, :], bbp, ALU.mult))
                    v_link(nc.vector.tensor_tensor(den, den, D4[:, k, :, :], ALU.add))
                    v_link(nc.vector.tensor_tensor(D4[:, k, :, :], D4[:, k, :, :], v, ALU.mult))
                    v_link(nc.vector.tensor_tensor(num, num, D4[:, k, :, :], ALU.add))
                    v_link(nc.vector.reciprocal(den, den))
                    v_link(nc.vector.tensor_tensor(D3[:, k, :, :], num, den, ALU.mult))
                nc.vector.engine_nop().then_inc(c_y, 1)
                add_tokens(dve, c_back)

            @block.tensor
            def _(pe):
                pe.wait_ge(c_xn, 1)
                to_features(pe, c_tp)
                pe.wait_ge(c_kt, 4)
                pe.wait_ge(c_y, 1)
                to_tokens(pe, D3, None, c_back)

        lay1 = Layer(number=1, experts=E1, choices=K1, slices=SU1, tiles=NT1)
        lay1.zero_rows = zero_rows
        lay1.looped = False
        lay1.wait_weights = lambda pe: None
        lay1.counts_at, lay1.tables_at = 4, (18, 21, 24, 27)
        lay1.expert_of = lambda pe, eti, j: None

        def load_rest(sp, dn, ns):
            for q in range(4, 8):
                sp.wait_ge(dn, ns + 4 * (q - 3))
                s4 = 4 * (q - 4)
                sp.dma_start(W1[:, s4:s4 + 4, :, :], w1_1[:, 4 * q:4 * q + 4, :, :]).then_inc(ring_w1[q - 4], 16)
                sp.dma_start(W2[:, s4:s4 + 4, :, :], w2_1[:, 4 * q:4 * q + 4, :, :]).then_inc(ring_w2[q - 4], 16)
        lay1.load_rest = load_rest

        def up1(pe, j, e):
            q = j // 4
            pe.wait_ge(ring_w1[q % 4], 16 * (q // 4 + 1))
            return lambda k: W1[:, j % 16, k, :]

        def down1(pe, j, e):
            q = j // 4
            pe.wait_ge(ring_w2[q % 4], 16 * (q // 4 + 1))
            return lambda k: W2[:, j % 16, k, :]
        lay1.up_weights, lay1.down_weights = up1, down1
        routed(lay1)


_ORDER = ["x", "ctx_t", "toep", "d_skip", "gate0", "w1_0", "w2_0", "sw1_0", "sw2_0", "decay", "first",
          "norm_w", "gate1", "w1_1", "w2_1", "sw1_1", "sw2_1"]


def kernel(**inputs):
    import numpy as np
    import concourse.bacc as bacc
    from concourse.bass_utils import run_bass_kernel_spmd

    g = {k: np.asarray(v) for k, v in inputs.items()}

    def rows_first(a):
        a = a.reshape(*a.shape[:-2], KT, P, a.shape[-1])
        return np.moveaxis(a, -2, 0)

    def halves(a):
        a = a.reshape(*a.shape[:-2], 2, FH, a.shape[-1])
        return np.moveaxis(a, -2, 0)

    ker = g["L0_xattn_ssm_kernel"]
    lag = np.arange(C)[None, :] - np.arange(P)[:, None]
    padded = np.concatenate([np.zeros((NH, P), ker.dtype), ker], 1)
    a = {
        "x": g["x"],
        "ctx_t": g["ctx_2048"].transpose(2, 0, 1).reshape(KT, P, NB, P).transpose(1, 0, 2, 3),
        "toep": padded[:, lag + P].transpose(1, 0, 2),
        "d_skip": np.broadcast_to(g["L0_xattn_D"], (P, NH)),
        "gate0": rows_first(g["L0_ffn_gate_w"].T),
        "w1_0": rows_first(g["L0_ffn_w1"].transpose(0, 2, 1)),
        "w2_0": halves(g["L0_ffn_w2"].transpose(0, 2, 1)),
        "decay": g["L1_xattn_time_decay"].reshape(KT, P).T,
        "first": g["L1_xattn_time_first"].reshape(KT, P).T,
        "norm_w": np.broadcast_to(g["L1_ffn_w_norm"], (P, C)),
        "gate1": rows_first(np.concatenate([g["L1_ffn_w_router"], g["L1_ffn_w_shared_gate"]], 1)),
        "w1_1": rows_first(np.concatenate([g["L1_ffn_w_gate"], g["L1_ffn_w_up"]], 2)),
        "w2_1": halves(g["L1_ffn_w_down"]),
    }
    s0 = g["L0_ffn_shared_w1"].T.reshape(C, 2, SU0, F).transpose(2, 0, 1, 3).reshape(SU0, C, 2 * F)
    s1 = np.stack([g["L1_ffn_sw_gate"].reshape(C, SU1, F), g["L1_ffn_sw_up"].reshape(C, SU1, F)], 2)
    a["sw1_0"] = rows_first(s0)
    a["sw2_0"] = halves(g["L0_ffn_shared_w2"].T.reshape(SU0, F, C))
    a["sw1_1"] = rows_first(s1.transpose(1, 0, 2, 3).reshape(SU1, C, 2 * F))
    a["sw2_1"] = halves(g["L1_ffn_sw_down"].reshape(SU1, F, C))

    nc = bacc.Bacc("TRN2", target_bir_lowering=False, num_devices=1)
    arrays, args = {}, []
    for name in _ORDER:
        v = np.ascontiguousarray(a[name])
        arrays[f"in_{name}"] = v
        args.append(nc.dram_tensor(f"in_{name}", v.shape, mybir.dt.from_np(v.dtype), kind="ExternalInput").ap())
    out = nc.dram_tensor("out_x", (NB, P, C), F32, kind="ExternalOutput").ap()
    build(nc, *args, out)
    r = run_bass_kernel_spmd(nc, [arrays], core_ids=[0])
    return r.results[0]["out_x"]
```

```python
from contextlib import ExitStack

import concourse.bass as bass
from concourse import mybir

F32 = mybir.dt.float32
F32R = mybir.dt.float32r
I32 = mybir.dt.int32
ALU = mybir.AluOpType
ACT = mybir.ActivationFunctionType
AX = mybir.AxisListType

P = 128
NB = 8
C = 256
KT = C // P
NH = 16
HD = 8
F = 176
FH = F // 2
E0, K0, SU0 = 16, 6, 2
E1, K1, SU1 = 32, 4, 4
NT0 = 63
NT1 = E1
NTOK = NB * P
T1 = P + 1
LOW = -1e38
UNUSED = 8192.0
GR = 8
RING = 4
WR = 4
WR2 = 8
WAHEAD = 2


class Steps:

    def __init__(self, sem):
        self.sem, self.n = sem, 0

    def done(self, instruction):
        instruction.then_inc(self.sem, 1)
        self.n += 1
        return self.n


class Layer:

    def __init__(self, number, experts, choices, slices, tiles):
        self.number, self.experts, self.choices, self.slices, self.tiles = number, experts, choices, slices, tiles


def build(nc, x, ctx_t, toep, d_skip, gate0, w1_0, w2_0, sw1_0, sw2_0, decay, first, norm_w,
          gate1, w1_1, w2_1, sw1_1, sw2_1, out):
    stack = ExitStack()
    with stack:
        def sem(name):
            return stack.enter_context(nc.semaphore(name))

        def sb(name, shape, dt=F32):
            return stack.enter_context(nc.sbuf_tensor(name, shape, dt))

        X = sb("X", [P, NB, C])
        CT = sb("CT", [P, KT, NB, P])
        XN = sb("XN", [P, NB, C])
        XNT = sb("XNT", [P, KT, NB, P])
        SW1_1 = sb("SW1_1", [P, SU1, KT, 2 * F])
        SW2_1 = sb("SW2_1", [FH, SU1, 2, C])
        GATE0 = sb("GATE0", [P, KT, E0])
        GATE1 = sb("GATE1", [P, KT, E1 + 1])
        NORM_W = sb("NORM_W", [P, C])
        IDENT = sb("IDENT", [P, P])
        UPPER = sb("UPPER", [P, P])
        ONES = sb("ONES", [P, P])
        IOTA = sb("IOTA", [P, P])
        VAL = sb("VAL", [P, K0, NB])
        IOTA1 = sb("IOTA1", [P, P])
        IOTA_I = sb("IOTA_I", [P, P], I32)
        VAL_I = sb("VAL_I", [P, K0, NB], I32)
        LIM = sb("LIM", [P, NB])
        RES = sb("RES", [P, NB * E1])
        RES1 = sb("RES1", [P, NB * E1])
        RES8 = sb("RES8", [P, E1 * NB])
        DEC = sb("DEC", [P, KT])
        FIRST = sb("FIRST", [P, KT])
        STAT = sb("STAT", [P, NB, 6])
        MV = sb("MV", [P, NB, 2])
        STD = sb("STD", [P, NB])
        RSTD = sb("RSTD", [P, NB])
        weights0 = ExitStack()

        def sb0(name, shape):
            return weights0.enter_context(nc.sbuf_tensor(name, shape, F32))
        W1_0 = sb0("W1_0", [P, E0, KT, 2 * F])
        W2_0 = sb0("W2_0", [FH, E0, 2, C])
        SW1_0 = sb0("SW1_0", [P, SU0, KT, 2 * F])
        SW2_0 = sb0("SW2_0", [FH, SU0, 2, C])
        PS = stack.enter_context(nc.psum_tensor("PS", [P, 8, 512], F32))

        xn_dram = [nc.dram_tensor(f"xn_rows{i}", [NTOK, C], F32, kind="Internal").ap() for i in range(2)]
        y_dram = [nc.dram_tensor(f"y_rows{i}", [k * NTOK, C], F32, kind="Internal").ap()
                  for i, k in enumerate((K0, K1))]

        loaded_x = sem("loaded_x")
        loaded_ctx = sem("loaded_ctx")
        loaded_toep = [sem(f"loaded_toep{g}") for g in range(2)]
        loaded_small = sem("loaded_small")
        loaded_w0 = sem("loaded_w0")
        loaded_shared = sem("loaded_shared")
        consts_ready = sem("consts_ready")
        vec = Steps(sem("vector_step"))
        pool = Steps(sem("gpsimd_step"))

        def v_link(instruction):
            nc.vector.wait_ge(vec.sem, vec.done(instruction))

        def v_do(instruction):
            vec.done(instruction)

        def v_sync():
            nc.vector.wait_ge(vec.sem, vec.n)

        def p_link(instruction):
            nc.gpsimd.wait_ge(pool.sem, pool.done(instruction))

        def tile_statistics(i):
            v_do(nc.vector.bn_stats(STAT[:, i, :], X[:, i, :]))

        def deviations(dve, eps, standard_ready, variance_ready):
            v_sync()
            for i in range(NB):
                v_do(nc.vector.bn_aggr(MV[:, i, :], STAT[:, i, :]))
            v_sync()
            v_link(nc.vector.tensor_scalar(STD[:, :], MV[:, :, 1], eps, None, ALU.add))
            nc.vector.engine_nop().then_inc(variance_ready, 1)
            dve.wait_ge(standard_ready, 1)
            v_link(nc.vector.reciprocal(RSTD[:, :], STD[:, :]))

        def normalize(dst, halves_ready):
            for i in range(NB):
                v_do(nc.vector.tensor_scalar(dst[:, i, :], X[:, i, :], MV[:, i, 0:1], RSTD[:, i:i + 1],
                                             ALU.subtract, ALU.mult))
                if i % 4 == 3:
                    v_sync()
                    nc.vector.engine_nop().then_inc(halves_ready, 1)

        def to_features(pe, halves_ready, done):
            for n in range(4):
                if n % 2 == 0:
                    pe.wait_ge(halves_ready, n // 2 + 1)
                for j in range(4):
                    k, b = n % 2, 4 * (n // 2) + j
                    last = nc.tensor.transpose(PS[:, 4 + n, j * P:(j + 1) * P],
                                               XN[:, b, k * P:(k + 1) * P], IDENT[:, :])
                last.then_inc(done, 1)

        def features_out(act, done, copied, dst, rounded=None):
            for n in range(4):
                act.wait_ge(done, n + 1)
                k, b = n % 2, 4 * (n // 2)
                nc.scalar.activation(dst[:, k, b:b + 4, :], PS[:, 4 + n, :].rearrange("p (b t) -> p b t", b=4),
                                     ACT.Copy).then_inc(copied, 1)
                if rounded:
                    nc.scalar.activation(rounded[1][:, k, b:b + 4, :], PS[:, 4 + n, :].rearrange("p (b t) -> p b t", b=4),
                                         ACT.Copy).then_inc(rounded[0], 1)

        def to_tokens(pe, src, ready, counts, done):
            for k in range(KT):
                pe.wait_ge(ready, counts[k])
                for n in range(4):
                    for b in (2 * n, 2 * n + 1):
                        at = (b % 2) * C + k * P
                        last = nc.tensor.transpose(PS[:, 4 + n, at:at + P], src[:, k, b, :], IDENT[:, :])
                    if k == KT - 1:
                        last.then_inc(done, 1)

        def add_tokens(dve, done):
            def pair_statistics(n):
                dve.wait_ge(vec.sem, summed[n])
                tile_statistics(2 * n)
                tile_statistics(2 * n + 1)
            summed = []
            for n in range(4):
                dve.wait_ge(done, n + 1)
                summed.append(vec.done(nc.vector.tensor_tensor(X[:, 2 * n:2 * n + 2, :],
                                             PS[:, 4 + n, :].rearrange("p (b c) -> p b c", b=2),
                                             X[:, 2 * n:2 * n + 2, :], ALU.add)))
                if n:
                    pair_statistics(n - 1)
            pair_statistics(3)
            v_sync()

        a_std = sem("a_std"); a_var = sem("a_var"); a_xn = sem("a_xn"); a_tp = sem("a_tp")
        a_qt = sem("a_qt"); a_toep = sem("a_toep"); a_kv = sem("a_kv"); a_conv = sem("a_conv")
        a_prod = sem("a_prod"); a_out = sem("a_out"); a_back = sem("a_back"); a_dec = sem("a_dec")
        a_copy = sem("a_copy"); a_pprod = sem("a_pprod")
        KVR = 3
        NC = 2 * NH
        OFF = NC // 4 - 1

        def offloaded(n):
            return n % 4 == 3 and n // 4 < OFF

        sums = []
        for n in range(NC):
            if n < NC and not offloaded(n):
                sums.append(n)
            if n >= 2 and offloaded(n - 2):
                sums.append(n - 2)

        def out_count(n):
            return sums.index(n) + 1

        def by_vector(n):
            return n + 1 - (n + 1) // 4
        with ExitStack() as sa:
            TOEP = sa.enter_context(nc.sbuf_tensor("TOEP", [P, NH, C], F32))
            DSK = sa.enter_context(nc.sbuf_tensor("DSK", [P, NH], F32))
            KV = sa.enter_context(nc.sbuf_tensor("KV", [P, KVR, KT * NB, HD, HD], F32))
            Z = sa.enter_context(nc.sbuf_tensor("Z", [P, 2, NB, HD, HD], F32))
            CONV = sa.enter_context(nc.sbuf_tensor("CONV", [P, 2, NB, HD, HD], F32))
            ZP = sa.enter_context(nc.sbuf_tensor("ZP", [P, 2, NB, HD, HD], F32))
            OT = sa.enter_context(nc.sbuf_tensor("OT", [P, KT, NB, P], F32))
            TD = sa.enter_context(nc.sbuf_tensor("TD", [P, KT], F32))
            block = sa.enter_context(nc.Block())

            @block.sync
            def _(sp):
                sp.dma_start(X[:, :, :], x.rearrange("b p c -> p b c")).then_inc(loaded_x, 16)
                sp.dma_start(CT[:, :, :, :], ctx_t).then_inc(loaded_ctx, 16)
                for g in range(4):
                    sp.dma_start(TOEP[:, 4 * g:4 * g + 4, :],
                                 toep[:, 4 * g:4 * g + 4, :]).then_inc(loaded_toep[min(g, 1)], 16)
                sp.wait_ge(loaded_toep[1], 48)
                for q in range(4):
                    sp.dma_start(SW1_0[:, :, :, :] if q == 0 else W1_0[:, 4 * q:4 * q + 4, :, :],
                                 sw1_0 if q == 0 else w1_0[:, 4 * q:4 * q + 4, :, :]
                                 ).then_inc(loaded_shared if q == 0 else loaded_w0, 16)
                sp.dma_start(W1_0[:, 0:4, :, :], w1_0[:, 0:4, :, :]).then_inc(loaded_w0, 16)
                sp.dma_start(SW2_0[:, :, :, :], sw2_0).then_inc(loaded_shared, 16)
                sp.dma_start(W2_0[:, :, :, :], w2_0).then_inc(loaded_w0, 16)
                sp.dma_start(SW1_1[:, :, :, :], sw1_1).then_inc(loaded_shared, 16)
                sp.dma_start(SW2_1[:, :, :, :], sw2_1).then_inc(loaded_shared, 16)

            @block.gpsimd
            def _(gp):
                p_link(nc.gpsimd.memset(IDENT[:, :], 0.0))
                p_link(nc.gpsimd.affine_select(out=IDENT[:, :], in_=IDENT[:, :], compare_op=ALU.not_equal, fill=1.0,
                                               base=0, pattern=[[-1, P]], channel_multiplier=1))
                nc.gpsimd.memset(ONES[:, :], 1.0).then_inc(consts_ready, 1)
                def times_q(j):
                    gp.wait_ge(a_copy, j + 1)
                    if j == 0:
                        gp.wait_ge(a_qt, 4)
                    if j >= 2:
                        gp.wait_ge(a_out, out_count(4 * j - 5))
                    y = CONV[:, j % 2, :, :, :].rearrange("p b i j -> p b j i")
                    h = 2 * j + 1
                    q = XNT[:, 1, :, h * HD:(h + 1) * HD].rearrange("p b (o i) -> p b o i", o=1)
                    nc.gpsimd.tensor_tensor(ZP[:, j % 2, :, :, :], y, q.broadcast_to([P, NB, HD, HD]),
                                            ALU.mult).then_inc(a_pprod, 1)

                gp.wait_ge(loaded_ctx, 16)
                for h in range(NH):
                    if h >= KVR:
                        gp.wait_ge(a_conv, 2 * (h - KVR + 1))
                    c = CT[:, :, :, h * HD:(h + 1) * HD].rearrange("p k b i -> p (k b) i")
                    nc.gpsimd.tensor_tensor(
                        KV[:, h % KVR, :, :, :],
                        c.rearrange("p n (i o) -> p n i o", o=1).broadcast_to([P, KT * NB, HD, HD]),
                        c.rearrange("p n (o i) -> p n o i", o=1).broadcast_to([P, KT * NB, HD, HD]),
                        ALU.mult).then_inc(a_kv, 1)
                    if h >= 4 and h % 2 == 0:
                        times_q(h // 2 - 2)
                times_q(OFF - 1)
                p_link(nc.gpsimd.memset(UPPER[:, :], 1.0))
                p_link(nc.gpsimd.affine_select(out=UPPER[:, :], in_=UPPER[:, :], compare_op=ALU.is_ge, fill=0.0,
                                               base=-1, pattern=[[1, P]], channel_multiplier=-1))
                p_link(nc.gpsimd.iota(IOTA_I[:, :], [[1, P]], base=0, channel_multiplier=0))
                p_link(nc.gpsimd.iota(VAL_I[:, :, :], [[NTOK, K0], [P, NB]], base=1, channel_multiplier=1))
                p_link(nc.gpsimd.tensor_copy(IOTA[:, :], IOTA_I[:, :]))
                p_link(nc.gpsimd.tensor_copy(VAL[:, :, :], VAL_I[:, :, :]))
                p_link(nc.gpsimd.tensor_scalar(IOTA1[:, :], IOTA[:, :], 1.0, None, ALU.add))
                p_link(nc.gpsimd.tensor_scalar(LIM[:, :], IOTA[:, 0:NB], float(P), None, ALU.mult))
                for r, n in ((RES, E0), (RES1, E1), (RES8, NB)):
                    p_link(nc.gpsimd.memset(r[:, :], 1.0))
                    p_link(nc.gpsimd.memset(r[:, :].rearrange("p (g n) -> p g n", n=n)[:, :, 0:1], 0.0))

            @block.scalar
            def _(act):
                for dst, src in ((DSK[:, :], d_skip), (GATE0[:, :, :], gate0), (GATE1[:, :, :], gate1),
                                 (NORM_W[:, :], norm_w), (TD[:, :], decay), (FIRST[:, :], first)):
                    act.dma_start(dst, src).then_inc(loaded_small, 16)
                act.wait_ge(a_var, 1)
                nc.scalar.activation(STD[:, :], STD[:, :], ACT.Sqrt).then_inc(a_std, 1)
                features_out(act, a_tp, a_qt, XNT)
                act.wait_ge(loaded_small, 96)
                nc.scalar.activation(DEC[:, :], TD[:, :], ACT.Exp).then_inc(a_dec, 1)
                act.wait_ge(a_dec, 1)
                nc.scalar.mul(DEC[:, :], DEC[:, :], -1.0).then_inc(a_dec, 1)
                for j in range(OFF):
                    act.wait_ge(a_conv, 4 * j + 4)
                    if j >= 2:
                        act.wait_ge(a_pprod, j - 1)
                    nc.scalar.activation(CONV[:, j % 2, :, :, :].rearrange("p b i j -> p (b i j)"), PS[:, 3, :],
                                         ACT.Copy).then_inc(a_copy, 1)

            @block.vector
            def _(dve):
                dve.wait_ge(loaded_x, 16)
                for i in range(NB):
                    tile_statistics(i)
                deviations(dve, 1e-5, a_std, a_var)
                normalize(XN, a_xn)
                dve.wait_ge(loaded_small, 96)
                dve.wait_ge(consts_ready, 1)

                def diagonal(h):
                    if h in (0, 4):
                        dve.wait_ge(loaded_toep[h // 4], 48 if h else 16)
                    nc.vector.scalar_tensor_tensor(TOEP[:, h, 0:P], IDENT[:, :], DSK[:, h:h + 1], TOEP[:, h, 0:P],
                                                   ALU.mult, ALU.add).then_inc(a_toep, 1)
                for h in range(3):
                    diagonal(h)
                products = 0
                for at, n in enumerate(sums):
                    h, lt = n // 2, n % 2
                    if offloaded(n):
                        dve.wait_ge(a_pprod, n // 4 + 1)
                        z = ZP[:, n // 4 % 2, :, :, :]
                    else:
                        dve.wait_ge(a_conv, n + 1)
                        dve.wait_ge(a_qt, 4)
                        if products >= 2:
                            dve.wait_ge(a_out, at - 1)
                        z = Z[:, products % 2, :, :, :]
                        y = PS[:, n % 4, :].rearrange("p (b i j) -> p b j i", b=NB, i=HD)
                        q = XNT[:, lt, :, h * HD:(h + 1) * HD].rearrange("p b (o i) -> p b o i", o=1)
                        nc.vector.tensor_tensor(z, y, q.broadcast_to([P, NB, HD, HD]), ALU.mult).then_inc(a_prod, 1)
                        products += 1
                        dve.wait_ge(a_prod, products)
                    nc.vector.tensor_reduce(OT[:, lt, :, h * HD:(h + 1) * HD], z, AX.X, ALU.add).then_inc(a_out, 1)
                    if n % 2 == 0 and h + 3 < NH:
                        diagonal(h + 3)
                add_tokens(dve, a_back)

            @block.tensor
            def _(pe):
                pe.wait_ge(consts_ready, 1)
                to_features(pe, a_xn, a_tp)
                for h in range(NH):
                    pe.wait_ge(a_kv, h + 1)
                    pe.wait_ge(a_toep, h + 1)
                    for lt in range(KT):
                        n = 2 * h + lt
                        if n >= 4 and n % 4 == 3:
                            pe.wait_ge(a_copy, n // 4)
                        elif n >= 4:
                            pe.wait_ge(a_prod, by_vector(n - 4))
                        kv = KV[:, h % KVR, :, :, :].rearrange("p (k b) i j -> p k (b i j)", k=KT)
                        if lt == 0:
                            last = nc.tensor.matmul(PS[:, n % 4, :], TOEP[:, h, 0:P], kv[:, 0, :], start=True, stop=True)
                        else:
                            nc.tensor.matmul(PS[:, n % 4, :], TOEP[:, h, P:C], kv[:, 0, :], start=True, stop=False)
                            last = nc.tensor.matmul(PS[:, n % 4, :], TOEP[:, h, 0:P], kv[:, 1, :],
                                                    start=False, stop=True)
                        last.then_inc(a_conv, 1)
                pe.wait_ge(a_qt, 4)
                to_tokens(pe, OT, a_out, [max(out_count(n) for n in range(lt, NC, 2)) for lt in range(KT)], a_back)

        def routed(lay):
            L, E, K, SU, NT = lay.number, lay.experts, lay.choices, lay.slices, lay.tiles
            SW1, SW2 = lay.shared
            G = E + (1 if L else 0)
            s = lambda name: sem(f"r{L}_{name}")
            var, std, xn_ok, tp, xnt, xn_rows = s("var"), s("std"), s("xn"), s("tp"), s("xnt"), s("xn_rows")
            logit, shifted, expd, sel_ok, counts, onehot, table, tables_ok = (
                s("logit"), s("shifted"), s("exp"), s("sel"), s("counts"), s("onehot"), s("table"), s("tables"))
            gathered = [s(f"gathered{i}") for i in range(GR)]
            scattered = [s(f"scattered{i}") for i in range(RING)]
            tx, xgt, gu, silu, up, hid, ta, at, dn, yout, so, so_used = (
                s("tx"), s("xgt"), s("gu"), s("silu"), s("up"), s("hid"), s("ta"), s("at"), s("dn"), s("yout"),
                s("so"), s("so_used"))
            hidx = s("hid_experts")
            if L == 1:
                ms, msr, sig_ok, stored = s("ms"), s("msr"), s("sig"), s("stored")
                h_ok, xnh, xnl, sw_hi, sw_lo, xgh, w_hi, w_lo = (
                    s("h"), s("xn_hi"), s("xn_lo"), s("sw_hi"), s("sw_lo"), s("xg_hi"), s("w_hi"), s("w_lo"))
            back_first, back_next = s("back_first"), s("back_next")
            back_last = [s(f"back_last{i}") for i in range(NB // 2)]
            v_summed, p_summed = s("v_summed"), s("p_summed")
            NS = NB * SU
            TAIL = (NT - 1) // 8 * 8
            DT = 6

            with ExitStack() as sr:
                def rb(name, shape, dt=F32):
                    return sr.enter_context(nc.sbuf_tensor(f"{name}_{L}", shape, dt))
                SH = rb("SH", [P, NB, E]); EX = rb("EX", [P, NB, E]); PR = rb("PR", [P, NB, E])
                GT = rb("GT", [P, NB, E]); EQ = rb("EQ", [P, NB, E]); CE = rb("CE", [P, NB, E])
                SEL = rb("SEL", [P, NB, E]); RK = rb("RK", [P, NB, E]); TMP = rb("TMP", [P, 4, NB, E])
                TOT = rb("TOT", [P, E, NB]); INC = rb("INC", [P, E, NB]); CMP = rb("CMP", [P, E, NB])
                POS = rb("POS", [P, NB, E]); VN = rb("VN", [P, NB, E]) if L else None
                OHJ = None if L else rb("OHJ", [P, NB, NT])
                M8 = rb("M8", [P, NB, 8]); MX = rb("MX", [P, NB]); NEED = rb("NEED", [P, NB])
                NTE = rb("NTE", [P, E]); ENDS = rb("ENDS", [P, E]); BASE = rb("BASE", [P, E])
                CK = rb("CK", [P, K, NB]); JK = rb("JK", [P, K, NB]); WK = rb("WK", [P, K, NB])
                GI = rb("GI", [P, K, NB], I32); CI = rb("CI", [P, K, NB], I32); JI = rb("JI", [P, K, NB], I32)
                OHA = rb("OHA", [P, 2, NB, P]); OHB = rb("OHB", [P, 2, NB, 2 * NT])
                ETC = rb("ETC", [1, NT, E]); ETF = rb("ETF", [1, NT]); ETI = rb("ETI", [1, NT], I32)
                DZ = rb("DZ", [P, NT]); DF = rb("DF", [P, NT]); DST = rb("DST", [P, NT], I32)
                SRC = rb("SRC", [P, NT], I32); WS = rb("WS", [P, NT])
                SIG = rb("SIG", [P, NB])
                if L == 0:
                    CTI = rb("CTI", [1, RING, K - 1], I32); CTA = rb("CTA", [1, RING, K - 1], I32)
                    CTF = rb("CTF", [1, RING, K - 1])
                XG = rb("XG", [P, GR, C])
                if L == 0:
                    XGT = rb("XGT", [P, 2, KT, P])
                else:
                    XGH = rb("XGH", [P, 2, KT, P], F32R); XGL = rb("XGL", [P, 2, KT, P], F32R)
                    XNTH = rb("XNTH", [P, KT, NB, P], F32R); XNTL = rb("XNTL", [P, KT, NB, P], F32R)
                    SW1H = rb("SW1H", [P, SU, KT, 2 * F], F32R); SW1L = rb("SW1L", [P, SU, KT, 2 * F], F32R)
                    W1H = rb("W1H", [P, WR, KT, 2 * F], F32R); W1L = rb("W1L", [P, WR, KT, 2 * F], F32R)
                SG = rb("SG", [P, 2, F]); UP = rb("UP", [P, 2, F]); HID = rb("HID", [P, 2, F])
                AT = rb("AT", [FH, 2, 2, P]); SO = rb("SO", [P, 2, C])
                Y = rb("Y", [P, RING, C])
                if L == 0:
                    weights = W1_0[:, :, :, :].rearrange("p e k n -> p (e k n)")
                    back = [weights[:, k * NB * C:(k + 1) * NB * C].rearrange("p (i c) -> p i c", i=NB)
                            for k in range(K - 1)] + [XG[:, :, :]]
                else:
                    back = [XN[:, :, :]] + [t[:, :, :, :].rearrange("p k b t -> p (k b t)").rearrange(
                        "p (i c) -> p i c", i=NB) for t in (XNT, CT)] + [XG[:, :, :]]

                def wait_choice(eng, k):
                    if k < K - 2:
                        eng.wait_ge(back_first, 16 * (K - 2))
                    else:
                        eng.wait_ge(back_next, 16)
                block = sr.enter_context(nc.Block())
                b_gu, b_tx, b_ta, b_dn = 0, 2, 4, 6
                lg = PS[:, 2, 0:NB * G].rearrange("p (i e) -> p i e", e=G)
                pw = PS[:, 3, 0:NB * E].rearrange("p (i e) -> p i e", e=E)
                tot = PS[:, 3, 256:256 + NB * E].rearrange("p (i e) -> p e i", e=E)
                tab = PS[:, 2, 0:2 * NT]

                def wait_hidden(eng, n):
                    if isinstance(n, int) and n < NS:
                        eng.wait_ge(hid, n + 1)
                    else:
                        eng.wait_ge(hidx, n - NS + 1)

                def per_tile(a, n=E):
                    return a[:, :].rearrange("p (i o) -> p i o", o=1).broadcast_to([P, NB, n])

                @block.sync
                def _(sp):
                    sp.wait_ge(xn_ok, 2)
                    sp.dma_start(xn_dram[L].rearrange("(i p) c -> p i c", p=P), XN[:, :, :]).then_inc(xn_rows, 16)
                    if L == 1:
                        lay.load_rest(sp, w_lo, dn, NS)
                    yv = y_dram[L].rearrange("(k i p) c -> k p i c", k=K, p=P)
                    if L == 0:
                        sp.wait_ge(tables_ok, 1)
                        due = [[sp.value_load(CTI[0:1, r, k:k + 1], min_val=16, max_val=16 * ((NT + RING - 1) // RING))
                                for r in range(RING)] for k in range(K - 1)]
                    else:
                        due = [[16 * ((E - K + k + 1 + RING - 1 - r) // RING) for r in range(RING)]
                               for k in range(K - 1)]
                    for k in range(K - 1):
                        for r in range(RING):
                            sp.wait_ge(scattered[r], due[k][r])
                        sp.dma_start(back[k], yv[k]).then_inc(back_first if k < K - 2 else back_next, 16)
                    for r in range(RING):
                        sp.wait_ge(scattered[r], 16 * ((NT + RING - 1 - r) // RING))
                    for q in (3, 0, 1, 2):
                        sp.dma_start(back[K - 1][:, 2 * q:2 * q + 2, :],
                                     yv[K - 1][:, 2 * q:2 * q + 2, :]).then_inc(back_last[q], 16)
                    if L == 1:
                        for q in range(NB // 2):
                            if 2 * q < DT:
                                sp.wait_ge(v_summed, q + 1)
                            else:
                                sp.wait_ge(p_summed, 1)
                            sp.dma_start(out[2 * q:2 * q + 2].rearrange("b p c -> p b c"),
                                         X[:, 2 * q:2 * q + 2, :]).then_inc(stored, 16)
                        sp.wait_ge(stored, 16 * (NB // 2))

                @block.gpsimd
                def _(gp):
                    def gather(j):
                        if j >= GR:
                            gp.wait_ge(tx, j - GR + 1)
                        nc.gpsimd.indirect_dma_start(
                            XG[:, j % GR, :], None, xn_dram[L],
                            bass.IndirectOffsetOnAxis(ap=SRC[:, j:j + 1], axis=0)).then_inc(gathered[j % GR], 16)

                    def scatter(j):
                        gp.wait_ge(yout, j + 1)
                        nc.gpsimd.indirect_dma_start(
                            y_dram[L], bass.IndirectOffsetOnAxis(ap=DST[:, j:j + 1], axis=0),
                            Y[:, j % RING, :], None, bounds_check=K * NTOK - 1,
                            oob_is_err=False).then_inc(scattered[j % RING], 16)

                    def first_gather(j):
                        if j == 0:
                            gp.wait_ge(tables_ok, 1)
                            gp.wait_ge(xn_rows, 16)
                        gather(j)

                    def add_shared(i):
                        gp.wait_ge(so, i + 1)
                        nc.gpsimd.tensor_tensor(X[:, i, :], SO[:, i % 2, :], X[:, i, :],
                                                ALU.add).then_inc(so_used, 1)

                    if L == 1:
                        for u in range(SU):
                            gp.wait_ge(sw_hi, u + 1)
                            nc.gpsimd.tensor_tensor(SW1L[:, u, :, :], SW1[:, u, :, :],
                                                    SW1H[:, u, :, :].bitcast(F32), ALU.subtract).then_inc(sw_lo, 1)
                    ahead = 0
                    for n in range(NS):
                        if L == 0 and n >= NS - 2:
                            first_gather(ahead)
                            ahead += 1
                        gp.wait_ge(up, n + 1)
                        if n >= 2:
                            gp.wait_ge(ta, n - 1)
                        nc.gpsimd.tensor_tensor(HID[:, n % 2, :], SG[:, n % 2, :], UP[:, n % 2, :],
                                                ALU.mult).then_inc(hid, 1)
                        if L == 1 and n < 4:
                            gp.wait_ge(h_ok, n // 2 + 1)
                            for i in (2 * n, 2 * n + 1):
                                pool.done(nc.gpsimd.tensor_tensor(X[:, i, :], X[:, i, :], XG[:, i, :], ALU.add))
                        if n >= 3 and (n - 2) % SU == 0:
                            gp.wait_ge(pool.sem, pool.n)
                            add_shared((n - 2) // SU - 1)
                        if lay.gathers_at and n >= lay.gathers_at and ahead < GR - 1:
                            first_gather(ahead)
                            ahead += 1
                    for j in range(ahead, GR - 1):
                        first_gather(j)
                    for i in range((NS - 3) // SU, NB):
                        add_shared(i)
                    for j in range(NT):
                        if j + GR - 1 < NT:
                            gather(j + GR - 1)
                        scatter(j)
                    gp.wait_ge(so_used, NB)
                    for k in range(K - 1):
                        wait_choice(gp, k)
                        p_link(nc.gpsimd.tensor_tensor(X[:, DT:, :], X[:, DT:, :], back[k][:, DT:, :], ALU.add))
                    gp.wait_ge(back_last[3], 16)
                    nc.gpsimd.tensor_tensor(X[:, DT:, :], X[:, DT:, :], back[K - 1][:, DT:, :],
                                            ALU.add).then_inc(p_summed, 1)

                def shared_out(act, i):
                    act.wait_ge(dn, (i + 1) * SU)
                    if i >= 2:
                        act.wait_ge(so_used, i - 1)
                    if L == 1 and i == 0:
                        act.wait_ge(sig_ok, 1)
                    scale = SIG[:, i:i + 1] if L else 1.0
                    nc.scalar.activation(SO[:, i % 2, :], PS[:, b_dn + i % 2, 0:C], ACT.Copy,
                                         scale=scale).then_inc(so, 1)

                @block.scalar
                def _(act):
                    act.wait_ge(var, 1)
                    nc.scalar.activation(STD[:, :], STD[:, :], ACT.Sqrt).then_inc(std, 1)
                    if L == 1:
                        act.wait_ge(ms, 1)
                        nc.scalar.activation(STD[:, :], STD[:, :], ACT.Sqrt).then_inc(msr, 1)
                        for u in range(SU):
                            nc.scalar.activation(SW1H[:, u, :, :], SW1[:, u, :, :], ACT.Copy).then_inc(sw_hi, 1)
                    features_out(act, tp, xnt, XNT, (xnh, XNTH) if L else None)
                    def router_exp():
                        act.wait_ge(shifted, 1)
                        nc.scalar.activation(EX[:, :, :], SH[:, :, :], ACT.Exp).then_inc(expd, 1)
                        if L == 1:
                            nc.scalar.activation(SIG[:, :], lg[:, :, E], ACT.Exp, scale=-1.0).then_inc(expd, 1)


                    def silu_step(n, s_):
                        act.wait_ge(gu, n + 1)
                        if not isinstance(n, int) or n >= 2:
                            wait_hidden(act, n - 2)
                        nc.scalar.activation(SG[:, s_, :], PS[:, b_gu + s_, 0:F], ACT.Silu).then_inc(silu, 1)

                    def hidden_out(n, s_):
                        act.wait_ge(ta, n + 1)
                        if not isinstance(n, int) or n >= 2:
                            act.wait_ge(dn, n - 1)
                        nc.scalar.activation(AT[:, s_, :, :],
                                             PS[0:FH, b_ta + s_, 0:2 * P].rearrange("p (k t) -> p k t", k=2),
                                             ACT.Copy).then_inc(at, 1)

                    def round_weights(e):
                        g = e // 2
                        act.wait_ge(lay.ring_w1[g % (WR // 2)], 16 * (g // (WR // 2) + 1))
                        if e >= WR:
                            act.wait_ge(gu, NS + e - WR + 1)
                        nc.scalar.activation(W1H[:, e % WR, :, :], lay.w1[:, e % WR, :, :], ACT.Copy).then_inc(w_hi, 1)

                    def round_rows(j):
                        act.wait_ge(tx, j + 1)
                        if j >= 2:
                            act.wait_ge(gu, NS + j - 1)
                        nc.scalar.activation(XGH[:, j % 2, :, :],
                                             PS[:, b_tx + j % 2, 0:C].rearrange("p (k t) -> p k t", k=KT),
                                             ACT.Copy).then_inc(xgh, 1)

                    for n in range(NS):
                        if L == 0 and n == 0:
                            router_exp()
                        if L == 1 and NS - 16 <= n < NS - 16 + WAHEAD:
                            round_weights(n - NS + 16)
                        if n >= 3 and (n - 2) % SU == 0:
                            shared_out(act, (n - 2) // SU - 1)
                        if n >= 2:
                            hidden_out(n - 2, n % 2)
                        silu_step(n, n % 2)
                        nc.scalar.activation(UP[:, n % 2, :], PS[:, b_gu + n % 2, F:2 * F], ACT.Copy).then_inc(up, 1)
                        if L == 1 and n == 2:
                            router_exp()
                    done = (NS - 3) // SU

                    def expert_step(j, n, s_, r, sent, first=False, last=False):
                        if r is not None:
                            act.wait_ge(dn, n - 2)
                            if sent is not None:
                                act.wait_ge(scattered[r], sent)
                            nc.scalar.activation(Y[:, r, :], PS[:, b_dn + (s_ + 1) % 2, 0:C], ACT.Copy,
                                                 scale=WS[:, bass.ds(j - 3, 1)]).then_inc(yout, 1)
                        hidden_out(n - 2, s_ % 2)
                        if L == 1 and j + 1 < NT:
                            round_rows(j + 1)
                        silu_step(n, s_ % 2)
                        if L == 1 and j + WAHEAD < NT:
                            round_weights(j + WAHEAD)

                    for j in range(3):
                        if j == 0 and done < NB - 1:
                            shared_out(act, NB - 2)
                        if L == 1 and j == 0:
                            round_rows(0)
                        hidden_out(NS + j - 2, j % 2)
                        if j == 0:
                            act.wait_ge(tables_ok, 1)
                        if j == 1:
                            shared_out(act, NB - 1)
                        if L == 1:
                            round_rows(j + 1)
                        silu_step(NS + j, j % 2)
                        if L == 1:
                            round_weights(j + WAHEAD)
                    for j in range(3, 8):
                        expert_step(j, NS + j, j, (j - 3) % RING, 16 * ((j - 3) // RING) or None)
                    if lay.looped:
                        with act.Fori(1, TAIL // 8) as q:
                            for t in range(8):
                                expert_step(8 * q + t, NS + 8 * q + t, t, (t - 3) % RING, 16 * (2 * q + (t - 3) // RING))
                    for j in range(TAIL if lay.looped else 8, NT):
                        expert_step(j, NS + j, j, (j - 3) % RING, 16 * ((j - 3) // RING))
                    for j in range(NT, NT + 3):
                        act.wait_ge(dn, NS + j - 2)
                        act.wait_ge(scattered[(j - 3) % RING], 16 * ((j - 3) // RING))
                        nc.scalar.activation(Y[:, (j - 3) % RING, :], PS[:, b_dn + (j + 1) % 2, 0:C], ACT.Copy,
                                             scale=WS[:, j - 3:j - 2]).then_inc(yout, 1)
                        if j < NT + 2:
                            hidden_out(NS + j - 2, j % 2)

                @block.vector
                def _(dve):
                    deviations(dve, 1e-5, std, var)
                    if L == 0:
                        normalize(XN, xn_ok)
                    else:
                        v_link(nc.vector.tensor_tensor(STD[:, :], RSTD[:, :], RSTD[:, :], ALU.mult))
                        v_link(nc.vector.tensor_tensor(STD[:, :], STD[:, :], MV[:, :, 1], ALU.mult))
                        v_link(nc.vector.tensor_scalar(STD[:, :], STD[:, :], 1e-6, None, ALU.add))
                        nc.vector.engine_nop().then_inc(ms, 1)
                        normalize(XG, h_ok)
                        dve.wait_ge(msr, 1)
                        v_link(nc.vector.reciprocal(RSTD[:, :], STD[:, :]))
                        for i in range(NB):
                            v_do(nc.vector.scalar_tensor_tensor(XN[:, i, :], XG[:, i, :], RSTD[:, i:i + 1],
                                                                NORM_W[:, :], ALU.mult, ALU.mult))
                            if i % 4 == 3:
                                v_sync()
                                nc.vector.engine_nop().then_inc(xn_ok, 1)
                        for h in range(2):
                            b = 4 * h
                            dve.wait_ge(xnh, 2 * h + 2)
                            nc.vector.tensor_tensor(XNTL[:, :, b:b + 4, :], XNT[:, :, b:b + 4, :],
                                                    XNTH[:, :, b:b + 4, :].bitcast(F32), ALU.subtract).then_inc(xnl, 1)

                    dve.wait_ge(logit, 1)
                    v_link(nc.vector.tensor_reduce(MX[:, :], lg[:, :, 0:E], AX.X, ALU.max))
                    nc.vector.tensor_tensor(SH[:, :, :], lg[:, :, 0:E], per_tile(MX), ALU.subtract).then_inc(shifted, 1)
                    dve.wait_ge(expd, 1 + L)
                    v_link(nc.vector.tensor_reduce(MX[:, :], EX[:, :, :], AX.X, ALU.add))
                    v_link(nc.vector.reciprocal(MX[:, :], MX[:, :]))
                    v_do(nc.vector.tensor_tensor(PR[:, :, :], EX[:, :, :], per_tile(MX), ALU.mult))
                    if L == 1:
                        v_link(nc.vector.tensor_scalar(SIG[:, :], SIG[:, :], 1.0, None, ALU.add))
                        v_do(nc.vector.reciprocal(SIG[:, :], SIG[:, :]))
                    v_sync()
                    if L == 1:
                        nc.vector.engine_nop().then_inc(sig_ok, 1)
                    for i in range(NB):
                        v_do(nc.vector.max(M8[:, i, :], PR[:, i, :]))
                    v_sync()
                    kth = M8[:, :, K - 1:K].broadcast_to([P, NB, E])
                    v_do(nc.vector.tensor_tensor(GT[:, :, :], PR[:, :, :], kth, ALU.is_gt))
                    v_do(nc.vector.tensor_tensor(EQ[:, :, :], PR[:, :, :], kth, ALU.is_equal))
                    v_sync()
                    flat = lambda a: a[:, :, :].rearrange("p a b -> p (a b)")
                    resets = (RES1 if L else RES)[:, 0:NB * E]
                    v_do(nc.vector.tensor_reduce(MX[:, :], GT[:, :, :], AX.X, ALU.add))
                    v_do(nc.vector.tensor_tensor_scan(flat(CE), resets, flat(EQ), 0.0, ALU.mult, ALU.add))
                    v_sync()
                    v_link(nc.vector.tensor_scalar(NEED[:, :], MX[:, :], -1.0, float(K), ALU.mult, ALU.add))
                    v_link(nc.vector.tensor_tensor(CE[:, :, :], CE[:, :, :], per_tile(NEED), ALU.is_le))
                    v_link(nc.vector.tensor_tensor(EQ[:, :, :], EQ[:, :, :], CE[:, :, :], ALU.mult))
                    v_link(nc.vector.tensor_tensor(SEL[:, :, :], GT[:, :, :], EQ[:, :, :], ALU.add))
                    nc.vector.engine_nop().then_inc(sel_ok, 1)
                    v_do(nc.vector.tensor_tensor_scan(flat(RK), resets, flat(SEL), 0.0, ALU.mult, ALU.add))
                    dve.wait_ge(counts, 1)
                    v_link(nc.vector.tensor_copy(TOT[:, :, :], tot))
                    v_link(nc.vector.tensor_tensor_scan(flat(INC), RES8[:, 0:NB * E], flat(TOT), 0.0,
                                                        ALU.mult, ALU.add))
                    if L == 0:
                        total = INC[:, :, NB - 1:NB].broadcast_to([P, E, NB])
                        lim = LIM[:, :].rearrange("p (o i) -> p o i", o=1).broadcast_to([P, E, NB])
                        v_link(nc.vector.tensor_tensor(CMP[:, :, :], total, lim, ALU.is_gt))
                        v_link(nc.vector.tensor_reduce(NTE[:, :], CMP[:, :, :], AX.X, ALU.add))
                        v_link(nc.vector.tensor_tensor_scan(ENDS[:, :], ONES[:, 0:E], NTE[:, :], 0.0,
                                                            ALU.mult, ALU.add))
                        v_do(nc.vector.tensor_tensor(BASE[:, :], ENDS[:, :], NTE[:, :], ALU.subtract))
                        v_sync()
                        v_do(nc.vector.tensor_scalar(BASE[:, :], BASE[:, :], float(P), None, ALU.mult))
                    v_link(nc.vector.tensor_tensor(INC[:, :, :], INC[:, :, :], TOT[:, :, :], ALU.subtract))
                    v_link(nc.vector.tensor_tensor(POS[:, :, :], pw, INC[:, :, :].rearrange("p e i -> p i e"), ALU.add))
                    if L == 0:
                        base = BASE[:, :].rearrange("p (o e) -> p o e", o=1).broadcast_to([P, NB, E])
                        v_link(nc.vector.tensor_tensor(POS[:, :, :], POS[:, :, :], base, ALU.add))
                    else:
                        v_link(nc.vector.scalar_tensor_tensor(flat(SEL), flat(POS), float(P), flat(SEL),
                                                              ALU.is_lt, ALU.mult))
                    v_do(nc.vector.scalar_tensor_tensor(flat(POS), flat(POS), 1.0, flat(SEL), ALU.add, ALU.mult))
                    v_do(nc.vector.tensor_tensor(PR[:, :, :], PR[:, :, :], SEL[:, :, :], ALU.mult))
                    row_c = lambda a: a.rearrange("p (o c) -> p o c", o=1)
                    col_c = lambda a: a.rearrange("p (i o) -> p i o", o=1)
                    if L == 1:
                        v_link(nc.vector.tensor_scalar(VN[:, :, :], RK[:, :, :], -1.0, float(NTOK), ALU.add, ALU.mult))
                        v_link(nc.vector.tensor_tensor(VN[:, :, :], VN[:, :, :],
                                                       col_c(VAL[:, 0, :]).broadcast_to([P, NB, E]), ALU.add))
                        v_do(nc.vector.tensor_tensor(VN[:, :, :], VN[:, :, :], SEL[:, :, :], ALU.mult))
                    v_sync()

                    def pick(k, src, dst):
                        v_do(nc.vector.scalar_tensor_tensor(dst, RK[:, :, :], float(k + 1), src[:, :, :],
                                                            ALU.is_equal, ALU.mult))

                    if L == 0:
                        for k in range(K):
                            pick(k, POS, TMP[:, 2 * (k % 2), :, :])
                            pick(k, PR, TMP[:, 2 * (k % 2) + 1, :, :])
                            v_sync()
                            v_do(nc.vector.tensor_reduce(CK[:, k, :], TMP[:, 2 * (k % 2), :, :], AX.X, ALU.add))
                            v_do(nc.vector.tensor_reduce(WK[:, k, :], TMP[:, 2 * (k % 2) + 1, :, :], AX.X, ALU.add))
                        v_sync()
                        v_link(nc.vector.tensor_scalar(GI[:, :, :], CK[:, :, :], -1.0, None, ALU.add))
                        v_do(nc.vector.tensor_scalar(CI[:, :, :], GI[:, :, :], P - 1, None, ALU.bitwise_and))
                        v_do(nc.vector.tensor_scalar(JI[:, :, :], GI[:, :, :], 7, None, ALU.logical_shift_right))
                        v_sync()
                        v_do(nc.vector.tensor_copy(CK[:, :, :], CI[:, :, :]))
                        v_do(nc.vector.tensor_copy(JK[:, :, :], JI[:, :, :]))
                        v_sync()
                    for k in range(K):
                        if k >= 2:
                            dve.wait_ge(table, k - 1)
                        number, weight = OHB[:, k % 2, :, 0:NT], OHB[:, k % 2, :, NT:]
                        if L == 0:
                            one_hot = [P, NB, NT]
                            v_do(nc.vector.tensor_tensor(OHJ[:, :, :], row_c(IOTA[:, 0:NT]).broadcast_to(one_hot),
                                                         col_c(JK[:, k, :]).broadcast_to(one_hot), ALU.is_equal))
                            slot = CK[:, k, :]
                        else:
                            pick(k, VN, number)
                            pick(k, PR, weight)
                            pick(k, POS, TMP[:, 0, :, :])
                            v_sync()
                            v_link(nc.vector.tensor_reduce(CK[:, k, :], TMP[:, 0, :, :], AX.X, ALU.add))
                            slot = CK[:, k, :]
                        v_do(nc.vector.tensor_tensor(
                            OHA[:, k % 2, :, :], row_c(IOTA[:, :] if L == 0 else IOTA1[:, :]).broadcast_to([P, NB, P]),
                            col_c(slot).broadcast_to([P, NB, P]), ALU.is_equal))
                        if L == 0:
                            v_sync()
                            v_do(nc.vector.tensor_tensor(number, OHJ[:, :, :],
                                                         col_c(VAL[:, k, :]).broadcast_to(one_hot), ALU.mult))
                            v_do(nc.vector.tensor_tensor(weight, OHJ[:, :, :],
                                                         col_c(WK[:, k, :]).broadcast_to(one_hot), ALU.mult))
                        v_sync()
                        nc.vector.engine_nop().then_inc(onehot, 1)
                    if L == 0:
                        v_link(nc.vector.tensor_tensor(
                            ETC[:, :, :], IOTA[0:1, 0:NT].rearrange("p (j o) -> p j o", o=1).broadcast_to([1, NT, E]),
                            ENDS[0:1, :].rearrange("p (o e) -> p o e", o=1).broadcast_to([1, NT, E]), ALU.is_ge))
                        v_link(nc.vector.tensor_reduce(ETF[:, :], ETC[:, :, :], AX.X, ALU.add))
                        v_link(nc.vector.tensor_scalar(ETF[:, :], ETF[:, :], float(E - 1), None, ALU.min))
                        v_do(nc.vector.tensor_copy(ETI[:, :], ETF[:, :]))
                        for r in range(RING):
                            v_do(nc.vector.tensor_scalar(CTI[:, r, :], ENDS[0:1, E - K:E - 1], float(RING - 1 - r),
                                                         None, ALU.add))
                        v_sync()
                        v_link(nc.vector.tensor_scalar(CTA[:, :, :], CTI[:, :, :], 124, None, ALU.bitwise_and))
                        v_link(nc.vector.tensor_copy(CTF[:, :, :], CTA[:, :, :]))
                        v_link(nc.vector.tensor_scalar(CTI[:, :, :], CTF[:, :, :], float(16 // RING), None, ALU.mult))
                    dve.wait_ge(table, K)
                    v_do(nc.vector.tensor_copy(WS[:, :], tab[:, NT:]))
                    v_link(nc.vector.tensor_scalar(DZ[:, :], tab[:, 0:NT], 0.0, UNUSED, ALU.is_equal, ALU.mult))
                    v_link(nc.vector.scalar_tensor_tensor(DF[:, :], tab[:, 0:NT], -1.0, DZ[:, :], ALU.add, ALU.add))
                    v_link(nc.vector.tensor_copy(DST[:, :], DF[:, :]))
                    v_link(nc.vector.tensor_scalar(SRC[:, :], DST[:, :], NTOK - 1, None, ALU.bitwise_and))
                    nc.vector.engine_nop().then_inc(tables_ok, 1)

                    def weights_rest(e):
                        dve.wait_ge(w_hi, e + 1)
                        nc.vector.tensor_tensor(W1L[:, e % WR, :, :], lay.w1[:, e % WR, :, :],
                                                W1H[:, e % WR, :, :].bitcast(F32), ALU.subtract).then_inc(w_lo, 1)

                    def rows_out(j, s_):
                        dve.wait_ge(xgh if L else tx, j + 1)
                        if not isinstance(j, int) or j >= 2:
                            dve.wait_ge(gu, NS + j - 1)
                        if L == 1:
                            nc.vector.tensor_tensor(XGL[:, s_, :, :],
                                                    PS[:, b_tx + s_, 0:C].rearrange("p (k t) -> p k t", k=KT),
                                                    XGH[:, s_, :, :].bitcast(F32), ALU.subtract).then_inc(xgt, 1)
                            return
                        nc.vector.tensor_copy(XGT[:, s_, :, :],
                                              PS[:, b_tx + s_, 0:C].rearrange("p (k t) -> p k t", k=KT)).then_inc(xgt, 1)

                    def hidden(n, s_):
                        dve.wait_ge(silu, n + 1)
                        dve.wait_ge(ta, n - 1)
                        nc.vector.tensor_tensor(HID[:, s_, :], SG[:, s_, :], PS[:, b_gu + s_, F:2 * F],
                                                ALU.mult).then_inc(hidx, 1)

                    if L == 1:
                        for e in range(WAHEAD):
                            weights_rest(e)
                    rows_out(0, 0)
                    for j in range(8):
                        rows_out(j + 1, (j + 1) % 2)
                        hidden(NS + j, j % 2)
                        if L == 1:
                            weights_rest(j + WAHEAD)
                    if lay.looped:
                        with dve.Fori(1, TAIL // 8) as q:
                            for t in range(8):
                                rows_out(8 * q + t + 1, (t + 1) % 2)
                                hidden(NS + 8 * q + t, t % 2)
                    else:
                        for j in range(8, TAIL):
                            rows_out(j + 1, (j + 1) % 2)
                            hidden(NS + j, j % 2)
                            weights_rest(j + WAHEAD)
                    for j in range(TAIL, NT):
                        if j + 1 < NT:
                            rows_out(j + 1, (j + 1) % 2)
                        hidden(NS + j, j % 2)
                        if L == 1 and j + WAHEAD < NT:
                            weights_rest(j + WAHEAD)
                    dve.wait_ge(so_used, NB)
                    for k in range(K - 1):
                        wait_choice(dve, k)
                        v_link(nc.vector.tensor_tensor(X[:, 0:DT, :], X[:, 0:DT, :], back[k][:, 0:DT, :], ALU.add))
                    for q in range(DT // 2):
                        dve.wait_ge(back_last[q], 16)
                        pair = slice(2 * q, 2 * q + 2)
                        nc.vector.tensor_tensor(X[:, pair, :], X[:, pair, :], back[K - 1][:, pair, :],
                                                ALU.add).then_inc(v_summed, 1)
                        if L == 0 and q:
                            dve.wait_ge(v_summed, q)
                            tile_statistics(2 * q - 2)
                            tile_statistics(2 * q - 1)
                    if L == 0:
                        dve.wait_ge(v_summed, DT // 2)
                        tile_statistics(DT - 2)
                        tile_statistics(DT - 1)
                        dve.wait_ge(p_summed, 1)
                        tile_statistics(DT)
                        tile_statistics(DT + 1)
                        v_sync()

                @block.tensor
                def _(pe):
                    to_features(pe, xn_ok, tp)
                    pe.wait_ge(xnt, 4)

                    def router():
                        gate = GATE1 if L else GATE0
                        for i in range(NB):
                            for k in range(KT):
                                last = nc.tensor.matmul(lg[:, i, :], XNT[:, k, i, :], gate[:, k, :],
                                                        start=(k == 0), stop=(k == KT - 1))
                        last.then_inc(logit, 1)

                    if L == 0:
                        router()
                    pe.wait_ge(loaded_shared, 64)

                    def queue_counts():
                        pe.wait_ge(sel_ok, 1)
                        flat = SEL[:, :, :].rearrange("p a b -> p (a b)")
                        nc.tensor.matmul(PS[:, 3, 0:NB * E], UPPER[:, :], flat, start=True, stop=True)
                        nc.tensor.matmul(PS[:, 3, 256:256 + NB * E], ONES[:, :], flat, start=True,
                                         stop=True).then_inc(counts, 1)

                    def tables(k):
                        pe.wait_ge(onehot, k + 1)
                        for i in range(NB):
                            last = nc.tensor.matmul(tab, OHA[:, k % 2, i, :], OHB[:, k % 2, i, :],
                                                    start=(k == 0 and i == 0), stop=(k == K - 1 and i == NB - 1))
                        last.then_inc(table, 1)

                    def rows_t(j, s_, r, cnt):
                        pe.wait_ge(gathered[r], cnt)
                        if not isinstance(j, int) or j >= 2:
                            pe.wait_ge(xgt, j - 1)
                        for k in range(KT):
                            last = nc.tensor.transpose(PS[:, b_tx + s_, k * P:(k + 1) * P],
                                                       XG[:, r, k * P:(k + 1) * P], IDENT[:, :])
                        last.then_inc(tx, 1)

                    def gate_up(n, s_, lhs, w):
                        if not isinstance(n, int) or n >= 2:
                            wait_hidden(pe, n - 2)
                        for k in range(KT):
                            last = nc.tensor.matmul(PS[:, b_gu + s_, 0:2 * F], lhs(k), w(k),
                                                    start=(k == 0), stop=(k == KT - 1))
                        last.then_inc(gu, 1)

                    def gate_up_split(n, s_, hi, lo, w_hi_, w_lo_):
                        if n >= 2:
                            wait_hidden(pe, n - 2)
                        terms = [(a, w, k) for a, w in ((hi, w_hi_), (hi, w_lo_), (lo, w_hi_)) for k in range(KT)]
                        for m, (a, w, k) in enumerate(terms):
                            last = nc.tensor.matmul(PS[:, b_gu + s_, 0:2 * F], a(k), w(k),
                                                    start=(m == 0), stop=(m == len(terms) - 1))
                        last.then_inc(gu, 1)

                    def gate_up_shared(n):
                        i, u = n // SU, n % SU
                        if L == 0:
                            gate_up(n, n % 2, lambda k: XNT[:, k, i, :], lambda k: SW1[:, u, k, :])
                        else:
                            if n < SU:
                                pe.wait_ge(sw_lo, n + 1)
                            if n % (NS // 2) == 0:
                                pe.wait_ge(xnl, 1 + n // (NS // 2))
                            gate_up_split(n, n % 2, lambda k: XNTH[:, k, i, :], lambda k: XNTL[:, k, i, :],
                                          lambda k: SW1H[:, u, k, :], lambda k: SW1L[:, u, k, :])

                    def gate_up_expert(j, n, t, e):
                        if L == 0:
                            gate_up(n, t % 2, lambda k: XGT[:, t % 2, k, :], lay.up_weights(pe, j, e))
                        else:
                            pe.wait_ge(w_lo, j + 1)
                            gate_up_split(n, t % 2, lambda k: XGH[:, t % 2, k, :], lambda k: XGL[:, t % 2, k, :],
                                          lambda k: W1H[:, j % WR, k, :], lambda k: W1L[:, j % WR, k, :])

                    def hidden_t(n, s_):
                        wait_hidden(pe, n)
                        if not isinstance(n, int) or n >= 2:
                            pe.wait_ge(at, n - 1)
                        for k in range(2):
                            last = nc.tensor.transpose(PS[0:FH, b_ta + s_, k * P:(k + 1) * P],
                                                       HID[:, s_, k * FH:(k + 1) * FH], IDENT[:, :])
                        last.then_inc(ta, 1)

                    def down(n, s_, bank, w, start=True, stop=True):
                        pe.wait_ge(at, n + 1)
                        for k in range(2):
                            last = nc.tensor.matmul(PS[:, bank, 0:C], AT[:, s_, k, :], w(k),
                                                    start=(start and k == 0), stop=(stop and k == 1))
                        last.then_inc(dn, 1)

                    def down_shared(n):
                        i, u = n // SU, n % SU
                        if u == 0 and i >= 2:
                            pe.wait_ge(so, i - 1)
                        down(n, n % 2, b_dn + i % 2, lambda k: SW2[:, u, k, :], u == 0, u == SU - 1)

                    def down_expert(j, n, s_, e):
                        if not isinstance(j, int) or j >= 2:
                            pe.wait_ge(yout, j - 1)
                        down(n, s_, b_dn + s_, lay.down_weights(pe, j, e))

                    for n in range(NS):
                        i, u = n // SU, n % SU
                        if L == 1 and n == 2:
                            router()
                        if n == lay.counts_at:
                            queue_counts()
                        for k in range(K):
                            if n == lay.tables_at[k]:
                                tables(k)
                        if n >= 2:
                            hidden_t(n - 2, n % 2)
                        gate_up_shared(n)
                        if n >= 2:
                            down_shared(n - 2)
                    pe.wait_ge(tables_ok, 1)
                    lay.wait_weights(pe)

                    def expert_unit(j, n, t, e, before, cnt, more=True):
                        if more:
                            rows_t(j + 1, (t + 1) % 2, (t + 1) % GR, cnt)
                        hidden_t(n - 2, t % 2)
                        pe.wait_ge(xgt, j + 1)
                        gate_up_expert(j, n, t, e)
                        down_expert(j - 2, n - 2, t % 2, before)

                    rows_t(0, 0, 0, 16)
                    expert = lambda j: lay.expert_of(pe, ETI, j)
                    before = [None, None]
                    for j in range(8):
                        e = expert(j)
                        if j < 2:
                            rows_t(j + 1, (j + 1) % 2, j + 1, 16)
                            hidden_t(NS + j - 2, j % 2)
                            pe.wait_ge(xgt, j + 1)
                            gate_up_expert(j, NS + j, j, e)
                            down_shared(NS + j - 2)
                            if j == 1:
                                pe.wait_ge(so, NB)
                        else:
                            expert_unit(j, NS + j, j, e, before[0], 16 * ((j + 1) // GR + 1))
                        before = [before[1], e]
                    if lay.looped:
                        with pe.Fori(0, (TAIL - 8) // 16) as q:
                            before = [expert(16 * q + 6), expert(16 * q + 7)]
                            for t in range(16):
                                j = 16 * q + 8 + t
                                e = expert(j)
                                expert_unit(j, NS + 16 * q + 8 + t, t, e, before[0],
                                            16 * (2 * q + (t + 9) // GR + 1))
                                before = [before[1], e]
                        before = [expert(TAIL - 2), expert(TAIL - 1)]
                    else:
                        for j in range(8, TAIL):
                            expert_unit(j, NS + j, j, None, None, 16 * ((j + 1) // GR + 1))
                    for j in range(TAIL, NT):
                        e = expert(j)
                        expert_unit(j, NS + j, j, e, before[0], 16 * ((j + 1) // GR + 1), j + 1 < NT)
                        before = [before[1], e]
                    for j in range(NT, NT + 2):
                        hidden_t(NS + j - 2, j % 2)
                        down_expert(j - 2, NS + j - 2, j % 2, before[j - NT])

        lay0 = Layer(number=0, experts=E0, choices=K0, slices=SU0, tiles=NT0)
        lay0.looped = True
        lay0.wait_weights = lambda pe: pe.wait_ge(loaded_w0, 80)
        lay0.counts_at, lay0.tables_at, lay0.gathers_at = 3, (9, 10, 11, 12, 13, 13), None

        def expert_of(pe, eti, j):
            return pe.value_load(eti[0:1, bass.ds(j, 1)], min_val=0, max_val=E0 - 1)
        lay0.expert_of = expert_of
        lay0.up_weights = lambda pe, j, e: lambda k: W1_0[:, bass.ds(e, 1), k, :].rearrange("p o n -> p (o n)")
        lay0.down_weights = lambda pe, j, e: lambda k: W2_0[:, bass.ds(e, 1), k, :].rearrange("p o n -> p (o n)")
        lay0.shared = (SW1_0, SW2_0)
        routed(lay0)
        weights0.close()

        W1_1 = sb("W1_1", [P, WR, KT, 2 * F])
        W2_1 = sb("W2_1", [FH, WR2, 2, C])
        ring_w1 = [sem(f"ring_up{i}") for i in range(WR // 2)]
        ring_w2 = [sem(f"ring_down{i}") for i in range(WR2 // 4)]
        zero_rows = sem("zero_rows")
        c_std = sem("c_std"); c_var = sem("c_var"); c_xn = sem("c_xn"); c_tp = sem("c_tp"); c_kt = sem("c_kt")
        c_pad = sem("c_pad"); c_diff = sem("c_diff"); c_exp = sem("c_exp"); c_y = sem("c_y"); c_back = sem("c_back")
        c_zero = sem("c_zero"); c_max = sem("c_max"); c_den = sem("c_den"); c_ev = sem("c_ev")
        c_sums = sem("c_sums"); c_pdiff = sem("c_pdiff"); c_dec = sem("c_dec"); c_kb = sem("c_kb")
        c_relu = sem("c_relu"); c_aa = sem("c_aa"); c_ln = sem("c_ln"); c_guess = sem("c_guess")
        with ExitStack() as sc:
            def cb(name):
                return sc.enter_context(nc.sbuf_tensor(name, [P, KT, NB, T1], F32))
            KX = cb("KX"); WF = cb("WF"); PP = cb("PP"); E1B = cb("E1B"); E2B = cb("E2B"); KB = cb("KB")
            AA = WF
            BB = PP
            EV = KX[:, :, :, 1:T1]
            D3 = XNT
            D4 = XN[:, :, :].rearrange("p b c -> p (b c)").rearrange("p (k b t) -> p k b t", k=KT, b=NB)
            ZR = sc.enter_context(nc.sbuf_tensor("ZR", [P, 1024], F32))
            block = sc.enter_context(nc.Block())

            @block.sync
            def _(sp):
                sp.wait_ge(c_zero, 1)
                z = y_dram[1].rearrange("(g p r) c -> g p (r c)", p=P, r=4)
                for g in range(8):
                    sp.dma_start(z[g], ZR[:, :]).then_inc(zero_rows, 16)
                for g in range(WR // 2):
                    sp.dma_start(W1_1[:, 2 * g:2 * g + 2, :, :], w1_1[:, 2 * g:2 * g + 2, :, :]).then_inc(ring_w1[g], 16)
                for q in range(WR2 // 4):
                    sp.dma_start(W2_1[:, 4 * q:4 * q + 4, :, :],
                                 w2_1[:, 4 * q:4 * q + 4, :, :]).then_inc(ring_w2[q], 16)

            @block.gpsimd
            def _(gp):
                nc.gpsimd.memset(ZR[:, :], 0.0).then_inc(c_zero, 1)
                nc.gpsimd.memset(WF[:, :, :, 0:1], LOW)
                nc.gpsimd.memset(KX[:, :, :, 0:1], LOW)
                for a in (E1B, E2B, KB):
                    last = nc.gpsimd.memset(a[:, :, :, 0:1], 0.0)
                last.then_inc(c_pad, 1)
                gp.wait_ge(c_pad, 1)
                gp.wait_ge(c_kt, 4)
                for k in range(KT):
                    gp.wait_ge(c_max, k + 1)
                    nc.gpsimd.tensor_tensor(E2B[:, k, :, 1:T1], KX[:, k, :, 1:T1], PP[:, k, :, 1:T1],
                                            ALU.subtract).then_inc(c_pdiff, 1)

                def value_weight(k):
                    gp.wait_ge(c_exp, 4 * k + 4)
                    nc.gpsimd.tensor_tensor(EV[:, k, :, :], D4[:, k, :, :], CT[:, k, :, :],
                                            ALU.mult).then_inc(c_ev, 1)

                def denominator(k):
                    den = E2B[:, k, :, 0:P]
                    gp.wait_ge(c_exp, 4 * k + 4)
                    gp.wait_ge(c_sums, k + 1)
                    gp.wait_ge(c_kb, k + 1)
                    p_link(nc.gpsimd.tensor_tensor(den, D3[:, k, :, :], BB[:, k, :, 0:P], ALU.mult))
                    nc.gpsimd.tensor_tensor(den, den, D4[:, k, :, :], ALU.add).then_inc(c_den, 1)

                value_weight(0)
                denominator(0)
                denominator(1)
                value_weight(1)
                gp.wait_ge(zero_rows, 16 * 8)

            @block.scalar
            def _(act):
                act.wait_ge(c_var, 1)
                nc.scalar.activation(STD[:, :], STD[:, :], ACT.Sqrt).then_inc(c_std, 1)
                act.wait_ge(c_zero, 1)
                for k in range(KT):
                    nc.scalar.activation(WF[:, k, :, 1:T1], ZR[:, :].rearrange("p (b t) -> p b t", b=NB), ACT.Identity,
                                         bias=DEC[:, k:k + 1]).then_inc(c_dec, 1)
                features_out(act, c_tp, c_kt, KX[:, :, :, 1:T1])
                for k in range(KT):
                    e1, e2 = E1B[:, k, :, 1:T1], E2B[:, k, :, 1:T1]
                    act.wait_ge(c_diff, 2 * k + 1)
                    nc.scalar.activation(e1, e1, ACT.Exp, bias=DEC[:, k:k + 1]).then_inc(c_exp, 1)
                    d3, d4 = D3[:, k, :, :], D4[:, k, :, :]
                    act.wait_ge(c_diff, 2 * k + 2)
                    nc.scalar.activation(d3, d4, ACT.Relu, scale=-1.0).then_inc(c_relu, 1)
                    act.wait_ge(c_pdiff, k + 1)
                    nc.scalar.activation(e2, e2, ACT.Exp).then_inc(c_exp, 1)
                    act.wait_ge(c_relu, 2 * k + 1)
                    nc.scalar.activation(d4, d4, ACT.Relu).then_inc(c_relu, 1)
                    nc.scalar.activation(d3, d3, ACT.Exp, scale=-1.0).then_inc(c_exp, 1)
                    act.wait_ge(c_relu, 2 * k + 2)
                    nc.scalar.activation(d4, d4, ACT.Exp, scale=-1.0).then_inc(c_exp, 1)
                for k in range(KT):
                    guess = E1B[:, k, :, 0:P]
                    act.wait_ge(c_den, k + 1)
                    act.wait_ge(c_aa, k + 1)
                    nc.scalar.activation(guess, E2B[:, k, :, 0:P], ACT.Ln).then_inc(c_ln, 1)
                    act.wait_ge(c_ln, k + 1)
                    nc.scalar.activation(guess, guess, ACT.Exp, scale=-1.0).then_inc(c_guess, 1)

            @block.vector
            def _(dve):
                deviations(dve, 1e-5, c_std, c_var)
                normalize(XN, c_xn)
                dve.wait_ge(c_pad, 1)
                dve.wait_ge(c_dec, 2)
                dve.wait_ge(c_kt, 4)
                two = lambda a, k: a[:, k, :, :].rearrange("p b t -> p (b t)")
                for k in range(KT):
                    v_link(nc.vector.tensor_tensor_scan(two(PP, k), two(WF, k), two(KX, k), 0.0, ALU.add, ALU.max))
                    prev, cur = PP[:, k, :, 0:P], PP[:, k, :, 1:T1]
                    kx = KX[:, k, :, 1:T1]
                    nc.vector.engine_nop().then_inc(c_max, 1)
                    nc.vector.tensor_tensor(E1B[:, k, :, 1:T1], prev, cur, ALU.subtract).then_inc(c_diff, 1)
                    nc.vector.scalar_tensor_tensor(D4[:, k, :, :], prev, FIRST[:, k:k + 1], kx,
                                                   ALU.subtract, ALU.subtract).then_inc(c_diff, 1)
                for k in range(KT):
                    num = KB[:, k, :, 0:P]
                    dve.wait_ge(c_exp, 4 * k + 2)
                    v_link(nc.vector.tensor_tensor_scan(two(BB, k), two(E1B, k), two(E2B, k), 0.0, ALU.mult, ALU.add))
                    nc.vector.engine_nop().then_inc(c_sums, 1)
                    v_link(nc.vector.tensor_tensor(KB[:, k, :, 1:T1], E2B[:, k, :, 1:T1], CT[:, k, :, :], ALU.mult))
                    nc.vector.engine_nop().then_inc(c_kb, 1)
                    v_link(nc.vector.tensor_tensor_scan(two(AA, k), two(E1B, k), two(KB, k), 0.0, ALU.mult, ALU.add))
                    nc.vector.engine_nop().then_inc(c_aa, 1)
                    dve.wait_ge(c_exp, 4 * k + 4)
                    v_link(nc.vector.tensor_tensor(num, D3[:, k, :, :], AA[:, k, :, 0:P], ALU.mult))
                for k in range(KT):
                    num, den, guess = KB[:, k, :, 0:P], E2B[:, k, :, 0:P], E1B[:, k, :, 0:P]
                    dve.wait_ge(c_ev, k + 1)
                    v_do(nc.vector.tensor_tensor(num, num, EV[:, k, :, :], ALU.add))
                    dve.wait_ge(c_guess, k + 1)
                    v_link(nc.vector.scalar_tensor_tensor(den, den, -1.0, guess, ALU.mult, ALU.mult))
                    v_link(nc.vector.scalar_tensor_tensor(den, den, 2.0, guess, ALU.add, ALU.mult))
                    v_link(nc.vector.tensor_tensor(D3[:, k, :, :], num, den, ALU.mult))
                    nc.vector.engine_nop().then_inc(c_y, 1)
                add_tokens(dve, c_back)

            @block.tensor
            def _(pe):
                to_features(pe, c_xn, c_tp)
                pe.wait_ge(c_kt, 4)
                to_tokens(pe, D3, c_y, (1, 2), c_back)

        lay1 = Layer(number=1, experts=E1, choices=K1, slices=SU1, tiles=NT1)
        lay1.looped = False
        lay1.wait_weights = lambda pe: None
        lay1.counts_at, lay1.tables_at, lay1.gathers_at = 7, (11, 12, 13, 14), 18
        lay1.expert_of = lambda pe, eti, j: None
        lay1.ring_w1, lay1.w1, lay1.shared = ring_w1, W1_1, (SW1_1, SW2_1)

        def load_rest(sp, w_lo, dn, ns):
            def load_down(q):
                sp.wait_ge(dn, ns + 4 * q - WR2 + 4)
                s4 = 4 * q % WR2
                sp.dma_start(W2_1[:, s4:s4 + 4, :, :],
                             w2_1[:, 4 * q:4 * q + 4, :, :]).then_inc(ring_w2[s4 // 4], 16)

            for g in range(WR // 2, E1 // 2):
                sp.wait_ge(w_lo, 2 * g - WR + 2)
                s2 = 2 * g % WR
                sp.dma_start(W1_1[:, s2:s2 + 2, :, :], w1_1[:, 2 * g:2 * g + 2, :, :]).then_inc(ring_w1[s2 // 2], 16)
                if g % 2 and g // 2 >= WR2 // 4:
                    load_down(g // 2)

        lay1.load_rest = load_rest

        def down1(pe, j, e):
            q = j // 4
            pe.wait_ge(ring_w2[q % 2], 16 * (q // 2 + 1))
            return lambda k: W2_1[:, j % WR2, k, :]
        lay1.down_weights = down1
        routed(lay1)


_ORDER = ["x", "ctx_t", "toep", "d_skip", "gate0", "w1_0", "w2_0", "sw1_0", "sw2_0", "decay", "first",
          "norm_w", "gate1", "w1_1", "w2_1", "sw1_1", "sw2_1"]


def kernel(**inputs):
    import numpy as np
    import concourse.bacc as bacc
    from concourse.bass_utils import run_bass_kernel_spmd

    g = {k: np.asarray(v) for k, v in inputs.items()}

    def rows_first(a):
        a = a.reshape(*a.shape[:-2], KT, P, a.shape[-1])
        return np.moveaxis(a, -2, 0)

    def halves(a):
        a = a.reshape(*a.shape[:-2], 2, FH, a.shape[-1])
        return np.moveaxis(a, -2, 0)

    ker = g["L0_xattn_ssm_kernel"]
    lag = np.arange(C)[None, :] - np.arange(P)[:, None]
    padded = np.concatenate([np.zeros((NH, P), ker.dtype), ker], 1)
    a = {
        "x": g["x"],
        "ctx_t": g["ctx_2048"].transpose(2, 0, 1).reshape(KT, P, NB, P).transpose(1, 0, 2, 3),
        "toep": padded[:, lag + P].transpose(1, 0, 2),
        "d_skip": np.broadcast_to(g["L0_xattn_D"], (P, NH)),
        "gate0": rows_first(g["L0_ffn_gate_w"].T),
        "w1_0": rows_first(g["L0_ffn_w1"].transpose(0, 2, 1)),
        "w2_0": halves(g["L0_ffn_w2"].transpose(0, 2, 1)),
        "decay": g["L1_xattn_time_decay"].reshape(KT, P).T,
        "first": g["L1_xattn_time_first"].reshape(KT, P).T,
        "norm_w": np.broadcast_to(g["L1_ffn_w_norm"], (P, C)),
        "gate1": rows_first(np.concatenate([g["L1_ffn_w_router"], g["L1_ffn_w_shared_gate"]], 1)),
        "w1_1": rows_first(np.concatenate([g["L1_ffn_w_gate"], g["L1_ffn_w_up"]], 2)),
        "w2_1": halves(g["L1_ffn_w_down"]),
    }
    s0 = g["L0_ffn_shared_w1"].T.reshape(C, 2, SU0, F).transpose(2, 0, 1, 3).reshape(SU0, C, 2 * F)
    s1 = np.stack([g["L1_ffn_sw_gate"].reshape(C, SU1, F), g["L1_ffn_sw_up"].reshape(C, SU1, F)], 2)
    a["sw1_0"] = rows_first(s0)
    a["sw2_0"] = halves(g["L0_ffn_shared_w2"].T.reshape(SU0, F, C))
    a["sw1_1"] = rows_first(s1.transpose(1, 0, 2, 3).reshape(SU1, C, 2 * F))
    a["sw2_1"] = halves(g["L1_ffn_sw_down"].reshape(SU1, F, C))

    nc = bacc.Bacc("TRN2", target_bir_lowering=False, num_devices=1)
    arrays, args = {}, []
    for name in _ORDER:
        v = np.ascontiguousarray(a[name])
        arrays[f"in_{name}"] = v
        args.append(nc.dram_tensor(f"in_{name}", v.shape, mybir.dt.from_np(v.dtype), kind="ExternalInput").ap())
    out = nc.dram_tensor("out_x", (NB, P, C), F32, kind="ExternalOutput").ap()
    build(nc, *args, out)
    r = run_bass_kernel_spmd(nc, [arrays], core_ids=[0])
    return r.results[0]["out_x"]
```
